# Optimizing a Trainium2 kernel written in Bass

```python
import numpy as np
import jax
import jax.numpy as jnp

def _softmax(x, axis=-1):
    return jax.nn.softmax(x, axis=axis)

def _gelu(x):
    return jax.nn.gelu(x, approximate=True)

def _silu(x):
    return jax.nn.silu(x)

def _sigmoid(x):
    return jax.nn.sigmoid(x)

def _layernorm(x, axis=-1, eps=1e-05):
    m = jnp.mean(x, axis=axis, keepdims=True)
    v = jnp.var(x, axis=axis, keepdims=True)
    return (x - m) / jnp.sqrt(v + eps)

def _scatter_add(tgt, idx, src, axis=0):
    return tgt.at[idx].add(src)

def _segment_sum(src, seg, n):
    return jax.ops.segment_sum(src, seg, n)
kernel_name = 'mk_decoder_postln_d2_seqx_r8_e49362'

def setup_inputs(seed: int=0):
    np.random.seed(seed)
    _w = jnp.asarray

    def _rec_inputs():
        import jax
        import jax.numpy as jnp
        _rk = jax.random.key(seed)
        x = -0.0002928 + 1 * jax.random.normal(jax.random.fold_in(_rk, 1), (8, 256, 128), jnp.float32)
        _lenS = 256 - jax.random.randint(jax.random.fold_in(_rk, 7), (8,), 0, max(1, 256 // 4) + 1, jnp.int32)
        _lenS2 = 256 - jax.random.randint(jax.random.fold_in(_rk, 8), (8,), 0, max(1, 256 // 4) + 1, jnp.int32)
        _ctx_512P = jax.random.normal(jax.random.fold_in(_rk, 11), (8, 16, 64), jnp.float32)
        _ctx_512c = jax.random.dirichlet(jax.random.fold_in(_rk, 511), 0.3 * jnp.ones((16,), jnp.float32), (8, 256))
        _ctx_512t = jnp.einsum('bsk,bkd->bsd', _ctx_512c, _ctx_512P)
        _ctx_512t = _ctx_512t * jax.lax.rsqrt(jnp.mean(jnp.square(_ctx_512t)) + 1e-12) * 0.953939
        ctx_512 = 0.00222621 + 0.99962 * (_ctx_512t + 0.3 * jax.random.normal(jax.random.fold_in(_rk, 611), (8, 256, 64), jnp.float32))
        return (x, ctx_512)
    x, ctx_512 = _rec_inputs()

    def _L0_attn_setup():
        import jax, jax.numpy as jnp
        import numpy as np
        N_HEADS = 16
        HEAD_DIM = 64
        HIDDEN = 128
        key = jax.random.key(seed)
        kx, kq, kk, kv, ko = jax.random.split(key, 5)
        B, S = (1, 512)
        lim = float(np.sqrt(6.0 / (HIDDEN + N_HEADS * HEAD_DIM)))
        x = jax.random.normal(kx, (B, S, HIDDEN), dtype=jnp.float32)
        wq = jax.random.uniform(kq, (N_HEADS * HEAD_DIM, HIDDEN), jnp.float32, -lim, lim)
        wk = jax.random.uniform(kk, (N_HEADS * HEAD_DIM, HIDDEN), jnp.float32, -lim, lim)
        wv = jax.random.uniform(kv, (N_HEADS * HEAD_DIM, HIDDEN), jnp.float32, -lim, lim)
        wo = jax.random.uniform(ko, (HIDDEN, N_HEADS * HEAD_DIM), jnp.float32, -lim, lim)
        return {'x': x, 'wq': wq, 'wk': wk, 'wv': wv, 'wo': wo}
    _L0_attn_all = _L0_attn_setup()
    _L0_attn_in = {k: v for k, v in _L0_attn_all.items() if k in ('wq', 'wk', 'wv', 'wo')}
    del _L0_attn_all

    def _L0_xattn_setup():
        import jax, jax.numpy as jnp
        import numpy as np
        B, T, TC, C, CC, H = (2, 256, 64, 128, 64, 16)
        D = C // H

        def _heads(t):
            b, l, _ = t.shape
            return t.reshape(b, l, H, D).transpose(0, 2, 1, 3)
        key = jax.random.key(seed)
        ks = jax.random.split(key, 18)
        w = lambda k, i, o: jax.random.normal(k, (i, o), jnp.float32) / np.sqrt(i).astype(np.float32)
        return {'x': jax.random.normal(ks[0], (B, T, C), jnp.float32), 'cross_input': jax.random.normal(ks[1], (B, TC, CC), jnp.float32), 'Wk': w(ks[2], C, C), 'bk': jnp.zeros((C,), jnp.float32), 'Wq': w(ks[3], C, C), 'bq': jnp.zeros((C,), jnp.float32), 'Wv': w(ks[4], C, C), 'bv': jnp.zeros((C,), jnp.float32), 'Wck': w(ks[5], CC, C), 'bck': jnp.zeros((C,), jnp.float32), 'Wcq': w(ks[6], C, C), 'bcq': jnp.zeros((C,), jnp.float32), 'Wcv': w(ks[7], CC, C), 'bcv': jnp.zeros((C,), jnp.float32), 'Wp': w(ks[8], C, C), 'bp': jnp.zeros((C,), jnp.float32)}
    _L0_xattn_all = _L0_xattn_setup()
    _L0_xattn_in = {k: v for k, v in _L0_xattn_all.items() if k in ('Wk', 'bk', 'Wq', 'bq', 'Wv', 'bv', 'Wck', 'bck', 'Wcq', 'bcq', 'Wcv', 'bcv', 'Wp', 'bp')}
    del _L0_xattn_all

    def _L0_ffn_setup():
        import jax, jax.numpy as jnp
        import numpy as np
        B, T, D = (8, 512, 128)
        NUM_SLOTS = 64
        TOP_K = 8
        DQ = D // 4
        DH = D // 2

        def _forward(x, slot_init, w1, b1, w2, b2, tau, Wih, Whh, bih, bhh, wq, bq, wk, bk, wv, bv, ln_g, ln_b, wvp, bvp, wo, bo):
            Bx, Tx, Dx = x.shape
            S = jnp.broadcast_to(slot_init[None], (Bx, NUM_SLOTS, Dx)).astype(x.dtype)
            slot_mean = jnp.broadcast_to(S.mean(axis=1, keepdims=True), (Bx, Tx, Dx))
            ctx = jnp.concatenate([x, slot_mean], axis=-1)
            h = jax.nn.gelu(ctx @ w1 + b1, approximate=False)
            route_logits = (h @ w2 + b2) / (jnp.abs(tau) + 0.1)
            topk_vals, topk_idx = jax.lax.top_k(route_logits, TOP_K)
            topk_w = jax.nn.softmax(topk_vals, axis=-1)
            alpha = (jax.nn.one_hot(topk_idx, NUM_SLOTS, dtype=x.dtype) * topk_w[..., None]).sum(axis=-2)
            slot_input = jnp.einsum('bts,btd->bsd', alpha, x)
            denom = alpha.sum(axis=1) + 1e-08
            si = slot_input / denom[..., None]
            gi = si @ Wih.T + bih
            gh = S @ Whh.T + bhh
            i_r, i_z, i_n = jnp.split(gi, 3, axis=-1)
            h_r, h_z, h_n = jnp.split(gh, 3, axis=-1)
            r = jax.nn.sigmoid(i_r + h_r)
            z = jax.nn.sigmoid(i_z + h_z)
            n = jnp.tanh(i_n + r * h_n)
            S_new = (1.0 - z) * n + z * S
            q = S_new @ wq + bq
            k = S_new @ wk + bk
            v = S_new @ wv + bv
            scale = DQ ** (-0.5)
            attn = jax.nn.softmax(jnp.einsum('bsq,btq->bst', q, k) * scale, axis=-1)
            S_comm = jnp.einsum('bst,btd->bsd', attn, v)
            y = S_new + S_comm
            mu = y.mean(axis=-1, keepdims=True)
            var = y.var(axis=-1, keepdims=True)
            y = (y - mu) * jax.lax.rsqrt(var + 1e-05) * ln_g + ln_b
            slot_values = y @ wvp + bvp
            out = jnp.einsum('bts,bsd->btd', alpha, slot_values)
            return out @ wo + bo
        key = jax.random.key(seed)
        ks = jax.random.split(key, 24)
        n = lambda k, shp, s=0.02: jax.random.normal(k, shp, dtype=jnp.float32) * s
        return {'x': jax.random.normal(ks[0], (B, T, D), dtype=jnp.float32), 'slot_init': n(ks[1], (NUM_SLOTS, D)), 'w1': n(ks[2], (2 * D, DH)), 'b1': jnp.zeros((DH,)), 'w2': n(ks[3], (DH, NUM_SLOTS)), 'b2': jnp.zeros((NUM_SLOTS,)), 'tau': jnp.ones((1,)), 'Wih': n(ks[4], (3 * D, D)), 'Whh': n(ks[5], (3 * D, D)), 'bih': jnp.zeros((3 * D,)), 'bhh': jnp.zeros((3 * D,)), 'wq': n(ks[6], (D, DQ)), 'bq': jnp.zeros((DQ,)), 'wk': n(ks[7], (D, DQ)), 'bk': jnp.zeros((DQ,)), 'wv': n(ks[8], (D, D)), 'bv': jnp.zeros((D,)), 'ln_g': jnp.ones((D,)), 'ln_b': jnp.zeros((D,)), 'wvp': n(ks[9], (D, D)), 'bvp': jnp.zeros((D,)), 'wo': n(ks[10], (D, D)), 'bo': jnp.zeros((D,))}
    _L0_ffn_all = _L0_ffn_setup()
    _L0_ffn_in = {k: v for k, v in _L0_ffn_all.items() if k in ('slot_init', 'w1', 'b1', 'w2', 'b2', 'tau', 'Wih', 'Whh', 'bih', 'bhh', 'wq', 'bq', 'wk', 'bk', 'wv', 'bv', 'ln_g', 'ln_b', 'wvp', 'bvp', 'wo', 'bo')}
    del _L0_ffn_all

    def _L1_attn_setup():
        import jax, jax.numpy as jnp
        import numpy as np
        B, S, D = (2, 256, 128)
        H, L = (16, 64)
        ROPE_BASE = 10000.0

        def _rope_tables(seq_len, dim):
            inv_freq = 1.0 / ROPE_BASE ** (2.0 * jnp.arange(0, dim // 2, dtype=jnp.float32) / dim)
            pos = jnp.arange(seq_len, dtype=jnp.float32)
            ang = pos[:, None] * inv_freq[None, :]
            cos = jnp.cos(ang).reshape(1, seq_len, 1, dim // 2)
            sin = jnp.sin(ang).reshape(1, seq_len, 1, dim // 2)
            return (cos, sin)

        def _apply_rope(t, cos, sin):
            tr = t.reshape(*t.shape[:-1], -1, 2)
            x0, x1 = (tr[..., 0], tr[..., 1])
            out = jnp.concatenate([x0 * cos - x1 * sin, x0 * sin + x1 * cos], axis=-1)
            return out.reshape(t.shape)
        key = jax.random.key(seed)
        ks = jax.random.split(key, 5)
        scale = 0.03
        return {'x': jax.random.normal(ks[0], (B, S, D), dtype=jnp.float32), 'Wq': jax.random.normal(ks[1], (D, H * L), dtype=jnp.float32) * scale, 'bq': jnp.zeros((H * L,), dtype=jnp.float32), 'Wk': jax.random.normal(ks[2], (D, H * L), dtype=jnp.float32) * scale, 'bk': jnp.zeros((H * L,), dtype=jnp.float32), 'Wv': jax.random.normal(ks[3], (D, H * L), dtype=jnp.float32) * scale, 'bv': jnp.zeros((H * L,), dtype=jnp.float32), 'Wo': jax.random.normal(ks[4], (H * L, D), dtype=jnp.float32) * scale, 'bo': jnp.zeros((D,), dtype=jnp.float32)}
    _L1_attn_all = _L1_attn_setup()
    _L1_attn_in = {k: v for k, v in _L1_attn_all.items() if k in ('Wq', 'bq', 'Wk', 'bk', 'Wv', 'bv', 'Wo', 'bo')}
    del _L1_attn_all

    def _L1_xattn_setup():
        import jax, jax.numpy as jnp
        import numpy as np
        DIM = 128
        LATENT_DIM = 64
        NUM_HEADS = 16
        HEAD_DIM = DIM // NUM_HEADS
        SCALE = HEAD_DIM ** (-0.5)
        key = jax.random.key(seed)
        k1, k2, k3, k4, k5 = jax.random.split(key, 5)
        B, xN, zN = (2, 256, 256)
        x = jax.random.normal(k1, (B, xN, DIM), dtype=jnp.float32)
        z = jax.random.normal(k2, (B, zN, LATENT_DIM), dtype=jnp.float32)
        Wq = jax.random.normal(k3, (DIM, DIM), dtype=jnp.float32) * DIM ** (-0.5)
        Wkv = jax.random.normal(k4, (2 * DIM, LATENT_DIM), dtype=jnp.float32) * LATENT_DIM ** (-0.5)
        Wo = jax.random.normal(k5, (DIM, DIM), dtype=jnp.float32) * DIM ** (-0.5)
        return {'x': x, 'z': z, 'Wq': Wq, 'Wkv': Wkv, 'Wo': Wo}
    _L1_xattn_all = _L1_xattn_setup()
    _L1_xattn_in = {k: v for k, v in _L1_xattn_all.items() if k in ('Wq', 'Wkv', 'Wo')}
    del _L1_xattn_all

    def _L1_ffn_setup():
        import jax, jax.numpy as jnp
        import numpy as np
        TOP_K = 2
        CAPACITY_FACTOR = 1.0
        key = jax.random.key(seed)
        ks = jax.random.split(key, 4)
        sl, bs, hs, ffn, E = (256, 8, 128, 512, 8)
        x = jax.random.normal(ks[0], (sl, bs, hs), dtype=jnp.float32)
        w_router = jax.random.normal(ks[1], (hs, E), dtype=jnp.float32) * 0.02
        w1 = jax.random.normal(ks[2], (E, hs, ffn), dtype=jnp.float32) * 0.02
        w2 = jax.random.normal(ks[3], (E, ffn, hs), dtype=jnp.float32) * 0.02
        bias = jnp.zeros((1, 1, hs), dtype=jnp.float32)
        return {'x': x, 'w_router': w_router, 'w1': w1, 'w2': w2, 'bias': bias}
    _L1_ffn_all = _L1_ffn_setup()
    _L1_ffn_in = {k: v for k, v in _L1_ffn_all.items() if k in ('w_router', 'w1', 'w2', 'bias')}
    del _L1_ffn_all
    return {'x': x, 'ctx_512': ctx_512, 'L0_attn_wq': _L0_attn_in['wq'], 'L0_attn_wk': _L0_attn_in['wk'], 'L0_attn_wv': _L0_attn_in['wv'], 'L0_attn_wo': _L0_attn_in['wo'], 'L0_xattn_Wk': _L0_xattn_in['Wk'], 'L0_xattn_bk': _L0_xattn_in['bk'], 'L0_xattn_Wq': _L0_xattn_in['Wq'], 'L0_xattn_bq': _L0_xattn_in['bq'], 'L0_xattn_Wv': _L0_xattn_in['Wv'], 'L0_xattn_bv': _L0_xattn_in['bv'], 'L0_xattn_Wck': _L0_xattn_in['Wck'], 'L0_xattn_bck': _L0_xattn_in['bck'], 'L0_xattn_Wcq': _L0_xattn_in['Wcq'], 'L0_xattn_bcq': _L0_xattn_in['bcq'], 'L0_xattn_Wcv': _L0_xattn_in['Wcv'], 'L0_xattn_bcv': _L0_xattn_in['bcv'], 'L0_xattn_Wp': _L0_xattn_in['Wp'], 'L0_xattn_bp': _L0_xattn_in['bp'], 'L0_ffn_slot_init': _L0_ffn_in['slot_init'], 'L0_ffn_w1': _L0_ffn_in['w1'], 'L0_ffn_b1': _L0_ffn_in['b1'], 'L0_ffn_w2': _L0_ffn_in['w2'], 'L0_ffn_b2': _L0_ffn_in['b2'], 'L0_ffn_tau': _L0_ffn_in['tau'], 'L0_ffn_Wih': _L0_ffn_in['Wih'], 'L0_ffn_Whh': _L0_ffn_in['Whh'], 'L0_ffn_bih': _L0_ffn_in['bih'], 'L0_ffn_bhh': _L0_ffn_in['bhh'], 'L0_ffn_wq': _L0_ffn_in['wq'], 'L0_ffn_bq': _L0_ffn_in['bq'], 'L0_ffn_wk': _L0_ffn_in['wk'], 'L0_ffn_bk': _L0_ffn_in['bk'], 'L0_ffn_wv': _L0_ffn_in['wv'], 'L0_ffn_bv': _L0_ffn_in['bv'], 'L0_ffn_ln_g': _L0_ffn_in['ln_g'], 'L0_ffn_ln_b': _L0_ffn_in['ln_b'], 'L0_ffn_wvp': _L0_ffn_in['wvp'], 'L0_ffn_bvp': _L0_ffn_in['bvp'], 'L0_ffn_wo': _L0_ffn_in['wo'], 'L0_ffn_bo': _L0_ffn_in['bo'], 'L1_attn_Wq': _L1_attn_in['Wq'], 'L1_attn_bq': _L1_attn_in['bq'], 'L1_attn_Wk': _L1_attn_in['Wk'], 'L1_attn_bk': _L1_attn_in['bk'], 'L1_attn_Wv': _L1_attn_in['Wv'], 'L1_attn_bv': _L1_attn_in['bv'], 'L1_attn_Wo': _L1_attn_in['Wo'], 'L1_attn_bo': _L1_attn_in['bo'], 'L1_xattn_Wq': _L1_xattn_in['Wq'], 'L1_xattn_Wkv': _L1_xattn_in['Wkv'], 'L1_xattn_Wo': _L1_xattn_in['Wo'], 'L1_ffn_w_router': _L1_ffn_in['w_router'], 'L1_ffn_w1': _L1_ffn_in['w1'], 'L1_ffn_w2': _L1_ffn_in['w2'], 'L1_ffn_bias': _L1_ffn_in['bias']}

def reference(x, ctx_512, L0_attn_wq, L0_attn_wk, L0_attn_wv, L0_attn_wo, L0_xattn_Wk, L0_xattn_bk, L0_xattn_Wq, L0_xattn_bq, L0_xattn_Wv, L0_xattn_bv, L0_xattn_Wck, L0_xattn_bck, L0_xattn_Wcq, L0_xattn_bcq, L0_xattn_Wcv, L0_xattn_bcv, L0_xattn_Wp, L0_xattn_bp, L0_ffn_slot_init, L0_ffn_w1, L0_ffn_b1, L0_ffn_w2, L0_ffn_b2, L0_ffn_tau, L0_ffn_Wih, L0_ffn_Whh, L0_ffn_bih, L0_ffn_bhh, L0_ffn_wq, L0_ffn_bq, L0_ffn_wk, L0_ffn_bk, L0_ffn_wv, L0_ffn_bv, L0_ffn_ln_g, L0_ffn_ln_b, L0_ffn_wvp, L0_ffn_bvp, L0_ffn_wo, L0_ffn_bo, L1_attn_Wq, L1_attn_bq, L1_attn_Wk, L1_attn_bk, L1_attn_Wv, L1_attn_bv, L1_attn_Wo, L1_attn_bo, L1_xattn_Wq, L1_xattn_Wkv, L1_xattn_Wo, L1_ffn_w_router, L1_ffn_w1, L1_ffn_w2, L1_ffn_bias):
    import jax
    import jax.numpy as jnp

    def _L0_attn_ref(x, wq, wk, wv, wo):
        import jax, jax.numpy as jnp
        import numpy as np
        N_HEADS = 16
        HEAD_DIM = 64
        HIDDEN = 128
        B, S, _ = x.shape
        scale = HEAD_DIM ** (-0.5)

        def proj(w):
            return jnp.einsum('bsh,eh->bse', x, w).reshape(B, S, N_HEADS, HEAD_DIM).transpose(0, 2, 1, 3)
        q, k, v = (proj(wq), proj(wk), proj(wv))
        scores = jnp.einsum('bhqd,bhkd->bhqk', q, k) * scale
        causal = jnp.tril(jnp.ones((S, S), dtype=bool))
        scores = jnp.where(causal, scores, -jnp.inf)
        probs = jax.nn.softmax(scores, axis=-1)
        out = jnp.einsum('bhqk,bhkd->bhqd', probs, v)
        out = out.transpose(0, 2, 1, 3).reshape(B, S, N_HEADS * HEAD_DIM)
        return jnp.einsum('bse,he->bsh', out, wo)

    def _L0_xattn_ref(x, cross_input, Wk, bk, Wq, bq, Wv, bv, Wck, bck, Wcq, bcq, Wcv, bcv, Wp, bp):
        import jax, jax.numpy as jnp
        import numpy as np
        B, T, TC, C, CC, H = (2, 256, 64, 128, 64, 16)
        D = C // H

        def _heads(t):
            b, l, _ = t.shape
            return t.reshape(b, l, H, D).transpose(0, 2, 1, 3)
        scale = np.float32(1.0 / np.sqrt(D))
        q = _heads(x @ Wq + bq)
        k = _heads(x @ Wk + bk)
        v = _heads(x @ Wv + bv)
        att = jnp.einsum('bhqd,bhkd->bhqk', q, k) * scale
        causal = jnp.tril(jnp.ones((T, T), bool))
        att = jnp.where(causal[None, None], att, -jnp.inf)
        y = jnp.einsum('bhqk,bhkd->bhqd', jax.nn.softmax(att, axis=-1), v)
        qc = _heads(x @ Wcq + bcq)
        kc = _heads(cross_input @ Wck + bck)
        vc = _heads(cross_input @ Wcv + bcv)
        attc = jnp.einsum('bhqd,bhkd->bhqk', qc, kc) * scale
        y = y + jnp.einsum('bhqk,bhkd->bhqd', jax.nn.softmax(attc, axis=-1), vc)
        y = y.transpose(0, 2, 1, 3).reshape(x.shape[0], T, C)
        return y @ Wp + bp

    def _L0_ffn_ref(x, slot_init, w1, b1, w2, b2, tau, Wih, Whh, bih, bhh, wq, bq, wk, bk, wv, bv, ln_g, ln_b, wvp, bvp, wo, bo):
        import jax, jax.numpy as jnp
        import numpy as np
        B, T, D = (8, 512, 128)
        NUM_SLOTS = 64
        TOP_K = 8
        DQ = D // 4
        DH = D // 2

        def _forward(x, slot_init, w1, b1, w2, b2, tau, Wih, Whh, bih, bhh, wq, bq, wk, bk, wv, bv, ln_g, ln_b, wvp, bvp, wo, bo):
            Bx, Tx, Dx = x.shape
            S = jnp.broadcast_to(slot_init[None], (Bx, NUM_SLOTS, Dx)).astype(x.dtype)
            slot_mean = jnp.broadcast_to(S.mean(axis=1, keepdims=True), (Bx, Tx, Dx))
            ctx = jnp.concatenate([x, slot_mean], axis=-1)
            h = jax.nn.gelu(ctx @ w1 + b1, approximate=False)
            route_logits = (h @ w2 + b2) / (jnp.abs(tau) + 0.1)
            topk_vals, topk_idx = jax.lax.top_k(route_logits, TOP_K)
            topk_w = jax.nn.softmax(topk_vals, axis=-1)
            alpha = (jax.nn.one_hot(topk_idx, NUM_SLOTS, dtype=x.dtype) * topk_w[..., None]).sum(axis=-2)
            slot_input = jnp.einsum('bts,btd->bsd', alpha, x)
            denom = alpha.sum(axis=1) + 1e-08
            si = slot_input / denom[..., None]
            gi = si @ Wih.T + bih
            gh = S @ Whh.T + bhh
            i_r, i_z, i_n = jnp.split(gi, 3, axis=-1)
            h_r, h_z, h_n = jnp.split(gh, 3, axis=-1)
            r = jax.nn.sigmoid(i_r + h_r)
            z = jax.nn.sigmoid(i_z + h_z)
            n = jnp.tanh(i_n + r * h_n)
            S_new = (1.0 - z) * n + z * S
            q = S_new @ wq + bq
            k = S_new @ wk + bk
            v = S_new @ wv + bv
            scale = DQ ** (-0.5)
            attn = jax.nn.softmax(jnp.einsum('bsq,btq->bst', q, k) * scale, axis=-1)
            S_comm = jnp.einsum('bst,btd->bsd', attn, v)
            y = S_new + S_comm
            mu = y.mean(axis=-1, keepdims=True)
            var = y.var(axis=-1, keepdims=True)
            y = (y - mu) * jax.lax.rsqrt(var + 1e-05) * ln_g + ln_b
            slot_values = y @ wvp + bvp
            out = jnp.einsum('bts,bsd->btd', alpha, slot_values)
            return out @ wo + bo
        return _forward(x, slot_init, w1, b1, w2, b2, tau, Wih, Whh, bih, bhh, wq, bq, wk, bk, wv, bv, ln_g, ln_b, wvp, bvp, wo, bo)

    def _L1_attn_ref(x, Wq, bq, Wk, bk, Wv, bv, Wo, bo):
        import jax, jax.numpy as jnp
        import numpy as np
        B, S, D = (2, 256, 128)
        H, L = (16, 64)
        ROPE_BASE = 10000.0

        def _rope_tables(seq_len, dim):
            inv_freq = 1.0 / ROPE_BASE ** (2.0 * jnp.arange(0, dim // 2, dtype=jnp.float32) / dim)
            pos = jnp.arange(seq_len, dtype=jnp.float32)
            ang = pos[:, None] * inv_freq[None, :]
            cos = jnp.cos(ang).reshape(1, seq_len, 1, dim // 2)
            sin = jnp.sin(ang).reshape(1, seq_len, 1, dim // 2)
            return (cos, sin)

        def _apply_rope(t, cos, sin):
            tr = t.reshape(*t.shape[:-1], -1, 2)
            x0, x1 = (tr[..., 0], tr[..., 1])
            out = jnp.concatenate([x0 * cos - x1 * sin, x0 * sin + x1 * cos], axis=-1)
            return out.reshape(t.shape)
        b, s, _ = x.shape
        q = (x @ Wq + bq).reshape(b, s, H, L)
        k = (x @ Wk + bk).reshape(b, s, H, L)
        v = (x @ Wv + bv).reshape(b, s, H, L)
        cos, sin = _rope_tables(s, L)
        q = _apply_rope(q, cos, sin)
        k = _apply_rope(k, cos, sin)
        q = jnp.transpose(q, (0, 2, 1, 3))
        k = jnp.transpose(k, (0, 2, 1, 3))
        v = jnp.transpose(v, (0, 2, 1, 3))
        scores = jnp.einsum('bnqd,bnkd->bnqk', q, k) / jnp.sqrt(jnp.float32(L))
        causal = jnp.arange(s)[None, :] <= jnp.arange(s)[:, None]
        scores = jnp.where(causal, scores, -1000000000.0)
        attn = jax.nn.softmax(scores, axis=-1)
        attended = jnp.einsum('bnqk,bnkd->bnqd', attn, v)
        attended = jnp.transpose(attended, (0, 2, 1, 3)).reshape(b, s, H * L)
        return attended @ Wo + bo

    def _L1_xattn_ref(x, z, Wq, Wkv, Wo):
        import jax, jax.numpy as jnp
        import numpy as np
        DIM = 128
        LATENT_DIM = 64
        NUM_HEADS = 16
        HEAD_DIM = DIM // NUM_HEADS
        SCALE = HEAD_DIM ** (-0.5)
        B, xN, _ = x.shape
        _, zN, _ = z.shape
        Q = (x @ Wq.T).reshape(B, xN, NUM_HEADS, HEAD_DIM)
        KV = (z @ Wkv.T).reshape(B, zN, 2, NUM_HEADS, HEAD_DIM)
        K = KV[:, :, 0]
        V = KV[:, :, 1]
        attn = jnp.einsum('bqhd,bkhd->bhqk', Q, K) * SCALE
        attn = jax.nn.softmax(attn, axis=-1)
        O = jnp.einsum('bhqk,bkhd->bqhd', attn, V).reshape(B, xN, DIM)
        return O @ Wo.T

    def _L1_ffn_ref(x, w_router, w1, w2, bias):
        import jax, jax.numpy as jnp
        import numpy as np
        TOP_K = 2
        CAPACITY_FACTOR = 1.0
        sl, bs, hs = x.shape
        E = w_router.shape[1]
        xf = x.reshape(-1, hs)
        T = xf.shape[0]
        capacity = int(CAPACITY_FACTOR * TOP_K * T / E)
        scores = jax.nn.softmax(xf @ w_router, axis=-1)
        expert_weights, top_experts = jax.lax.top_k(scores, TOP_K)
        flat_e = top_experts.reshape(-1)
        flat_w = expert_weights.reshape(-1)
        N = flat_e.shape[0]
        order = jnp.argsort(flat_e, stable=True)
        bin_ids = flat_e[order]
        tpe = jnp.zeros((E,), jnp.int32).at[flat_e].add(1)
        starts = jnp.cumsum(tpe) - tpe
        offsets = jnp.arange(N) - starts[bin_ids]
        valid = offsets < capacity
        slot = jnp.where(valid, bin_ids * capacity + offsets, E * capacity)
        src = order // TOP_K
        xb = jnp.zeros((E * capacity + 1, hs), x.dtype).at[slot].set(xf[src])
        xb = xb[:-1].reshape(E, capacity, hs)
        h = jax.nn.gelu(jnp.einsum('ech,ehf->ecf', xb, w1))
        y = jnp.einsum('ecf,efh->ech', h, w2).reshape(E * capacity, hs)
        yv = jnp.where(valid[:, None], y[jnp.minimum(slot, E * capacity - 1)], 0.0)
        out = jnp.zeros((T, hs), x.dtype).at[src].add(flat_w[order][:, None] * yv)
        return out.reshape(sl, bs, hs) + bias
    x = _layernorm(x + _L0_attn_ref(x, L0_attn_wq, L0_attn_wk, L0_attn_wv, L0_attn_wo), axis=-1)
    x = _layernorm(x + _L0_xattn_ref(x, ctx_512, L0_xattn_Wk, L0_xattn_bk, L0_xattn_Wq, L0_xattn_bq, L0_xattn_Wv, L0_xattn_bv, L0_xattn_Wck, L0_xattn_bck, L0_xattn_Wcq, L0_xattn_bcq, L0_xattn_Wcv, L0_xattn_bcv, L0_xattn_Wp, L0_xattn_bp), axis=-1)
    x = _layernorm(x + _L0_ffn_ref(x, L0_ffn_slot_init, L0_ffn_w1, L0_ffn_b1, L0_ffn_w2, L0_ffn_b2, L0_ffn_tau, L0_ffn_Wih, L0_ffn_Whh, L0_ffn_bih, L0_ffn_bhh, L0_ffn_wq, L0_ffn_bq, L0_ffn_wk, L0_ffn_bk, L0_ffn_wv, L0_ffn_bv, L0_ffn_ln_g, L0_ffn_ln_b, L0_ffn_wvp, L0_ffn_bvp, L0_ffn_wo, L0_ffn_bo), axis=-1)
    x = _layernorm(x + _L1_attn_ref(x, L1_attn_Wq, L1_attn_bq, L1_attn_Wk, L1_attn_bk, L1_attn_Wv, L1_attn_bv, L1_attn_Wo, L1_attn_bo), axis=-1)
    x = _layernorm(x + _L1_xattn_ref(x, ctx_512, L1_xattn_Wq, L1_xattn_Wkv, L1_xattn_Wo), axis=-1)
    x = _layernorm(x + _L1_ffn_ref(x, L1_ffn_w_router, L1_ffn_w1, L1_ffn_w2, L1_ffn_bias), axis=-1)
    return x

_drawn_inputs = setup_inputs


def setup_inputs(seed=0):
    import zlib

    import numpy as np

    out = dict(_drawn_inputs(seed))
    spreads = {'L0_xattn_bk': (0.0, 2.0),
     'L0_xattn_bq': (0.0, 0.514),
     'L0_xattn_bv': (0.0, 0.1),
     'L0_xattn_bck': (0.0, 2.0),
     'L0_xattn_bcq': (0.0, 0.434),
     'L0_xattn_bcv': (0.0, 0.1),
     'L0_xattn_bp': (0.0, 0.1),
     'L0_ffn_b1': (0.0, 0.8),
     'L0_ffn_b2': (0.0, 0.8),
     'L0_ffn_bih': (0.0, 0.425),
     'L0_ffn_bhh': (0.0, 0.8),
     'L0_ffn_bq': (0.0, 2.0),
     'L0_ffn_bk': (0.0, 2.0),
     'L0_ffn_bv': (0.0, 0.1),
     'L0_ffn_ln_g': (1.0, 0.6),
     'L0_ffn_ln_b': (0.0, 0.8),
     'L0_ffn_bvp': (0.0, 0.351),
     'L0_ffn_bo': (0.0, 0.1),
     'L1_attn_bq': (0.0, 0.8),
     'L1_attn_bk': (0.0, 0.8),
     'L1_attn_bv': (0.0, 0.1),
     'L1_attn_bo': (0.0, 0.1),
     'L1_ffn_bias': (0.0, 0.1)}
    factors = {'L0_attn_wq': 2.972,
     'L0_attn_wk': 2.882,
     'L0_ffn_slot_init': 8.0,
     'L0_ffn_w1': 8.0,
     'L0_ffn_w2': 8.0,
     'L0_ffn_Wih': 2.918,
     'L0_ffn_Whh': 8.0,
     'L0_ffn_wq': 38.643,
     'L0_ffn_wk': 32.202,
     'L0_ffn_wv': 8.0,
     'L1_attn_Wq': 8.0,
     'L1_attn_Wk': 8.0,
     'L1_ffn_w_router': 5.638,
     'L1_ffn_w1': 5.037,
     'L1_ffn_w2': 4.933}
    for name, (base, spread) in spreads.items():
        noise = np.random.default_rng([zlib.crc32(name.encode()), seed]).standard_normal(out[name].shape)
        drawn = base * np.exp(spread * noise) if base else spread * noise
        out[name] = jnp.asarray(drawn.astype(out[name].dtype))
    for name, factor in factors.items():
        out[name] = (out[name] * factor).astype(out[name].dtype)
    return out
```

```python
from contextlib import ExitStack

import numpy as np

import concourse.bass as bass
from concourse import mybir

F32 = mybir.dt.float32
BF16 = mybir.dt.bfloat16
ALU = mybir.AluOpType
ACT = mybir.ActivationFunctionType
AX = mybir.AxisListType

P = 128
BATCH, SEQ, D = 8, 256, 128
CTX = 64
PAIR = 2
ITERS = BATCH // PAIR
TOK = PAIR * SEQ
TT = TOK // P
NH = 16
HD = 64
E = NH * HD
NC = E // P
DX = D // NH
NG = 4
HG = NH // NG
VW = DX + 1
PARTS = 3
STACK = PARTS * PARTS * DX
MROW = 96
SLOTS, DQ, TOPK = 64, 32, 8
NE, FF, TOP = 8, 512, 2
FC = FF // P
CAPACITY = TOP * BATCH * SEQ // NE
EPS = 1e-5
MASKED = -1e30
FAR = 3e38


class Signal:

    def __init__(self, sem, places, step):
        self.sem, self.places, self.step, self.count, self.base = sem, places, step, 0, 0

    def open(self):
        self.base = 1
        return self.sem, 1

    def inc(self, key):
        self.count += 1
        self.places[key] = self.count
        return self.sem, self.step

    def at(self, it, key):
        return self.sem, (it * self.places.get("all", 1) + self.places.get(key, 1)) * self.step + self.base

    def once(self, key):
        return self.sem, self.places.get(key, 1) * self.step

    def before(self, it):
        return self.sem, it * self.places.get("all", 1) * self.step + self.base

    def close(self):
        self.places["all"] = self.count


class Ring:

    def __init__(self, tensor, full, free, places):
        self.tensor, self.full, self.free, self.places = tensor, full, free, places
        self.count = 0

    def open(self, eng):
        for sem in self.free:
            eng.sem_inc(sem, 1)

    def take(self, key):
        n, banks = self.count, len(self.full)
        self.places[key] = n
        self.count += 1
        return self.tensor[:, n % banks, :]

    def bank(self, key):
        return self.tensor[:, self.places.get(key, 0) % len(self.full), :]

    def _at(self, it, key, more):
        banks = len(self.full)
        n = self.places.get(key, 0)
        total = self.places.get("all", banks)
        each = total // banks + (n % banks < total % banks)
        return n % banks, it * each + n // banks + more

    def reusable(self, it, key):
        b, v = self._at(it, key, 1)
        return self.free[b], v

    def filled(self, it, key):
        b, v = self._at(it, key, 1)
        return self.full[b], v

    def emptied(self, it, key):
        b, v = self._at(it, key, 2)
        return self.free[b], v

    def fills(self, key):
        return self.full[self.places[key] % len(self.full)], 1

    def empties(self, key):
        return self.free[self.places.get(key, 0) % len(self.full)], 1

    def close(self):
        self.places["all"] = self.count


INPUTS = dict(
    x=(BATCH, SEQ, D), xT=(BATCH, D, SEQ), ctxT=(BATCH, CTX, SEQ),
    a0_wq=(D, E), a0_wk=(D, E), a0_wv=(D, E), a0_wo=(E, D),
    a1_wq=(D, E), a1_wqs=(D, E), a1_wk=(D, E), a1_wks=(D, E), a1_wv=(D, E), a1_wo=(E, D),
    a1_bq=(P, NC), a1_bqs=(P, NC), a1_bk=(P, NC), a1_bks=(P, NC), a1_bv=(1, E), a1_bo=(1, D),
    rope=(4, P, SEQ),
    s_wq=(D, D), s_wk=(D, D), s_wv=(D, D), s_bq=(D, 1), s_bk=(D, 1), s_bv=(1, D),
    c_wq=(D, D), c_wk=(CTX, D), c_wv=(CTX, D), c_bq=(D, 1), c_bk=(D, 1), c_bv=(1, D),
    p_w=(D, D), p_b=(1, D),
    z_wq=(D, D), z_wk=(CTX, D), z_wv=(CTX, D), z_wo=(D, D),
    f_slots=(SLOTS, D), f_slotsT=(D, SLOTS), f_w1=(2 * D, SLOTS), f_b1=(SLOTS, 1),
    f_w2=(SLOTS, SLOTS), f_b2=(1, SLOTS), f_tau=(1, 1),
    f_wihT=(D, 3 * D), f_whhT=(D, 3 * D), f_bih=(1, 3 * D), f_bhh=(1, 3 * D),
    f_wq=(D, DQ), f_bq=(DQ, 1), f_wk=(D, DQ), f_bk=(DQ, 1), f_wv=(D, D), f_bv=(1, D),
    f_lng=(1, D), f_lnb=(1, D), f_wvp=(D, D), f_bvp=(D, 1), f_wo=(D, D), f_bo=(1, D),
    m_wr=(D, NE), m_w1=(NE, D, FF), m_w2=(NE, FF, D), m_b=(1, D),
)


def build(nc, dram, out, places):
    with ExitStack() as ctx:
        def sb(name, shape, dt=F32):
            return ctx.enter_context(nc.sbuf_tensor(name, shape, dt))

        def psum(name, banks):
            tensor = ctx.enter_context(nc.psum_tensor(name, [P, banks, 512], F32))
            full = [ctx.enter_context(nc.semaphore(f"{name}_full{b}")) for b in range(banks)]
            free = [ctx.enter_context(nc.semaphore(f"{name}_free{b}")) for b in range(banks)]
            ring = Ring(tensor, full, free, places.setdefault(name, {}))
            closing.append(ring)
            return ring

        def signal(name, step=1):
            s = Signal(ctx.enter_context(nc.semaphore(name)), places.setdefault(name, {}), step)
            closing.append(s)
            return s

        closing = []

        loads = []

        def weight(name, shape=None, source=None):
            t = sb("w_" + name, list(shape or dram[name].shape))
            loads.append((t[:], dram[name] if source is None else source))
            return t

        def across(name, parts=P):
            n = dram[name].shape[1]
            t = sb("w_" + name, [parts, n])
            loads.append((t[:], dram[name].to_broadcast([parts, n])))
            return t

        def chunked(name, n):
            return weight(name, [P, n, D], dram[name].rearrange("(c p) h -> p c h", p=P))

        a0_wq, a0_wk, a0_wv = weight("a0_wq"), weight("a0_wk"), weight("a0_wv")
        a0_wo = chunked("a0_wo", NC)
        s_wq, s_wk, s_wv, s_bq, s_bk, s_bv = (weight("s_wq"), weight("s_wk"), weight("s_wv"),
                                              weight("s_bq"), weight("s_bk"), across("s_bv"))
        c_wq, c_wk, c_wv, c_bq, c_bk, c_bv = (weight("c_wq"), weight("c_wk"), weight("c_wv"),
                                              weight("c_bq"), weight("c_bk"), across("c_bv"))
        p_w, p_b = weight("p_w"), across("p_b")
        f_slots, f_slotsT = weight("f_slots"), weight("f_slotsT")
        f_w1 = weight("f_w1", [P, 2, SLOTS], dram["f_w1"].rearrange("(c p) h -> p c h", p=P))
        f_b1, f_b2, f_w2, f_tau = weight("f_b1"), across("f_b2"), weight("f_w2"), across("f_tau")
        f_wih, f_whh = weight("f_wihT"), weight("f_whhT")
        f_bih, f_bhh = across("f_bih", SLOTS), across("f_bhh", SLOTS)
        f_wq, f_bq, f_wk, f_bk = weight("f_wq"), weight("f_bq"), weight("f_wk"), weight("f_bk")
        f_wv, f_bv = weight("f_wv"), across("f_bv", SLOTS)
        f_lng, f_lnb = across("f_lng", SLOTS), across("f_lnb", SLOTS)
        f_wvp, f_bvp, f_wo, f_bo = weight("f_wvp"), weight("f_bvp"), weight("f_wo"), across("f_bo")
        a1_wq, a1_wqs, a1_wk, a1_wks = (weight("a1_wq"), weight("a1_wqs"), weight("a1_wk"),
                                        weight("a1_wks"))
        a1_wv, a1_wo = weight("a1_wv"), chunked("a1_wo", NC)
        a1_bq, a1_bqs, a1_bk, a1_bks = (weight("a1_bq"), weight("a1_bqs"), weight("a1_bk"),
                                        weight("a1_bks"))
        a1_bv, a1_bo = across("a1_bv"), across("a1_bo")
        rope = weight("rope", [P, 4, SEQ], dram["rope"].rearrange("a p n -> p a n"))
        z_wq, z_wk, z_wv, z_wo = weight("z_wq"), weight("z_wk"), weight("z_wv"), weight("z_wo")
        m_wr, m_b = weight("m_wr"), across("m_b")

        ident = sb("ident", [P, P])
        identb = sb("identb", [P, P], BF16)
        ones = sb("ones", [P, P])
        onesb = sb("onesb", [P, P], BF16)
        mask = sb("mask", [P, P], BF16)
        maskT = sb("maskT", [P, P], BF16)
        earlier = sb("earlier", [P, P], BF16)
        head_rows = sb("head_rows", [NH, NC, P])

        xa = sb("xa", [P, TT, D + 1])
        xb = sb("xb", [P, TT, D])
        xT = sb("xT", [P, TOK])
        ctxT = sb("ctxT", [CTX, TOK])
        stats = sb("stats", [P, TT, 6])
        mv = sb("mv", [P, TT, 2])
        ve = sb("ve", [P, TT])
        rstd = sb("rstd", [P, TT])
        half = sb("half", [P, TT])

        qT = sb("qT", [P, NC, TOK])
        kT = sb("kT", [P, NC, TOK])
        vv = sb("vv", [P, TT, E])
        oT = sb("oT", [P, NC, TOK])
        NPR = 3
        probs = sb("probs", [P, NPR, 3 * P])
        probsT = sb("probsT", [P, 4, 3 * P])
        nmax = sb("nmax", [P, 4, 2])
        sums = sb("sums", [P, TT, NH])
        rsum = sb("rsum", [P, TT, NH])
        rot = sb("rot", [P, 2, 2, TOK])

        def over(host, rows, shape, dt=F32, phase="small heads"):
            n = int(np.prod(shape)) // (2 if dt == BF16 else 1)
            at = taken.setdefault((host.name, phase), 0)
            taken[host.name, phase] = at + n
            flat_host = host[:].rearrange("p a b -> p (a b)")
            assert at + n <= flat_host.shape[1]
            v = flat_host[0:rows, at:at + n]
            v = v.bitcast(BF16) if dt == BF16 else v
            if len(shape) == 1:
                return v
            names = "abc"[:len(shape)]
            return v.rearrange(f"p ({' '.join(names)}) -> p {' '.join(names)}",
                               **dict(zip(names[1:], shape[1:])))

        taken = {}
        xr = over(vv, P, [TT, D], phase="norm")
        rT = over(qT, NH, [TOK], phase="row sums")

        flat = over(kT, P, [2, TOK])
        rest = over(kT, P, [2, TOK])
        part = over(qT, P, [2, PARTS, TOK], BF16)
        qs = sb("qs", [P, NH, TOK], BF16)
        ks = sb("ks", [P, NH, TOK], BF16)
        VA = NH * VW + 32 - VW
        va = sb("va", [P, TT, VA])
        nm = sb("nm", [P, TT, NH])
        nmf = over(qT, NH, [TOK])
        nmr = over(qT, NH, [TOK])
        nmp = over(qT, NH, [PARTS, TOK], BF16)
        NPX = 8
        px = vv[:].rearrange("p a b -> p (a b)").rearrange("p (s n) -> p s n", s=NPX)
        og = over(kT, P, [2, SEQ])
        den = sb("den", [P, NG, TT, HG])
        ys = over(qT, P, [TT, D])
        yc = over(kT, P, [TT, D])
        yT = over(kT, P, [TOK])

        c1 = sb("c1", [SLOTS, 1])
        smean = sb("smean", [P, 1])
        itau = sb("itau", [P, 1])
        crz = sb("crz", [SLOTS, 3 * D])
        ghn = sb("ghn", [SLOTS, D])
        hT = over(oT, SLOTS, [TOK])
        lg = over(oT, P, [TT, 2, SLOTS])
        top = sb("top", [P, TT, 8])
        ntop = sb("ntop", [P, TT])
        ex = over(oT, P, [TT, 2, SLOTS])
        alpha = over(kT, P, [TT, SLOTS], phase="slots")
        asum = sb("asum", [P, TT])
        arec = sb("arec", [P, TT])
        alphaT = over(oT, SLOTS, [TOK])
        dn = sb("dn", [SLOTS, PAIR])
        si = over(kT, SLOTS, [PAIR, D], phase="slots")
        siT = over(kT, P, [PAIR * SLOTS], phase="slots")
        gate = over(oT, SLOTS, [PAIR, 3 * D])
        ge = over(oT, SLOTS, [PAIR, 2 * D])
        rz = over(oT, SLOTS, [PAIR, 2 * D])
        gn = over(oT, SLOTS, [PAIR, D])
        sn = over(kT, SLOTS, [PAIR, D], phase="slots")
        snT = over(kT, P, [PAIR * SLOTS], phase="slots")
        sq = sb("sq", [DQ, PAIR * SLOTS])
        sk = sb("sk", [DQ, PAIR * SLOTS])
        svv = over(kT, SLOTS, [PAIR, D], phase="slots")
        sm = sb("sm", [SLOTS, PAIR, 4])
        sp_ = over(kT, SLOTS, [PAIR, SLOTS], phase="slots")
        spT = over(kT, SLOTS, [PAIR * SLOTS], phase="slots")
        sy = over(kT, SLOTS, [PAIR, D], phase="slots")
        sst = sb("sst", [SLOTS, PAIR, 6])
        smv = sb("smv", [SLOTS, PAIR, 2])
        srs = sb("srs", [SLOTS, PAIR, 2])
        syT = over(kT, P, [PAIR * SLOTS], phase="slots")
        svT = over(kT, P, [PAIR * SLOTS], phase="slots")
        svo = over(kT, SLOTS, [PAIR, D], phase="slots")

        hid = oT[:].rearrange("p c n -> p (c n)").rearrange("p (s f n) -> p s f n", s=2, f=FC)
        w1e = rot[:, 0].rearrange("p a n -> p (a n)").rearrange("p (s n) -> p s n", s=2)
        w2e = rot[:, 1].rearrange("p a n -> p (a n)").rearrange("p (s f n) -> p s f n", s=2, f=FC)
        RW = NE + 8 - TOP
        rl = sb("rl", [P, TT, 2, RW])
        rtop = sb("rtop", [P, TT, 8])
        rtwo = sb("rtwo", [P, TT, 8])
        nrt = sb("nrt", [P, TT])
        rex = sb("rex", [P, TT, 2, NE])
        rden = sb("rden", [P, TT])
        rrec = sb("rrec", [P, TT])
        chosen = sb("chosen", [P, TT, NE])
        chosenb = sb("chosenb", [P, TT, NE], BF16)
        seen = sb("seen", [P, TT + 1, NE])
        seenb = sb("seenb", [P, TT, NE], BF16)
        fits = sb("fits", [P, TT, NE])
        wexp = sb("wexp", [P, TT, NE])
        wgt = sb("wgt", [P, TT, NE])
        acc = over(kT, P, [TT, D], phase="experts")

        scores = psum("scores", 3)
        turned = psum("turned", 2)
        outs = psum("outs", 1)
        misc = psum("misc", 2)

        s_load = signal("weights_loaded", 16)
        s_const = signal("constants_made")
        s_fill = signal("fills_made")
        s_in = signal("x_loaded", 16)
        s_out = signal("y_stored", 16)
        s_split = signal("parts_stored", 16)
        s_stack = signal("parts_stacked", 16)
        s_mrow = signal("maxima_placed", 16)
        s_wexp = [signal(f"expert_loaded{b}", 16) for b in range(2)]
        s_dv = signal("vector_made")
        s_ac = signal("scalar_made")
        s_po = signal("pool_made")
        pre = signal("slot_terms_summed")
        pred = signal("slot_terms_made")
        passed = ctx.enter_context(nc.semaphore("passed"))
        parts_d = [[nc.dram_tensor(f"parts{a}{b}", (PARTS, P, TOK), BF16, kind="Internal").ap()
                    for b in range(2)] for a in range(3)]

        block = ctx.enter_context(nc.Block())
        XATT = ("self", "cross", "last")

        def settle(eng):
            eng.sem_inc(passed, 1)

        SCALE = {"self": DX ** -0.5, "cross": DX ** -0.5, "last": DX ** -0.5}

        def units():
            for c in range(NC):
                for u in range(PAIR):
                    for r in range(2):
                        yield c, u, r

        order = list(units())
        xorder = [(u, h) for u in range(PAIR) for h in range(NH)]

        @block.sync
        def _(sync):
            for sig in (s_out, s_split, s_mrow):
                sync.sem_inc(*sig.open())
            for dst, src in loads:
                sync.dma_start(dst, src).then_inc(*s_load.inc("w"))
            sync.wait_ge(*s_const.once("c"))
            with sync.Fori(0, ITERS) as it:
                def store_and_stack(k, which):
                    a = XATT.index(k)
                    sync.wait_ge(*s_po.at(it, (k, which, "low")))
                    sync.dma_start(parts_d[a][which].rearrange("a p n -> p a n"),
                                   part[:, which]).then_inc(*s_split.inc((k, which)))
                    sync.wait_ge(*s_split.at(it, (k, which)))
                    dst = (qs, ks)[which]
                    for i in range(PARTS):
                        for j in range(PARTS):
                            piece = (i, j)[which]
                            row = (PARTS * i + j) * DX
                            sync.dma_start(dst[row:row + DX],
                                           parts_d[a][which][piece].rearrange("(h d) n -> d h n", d=DX))\
                                .then_inc(*s_stack.inc((k, which)))

                def xattn(k, free):
                    for which in range(2):
                        if which == 0 and free is not None:
                            sync.wait_ge(*outs.emptied(it, free))
                            settle(sync)
                        store_and_stack(k, which)
                    sync.wait_ge(*s_dv.at(it, (k, "nmlow")))
                    for i in range(PARTS):
                        sync.dma_start(qs[MROW + i:MROW + i + 1].rearrange("p h n -> p (h n)"),
                                       nmp[:, i, :]).then_inc(*s_mrow.inc(k))

                sync.wait_ge(*s_out.before(it))
                settle(sync)
                for u in range(PAIR):
                    sync.dma_start(xa[:, 2 * u:2 * u + 2, 0:D],
                                   dram["x"][bass.ds(it * PAIR + u, 1)].rearrange("b (t p) d -> p (b t) d", p=P))\
                        .then_inc(*s_in.inc("x"))
                    sync.dma_start(xT[:, u * SEQ:(u + 1) * SEQ],
                                   dram["xT"][bass.ds(it * PAIR + u, 1)].rearrange("b p n -> p (b n)"))\
                        .then_inc(*s_in.inc("x"))
                    sync.dma_start(ctxT[:, u * SEQ:(u + 1) * SEQ],
                                   dram["ctxT"][bass.ds(it * PAIR + u, 1)].rearrange("b p n -> p (b n)"))\
                        .then_inc(*s_in.inc("x"))
                xattn("self", None)
                xattn("cross", ("self", "o", PAIR - 1, NG - 1))
                xattn("last", ("cross", "o", PAIR - 1, NG - 1))
                for e in range(NE):
                    if e >= 2:
                        sync.wait_ge(*misc.filled(it, ("moe", "y", e - 2)))
                    sync.dma_start(w1e[:, e % 2], dram["m_w1"][e]).then_inc(*s_wexp[e % 2].inc(e))
                    sync.dma_start(w2e[:, e % 2], dram["m_w2"][e].rearrange("(c p) h -> p c h", p=P))\
                        .then_inc(*s_wexp[e % 2].inc(e))
                sync.wait_ge(*s_dv.at(it, ("ln", "moe", "x")))
                settle(sync)
                for u in range(PAIR):
                    sync.dma_start(out[bass.ds(it * PAIR + u, 1)].rearrange("b (t p) d -> p (b t) d", p=P),
                                   xa[:, 2 * u:2 * u + 2, 0:D]).then_inc(*s_out.inc("y"))
            sync.wait_ge(*s_out.before(ITERS))

        @block.gpsimd
        def _(pool):
            g = nc.gpsimd
            fills = [(ident, 0.0), (identb, 0.0), (ones, 1.0), (onesb, 1.0), (mask, 0.0), (maskT, 0.0),
                     (earlier, 1.0), (head_rows, 1.0), (half, -0.5), (xa, 1.0), (qs, 0.0), (ks, 0.0),
                     (va, 1.0), (seen, 0.0), (rtwo, FAR), (rl, FAR)]
            for t, v in fills:
                g.memset(t[:], v).then_inc(*s_fill.inc("fill"))
            pool.wait_ge(s_fill.sem, len(fills))
            for t in (ident, identb):
                g.affine_select(out=t[:], in_=t[:], compare_op=ALU.not_equal, fill=1.0, base=0,
                                pattern=[[-1, P]], channel_multiplier=1).then_inc(*s_const.inc("c"))
            g.affine_select(out=mask[:], in_=mask[:], compare_op=ALU.is_ge, fill=MASKED, base=0,
                            pattern=[[-1, P]], channel_multiplier=1).then_inc(*s_const.inc("c"))
            g.affine_select(out=maskT[:], in_=maskT[:], compare_op=ALU.is_ge, fill=MASKED, base=0,
                            pattern=[[1, P]], channel_multiplier=-1).then_inc(*s_const.inc("c"))
            g.affine_select(out=earlier[:], in_=earlier[:], compare_op=ALU.is_gt, fill=0.0, base=0,
                            pattern=[[1, P]], channel_multiplier=-1).then_inc(*s_const.inc("c"))
            hr = head_rows[:]
            g.affine_select(out=hr, in_=hr, compare_op=ALU.is_ge, fill=0.0, base=0,
                            pattern=[[P, NC], [1, P]], channel_multiplier=-HD).then_inc(*s_const.inc("c"))
            pool.wait_ge(*s_const.once("c"))
            g.affine_select(out=hr, in_=hr, compare_op=ALU.is_gt, fill=0.0, base=HD,
                            pattern=[[-P, NC], [-1, P]], channel_multiplier=HD).then_inc(*s_const.inc("c"))
            g.memset(ks[MROW:MROW + PARTS], 1.0).then_inc(*s_const.inc("c"))
            pool.wait_ge(*s_load.once("w"))

            with pool.Fori(0, ITERS) as it:
                def add_bias(name, bias, after):
                    pool.wait_ge(*after)
                    if bias is None:
                        settle(pool)
                        g.tensor_copy(xb[:], xa[:, :, 0:D]).then_inc(*s_po.inc(("xb", name)))
                    else:
                        g.tensor_tensor(out=xb[:], in0=xa[:, :, 0:D],
                                        in1=bias[:].unsqueeze(1).to_broadcast([P, TT, D]),
                                        op=ALU.add).then_inc(*s_po.inc(("xb", name)))

                def rsqrt(name, n, parts, dst, src, exponent):
                    pool.wait_ge(*s_dv.at(it, (name, "ve")))
                    g.tensor_tensor(out=dst, in0=src, in1=exponent, op=ALU.pow)\
                        .then_inc(*s_po.inc((name, "rstd")))

                def norm(name):
                    rsqrt(("ln", name), TT, P, rstd[:], ve[:], half[:])

                def split(k):
                    for w in range(2):
                        pool.wait_ge(*s_ac.at(it, (k, w, "high")))
                        g.tensor_tensor(out=rest[:, w], in0=flat[:, w], in1=part[:, w, 0],
                                        op=ALU.subtract).then_inc(*s_po.inc((k, w, "rest")))
                        pool.wait_ge(*s_ac.at(it, (k, w, "mid")))
                        g.tensor_tensor(out=part[:, w, 2], in0=rest[:, w], in1=part[:, w, 1],
                                        op=ALU.subtract).then_inc(*s_po.inc((k, w, "low")))

                pool.wait_ge(*s_in.at(it, "x"))
                add_bias("a0", None, s_in.at(it, "x"))
                norm("a0")
                add_bias("x0", p_b, s_dv.at(it, ("ln", "a0", "x")))
                split("self")
                split("cross")
                norm("x0")
                add_bias("f0", f_bo, s_dv.at(it, ("ln", "x0", "x")))
                rsqrt(("ln", "slots"), PAIR, SLOTS, srs[:, :, 1], srs[:, :, 0], half[0:SLOTS, 0:PAIR])
                norm("f0")
                add_bias("a1", a1_bo, s_dv.at(it, ("ln", "f0", "x")))
                for c in range(NC):
                    for w in range(2):
                        n = 2 * c + w
                        for j in range(2):
                            pool.wait_ge(*misc.emptied(it, ("a1", w, j, c)))
                        g.tensor_tensor(out=(qT, kT)[w][:, c], in0=rot[:, n % 2, 0], in1=rot[:, n % 2, 1],
                                        op=ALU.add).then_inc(*s_po.inc(("qk1", c, w)))
                norm("a1")
                add_bias("x1", None, s_dv.at(it, ("ln", "a1", "x")))
                split("last")
                norm("x1")
                add_bias("moe", m_b, s_dv.at(it, ("ln", "x1", "x")))
                norm("moe")

        @block.scalar
        def _(act):
            a = nc.scalar
            act.wait_ge(*s_load.once("w"))
            act.wait_ge(*s_const.once("c"))
            with act.Fori(0, ITERS) as it:
                def attn64(L):
                    def project(c):
                        if L == 0:
                            for w, dst, sc in ((0, qT, HD ** -0.5), (1, kT, 1.0)):
                                act.wait_ge(*misc.filled(it, ("a0", w, c)))
                                a.activation(dst[:, c], misc.bank(("a0", w, c)), ACT.Copy, scale=sc)\
                                    .then_inc(*misc.empties(("a0", w, c)))
                    project(0)
                    for i, (c, u, r) in enumerate(units()):
                        if L == 0 and i % 4 == 0 and c + 1 < NC:
                            project(c + 1)
                        key = (L, "s", c, u, r)
                        h = 2 * c + r
                        if i >= 5 and i % 2 == 1:
                            out_copy(L, (i - 5) // 2)
                        act.wait_ge(*s_dv.at(it, (L, "max", c, u, r)))
                        if i >= NPR:
                            act.wait_ge(*turned.filled(it, (L, "t", *order[i - NPR])))
                        s = scores.bank(key)
                        for t, (lo, hi) in enumerate(((0, P), (P, 3 * P))):
                            ins = a.activation(probs[:, i % NPR, lo:hi], s[:, lo:hi], ACT.Exp,
                                               bias=nmax[:, i % 4, t:t + 1],
                                               accum_out=sums[:, 2 * u + t, h:h + 1])
                        ins.then_inc(*scores.empties(key))
                        if i >= 2 and (i - 2) % 4 == 3:
                            turn_copy(L, i - 2)
                    n = len(order)
                    out_copy(L, n // 2 - 2)
                    turn_copy(L, n - 1)
                    out_copy(L, n // 2 - 1)
                    act.wait_ge(*misc.filled(it, (L, "rT")))
                    a.activation(rT[:], misc.bank((L, "rT"))[0:NH], ACT.Copy)\
                        .then_inc(*misc.empties((L, "rT")))

                def turn_copy(L, i):
                    c, u, r = order[i]
                    act.wait_ge(*turned.filled(it, (L, "t", c, u, r)))
                    if i >= 4:
                        act.wait_ge(*outs.filled(it, (L, "o", *order[i - 4][:2])))
                    a.activation(probsT[:, i % 4], turned.bank((L, "t", c, u, r))[:, 0:3 * P], ACT.Copy)\
                        .then_inc(*turned.empties((L, "t", c, u, r)))

                def out_copy(L, j):
                    c, u = order[2 * j][:2]
                    act.wait_ge(*outs.filled(it, (L, "o", c, u)))
                    a.activation(oT[:, c, u * SEQ:(u + 1) * SEQ], outs.bank((L, "o", c, u))[:, 0:SEQ], ACT.Copy)\
                        .then_inc(*outs.empties((L, "o", c, u)))

                def to_xT(name):
                    act.wait_ge(*misc.filled(it, ("xT", name)))
                    a.activation(xT[:], misc.bank(("xT", name)), ACT.Copy)\
                        .then_inc(*misc.empties(("xT", name)))

                def split(k):
                    for w in range(2):
                        act.wait_ge(*misc.emptied(it, (k, w)))
                        a.activation(part[:, w, 0], flat[:, w], ACT.Copy).then_inc(*s_ac.inc((k, w, "high")))
                        act.wait_ge(*s_po.at(it, (k, w, "rest")))
                        a.activation(part[:, w, 1], rest[:, w], ACT.Copy).then_inc(*s_ac.inc((k, w, "mid")))

                def xattn(k):
                    split(k)
                    act.wait_ge(*misc.filled(it, (k, "nmT")))
                    a.activation(nmf[:], misc.bank((k, "nmT"))[0:NH], ACT.Copy)\
                        .then_inc(*misc.empties((k, "nmT")))
                    width = 3 * P if k == "self" else 2 * SEQ
                    for i, (u, h) in enumerate(xorder):
                        key = (k, "st", u, h)
                        act.wait_ge(*scores.filled(it, key))
                        if i >= NPX:
                            act.wait_ge(*outs.filled(it, (k, "o", xorder[i - NPX][0], xorder[i - NPX][1] // HG)))
                        a.activation(px[:, i % NPX, 0:width], scores.bank(key)[:, 0:width], ACT.Exp)\
                            .then_inc(*scores.empties(key))
                        if i >= 6 and (i - 6) % HG == 0:
                            og_copy(k, (i - 6) // HG)
                    og_copy(k, len(xorder) // HG - 1)

                def og_copy(k, n):
                    u, gr = n // NG, n % NG
                    act.wait_ge(*outs.filled(it, (k, "o", u, gr)))
                    if n >= 2:
                        act.wait_ge(*turned.filled(it, (k, "ot", (n - 2) // NG, (n - 2) % NG)))
                    a.activation(og[:, n % 2, 0:SEQ], outs.bank((k, "o", u, gr))[:, 0:SEQ], ACT.Copy)\
                        .then_inc(*outs.empties((k, "o", u, gr)))

                def to_yT(k):
                    act.wait_ge(*misc.filled(it, (k, "yT")))
                    a.activation(yT[:], misc.bank((k, "yT")), ACT.Copy).then_inc(*misc.empties((k, "yT")))

                attn64(0)
                to_xT("a0")
                xattn("self")
                xattn("cross")
                to_yT("x0")
                to_xT("x0")

                act.wait_ge(*misc.filled(it, ("f", "h")))
                act.wait_ge(*s_dv.once("c1"))
                a.activation(hT[:], misc.bank(("f", "h"))[0:SLOTS], ACT.Gelu, bias=c1[:, 0:1])\
                    .then_inc(*misc.empties(("f", "h")))
                for t in range(TT):
                    act.wait_ge(*s_dv.at(it, ("f", "struck", t)))
                    ins = a.activation(ex[:, t], lg[:, t], ACT.Exp, bias=ntop[:, t:t + 1])
                    ins.then_inc(*s_ac.inc(("f", "ex", t)))
                act.wait_ge(*misc.filled(it, ("f", "aT")))
                a.activation(alphaT[:], misc.bank(("f", "aT"))[0:SLOTS], ACT.Copy)\
                    .then_inc(*misc.empties(("f", "aT")))
                act.wait_ge(*misc.filled(it, ("f", "siT")))
                a.activation(siT[:], misc.bank(("f", "siT"))[:, 0:PAIR * SLOTS], ACT.Copy)\
                    .then_inc(*misc.empties(("f", "siT")))
                act.wait_ge(*outs.emptied(it, ("f", "gi", PAIR - 1)))
                a.activation(ge[:], gate[:, :, 0:2 * D], ACT.Exp, scale=-1.0).then_inc(*s_ac.inc(("f", "ge")))
                act.wait_ge(*s_dv.at(it, ("f", "npre")))
                a.activation(gn[:], gate[:, :, 2 * D:3 * D], ACT.Tanh).then_inc(*s_ac.inc(("f", "gn")))
                act.wait_ge(*misc.filled(it, ("f", "snT")))
                a.activation(snT[:], misc.bank(("f", "snT"))[:, 0:PAIR * SLOTS], ACT.Copy)\
                    .then_inc(*misc.empties(("f", "snT")))
                for u in range(PAIR):
                    act.wait_ge(*s_dv.at(it, ("f", "smax", u)))
                    a.activation(sp_[:, u], misc.bank(("f", "ss"))[0:SLOTS, u * SLOTS:(u + 1) * SLOTS], ACT.Exp,
                                 bias=sm[:, u, 1:2], scale=DQ ** -0.5,
                                 accum_out=sm[:, u, 2:3]).then_inc(
                                     *(misc.empties(("f", "ss")) if u == PAIR - 1 else s_ac.inc(("f", "sp", u))))
                act.wait_ge(*misc.filled(it, ("f", "spT")))
                a.activation(spT[:], misc.bank(("f", "spT"))[0:SLOTS, 0:PAIR * SLOTS], ACT.Copy)\
                    .then_inc(*misc.empties(("f", "spT")))
                act.wait_ge(*misc.filled(it, ("f", "syT")))
                a.activation(syT[:], misc.bank(("f", "syT"))[:, 0:PAIR * SLOTS], ACT.Copy)\
                    .then_inc(*misc.empties(("f", "syT")))
                to_xT("f0")

                attn64(1)
                to_xT("a1")
                xattn("last")
                to_yT("x1")
                to_xT("x1")

                for t in range(TT):
                    act.wait_ge(*s_dv.at(it, ("m", "struck", t)))
                    a.activation(rex[:, t], rl[:, t, :, 0:NE], ACT.Exp, bias=nrt[:, t:t + 1])\
                        .then_inc(*s_ac.inc(("m", "ex", t)))
                for e in range(NE):
                    for f in range(FC):
                        act.wait_ge(*scores.filled(it, ("moe", "h", e, f)))
                        if e >= 2:
                            act.wait_ge(*misc.filled(it, ("moe", "y", e - 2)))
                        a.activation(hid[:, e % 2, f], scores.bank(("moe", "h", e, f)), ACT.Gelu_apprx_tanh)\
                            .then_inc(*scores.empties(("moe", "h", e, f)))

        @block.vector
        def _(dve):
            v = nc.vector
            dve.wait_ge(*s_load.once("w"))
            dve.wait_ge(*s_const.once("c"))
            dve.wait_ge(*pre.at(0, "smean"))
            v.tensor_scalar(smean[:], misc.tensor[:, 0, 0:1], 1.0 / SLOTS, None, ALU.mult)\
                .then_inc(*pred.inc("smean"))
            dve.wait_ge(*pre.at(0, "c1"))
            v.tensor_tensor(out=c1[:], in0=misc.tensor[0:SLOTS, 0, 8:9], in1=f_b1[:], op=ALU.add)\
                .then_inc(*pred.inc("c1"))
            v.tensor_tensor(out=crz[:], in0=misc.tensor[0:SLOTS, 1, 0:3 * D], in1=f_bhh[:], op=ALU.add)\
                .then_inc(*pred.inc("crz"))
            dve.wait_ge(*pred.once("crz"))
            v.tensor_copy(ghn[:], crz[:, 2 * D:3 * D]).then_inc(*pred.inc("ghn"))
            dve.wait_ge(*pred.once("ghn"))
            v.tensor_tensor(out=crz[:, 0:2 * D], in0=crz[:, 0:2 * D], in1=f_bih[:, 0:2 * D], op=ALU.add)\
                .then_inc(*pred.inc("a"))
            v.tensor_copy(crz[:, 2 * D:3 * D], f_bih[:, 2 * D:3 * D]).then_inc(*pred.inc("b"))
            v.tensor_scalar(itau[:], f_tau[:, 0:1], -1.0, None, ALU.mult).then_inc(*pred.inc("t0"))
            dve.wait_ge(*pred.once("t0"))
            v.tensor_tensor(out=itau[:], in0=itau[:], in1=f_tau[:, 0:1], op=ALU.max).then_inc(*pred.inc("t1"))
            dve.wait_ge(*pred.once("t1"))
            v.tensor_scalar(itau[:], itau[:], 0.1, None, ALU.add).then_inc(*pred.inc("t2"))
            dve.wait_ge(*pred.once("t2"))
            v.reciprocal(itau[:], itau[:]).then_inc(*pred.inc("t3"))
            dve.wait_ge(*pred.once("t3"))

            with dve.Fori(0, ITERS) as it:
                def link(ins, key):
                    ins.then_inc(*s_dv.inc(key))
                    dve.wait_ge(*s_dv.at(it, key))

                def attn64(L):
                    def project(c):
                        if L == 0:
                            return
                        for w in range(2):
                            n = 2 * c + w
                            if n >= 2:
                                dve.wait_ge(*s_po.at(it, ("qk1", (n - 2) // 2, n % 2)))
                            for j in range(2):
                                key = ("a1", w, j, c)
                                dve.wait_ge(*misc.filled(it, key))
                                b = ((a1_bq, a1_bqs), (a1_bk, a1_bks))[w][j]
                                ins = v.scalar_tensor_tensor(
                                    out=rot[:, n % 2, j].rearrange("p (u n) -> p u n", u=PAIR),
                                    in0=misc.bank(key).rearrange("p (u n) -> p u n", u=PAIR),
                                    scalar=b[:, c:c + 1],
                                    in1=rope[:, 2 * w + j].unsqueeze(1).to_broadcast([P, PAIR, SEQ]),
                                    op0=ALU.add, op1=ALU.mult)
                                ins.then_inc(*misc.empties(key))

                    for t in range(TT):
                        for hf in range(2):
                            key = (L, "v", t, hf)
                            dve.wait_ge(*misc.filled(it, key))
                            dst = vv[:, t, hf * 512:(hf + 1) * 512]
                            if L == 0:
                                v.tensor_copy(dst, misc.bank(key)).then_inc(*misc.empties(key))
                            else:
                                v.tensor_tensor(out=dst, in0=misc.bank(key),
                                                in1=a1_bv[:, hf * 512:(hf + 1) * 512], op=ALU.add)\
                                    .then_inc(*misc.empties(key))
                    project(0)
                    n = len(order)
                    for i in range(n + 2):
                        if i < n:
                            c, u, r = order[i]
                            if i % 4 == 0 and c + 1 < NC:
                                project(c + 1)
                            key = (L, "s", c, u, r)
                            dve.wait_ge(*scores.filled(it, key))
                            if i >= 4:
                                dve.wait_ge(*scores.emptied(it, (L, "s", *order[i - 4])))
                            s = scores.bank(key)
                            v.tensor_reduce(nmax[:, i % 4, 0:1], s[:, 0:P], AX.X, ALU.max, negate=True)
                            v.tensor_reduce(nmax[:, i % 4, 1:2], s[:, P:3 * P], AX.X, ALU.max, negate=True)\
                                .then_inc(*s_dv.inc((L, "max", c, u, r)))
                        if i >= 2 and (i - 2) % 4 != 3:
                            j = i - 2
                            c, u, r = order[j]
                            dve.wait_ge(*turned.filled(it, (L, "t", c, u, r)))
                            if j >= 4:
                                dve.wait_ge(*outs.filled(it, (L, "o", *order[j - 4][:2])))
                            v.tensor_copy(probsT[:, j % 4], turned.bank((L, "t", c, u, r))[:, 0:3 * P])\
                                .then_inc(*turned.empties((L, "t", c, u, r)))
                    dve.wait_ge(*scores.emptied(it, (L, "s", *order[-1])))
                    dve.wait_ge(*scores.emptied(it, (L, "s", *order[-2])))
                    v.reciprocal(rsum[:], sums[:]).then_inc(*s_dv.inc((L, "rsum")))
                    for c in range(NC):
                        dve.wait_ge(*misc.filled(it, (L, "R", c)))
                        dve.wait_ge(*outs.emptied(it, (L, "o", c, PAIR - 1)))
                        v.tensor_tensor(out=oT[:, c], in0=oT[:, c], in1=misc.bank((L, "R", c)), op=ALU.mult)\
                            .then_inc(*misc.empties((L, "R", c)))

                def norm(name, src, last):
                    dve.wait_ge(*s_po.at(it, ("xb", name)))
                    if last is None:
                        dve.wait_ge(*misc.filled(it, src))
                        y = misc.bank(src).rearrange("p (t d) -> p t d", t=TT)
                        v.tensor_tensor(out=xr[:], in0=xb[:], in1=y, op=ALU.add)\
                            .then_inc(*misc.empties(src))
                        dve.wait_ge(*misc.emptied(it, src))
                    else:
                        link(v.tensor_tensor(out=xr[:], in0=xb[:], in1=acc[:], op=ALU.add), ("ln", name, "r"))
                    for t in range(TT):
                        ins = v.bn_stats(stats[:, t], xr[:, t])
                    link(ins, ("ln", name, "stats"))
                    settle(dve)
                    for t in range(TT):
                        ins = v.bn_aggr(mv[:, t], stats[:, t])
                    link(ins, ("ln", name, "mv"))
                    v.tensor_scalar(ve[:], mv[:, :, 1], EPS, None, ALU.add).then_inc(*s_dv.inc((("ln", name), "ve")))
                    dve.wait_ge(*s_po.at(it, (("ln", name), "rstd")))
                    for t in range(TT):
                        ins = v.tensor_scalar(xa[:, t, 0:D], xr[:, t], mv[:, t, 0:1], rstd[:, t:t + 1],
                                              ALU.subtract, ALU.mult)
                    ins.then_inc(*s_dv.inc(("ln", name, "x")))

                def xattn(k, bq, bk, bv, dest):
                    for w, b in ((0, bq), (1, bk)):
                        dve.wait_ge(*misc.filled(it, (k, w)))
                        dve.wait_ge(*(s_split.before(it) if k == "self" else
                                      s_split.at(it, (XATT[XATT.index(k) - 1], 1))))
                        sc = SCALE[k] if w == 0 else 1.0
                        if b is None:
                            ins = v.tensor_scalar(flat[:, w], misc.bank((k, w)), sc, None, ALU.mult)
                        else:
                            ins = v.tensor_scalar(flat[:, w], misc.bank((k, w)), b[:, 0:1], sc, ALU.add, ALU.mult)
                        ins.then_inc(*misc.empties((k, w)))
                    dve.wait_ge(*misc.filled(it, (k, "v")))
                    dst = va[:, :, 0:NH * VW].rearrange("p t (h w) -> p t h w", w=VW)[:, :, :, 0:DX]
                    src = misc.bank((k, "v")).rearrange("p (t h d) -> p t h d", t=TT, h=NH)
                    if bv is None:
                        v.tensor_copy(dst, src).then_inc(*misc.empties((k, "v")))
                    else:
                        for t in range(TT):
                            ins = v.tensor_tensor(out=dst[:, t], in0=src[:, t],
                                                  in1=bv[:].rearrange("p (h d) -> p h d", h=NH), op=ALU.add)
                        ins.then_inc(*misc.empties((k, "v")))
                    for u, h in xorder:
                        key = (k, "s", u, h)
                        dve.wait_ge(*scores.filled(it, key))
                        s = scores.bank(key)
                        if k == "self":
                            v.tensor_reduce(nm[:, 2 * u, h:h + 1], s[:, 0:P], AX.X, ALU.max, negate=True)
                            ins = v.tensor_reduce(nm[:, 2 * u + 1, h:h + 1], s[:, P:3 * P], AX.X, ALU.max,
                                                  negate=True)
                        else:
                            ins = v.tensor_reduce(nm[:, 2 * u:2 * u + 2, h],
                                                  s.rearrange("p (t n) -> p t n", t=2), AX.X, ALU.max,
                                                  negate=True)
                        ins.then_inc(*scores.empties(key))
                    dve.wait_ge(*misc.emptied(it, (k, "nmT")))
                    dve.wait_ge(*(s_mrow.before(it) if k == "self" else
                                  s_mrow.at(it, XATT[XATT.index(k) - 1])))
                    link(v.tensor_copy(nmp[:, 0], nmf[:]), (k, "nmhigh"))
                    link(v.tensor_tensor(out=nmr[:], in0=nmf[:], in1=nmp[:, 0], op=ALU.subtract), (k, "nmrest"))
                    link(v.tensor_copy(nmp[:, 1], nmr[:]), (k, "nmmid"))
                    v.tensor_tensor(out=nmp[:, 2], in0=nmr[:], in1=nmp[:, 1], op=ALU.subtract)\
                        .then_inc(*s_dv.inc((k, "nmlow")))
                    for n in range(PAIR * NG):
                        u, gr = n // NG, n % NG
                        key = (k, "ot", u, gr)
                        dve.wait_ge(*turned.filled(it, key))
                        o = turned.bank(key)[:, 0:2 * P].rearrange("p (t h w) -> p t h w", t=2, h=HG)
                        link(v.reciprocal(den[:, gr, 2 * u:2 * u + 2, :], o[:, :, :, DX]), (k, "den", u, gr))
                        d = den[:, gr, 2 * u:2 * u + 2, :].unsqueeze(3).to_broadcast([P, 2, HG, DX])
                        dst = dest[:, 2 * u:2 * u + 2, gr * HG * DX:(gr + 1) * HG * DX]
                        v.tensor_tensor(out=dst.rearrange("p t (h d) -> p t h d", h=HG), in0=o[:, :, :, 0:DX],
                                        in1=d, op=ALU.mult).then_inc(*turned.empties(key))

                attn64(0)
                norm("a0", ("y", "a0"), None)
                xattn("self", s_bq, s_bk, s_bv, ys)
                xattn("cross", c_bq, c_bk, c_bv, yc)
                dve.wait_ge(*turned.emptied(it, ("cross", "ot", PAIR - 1, NG - 1)))
                dve.wait_ge(*turned.emptied(it, ("cross", "ot", PAIR - 1, NG - 2)))
                v.tensor_tensor(out=ys[:], in0=ys[:], in1=yc[:], op=ALU.add).then_inc(*s_dv.inc(("x0", "y")))
                norm("x0", ("y", "x0"), None)

                for t in range(TT):
                    key = ("f", "lg", t)
                    dve.wait_ge(*outs.filled(it, key))
                    v.tensor_tensor(out=lg[:, t, 0], in0=outs.bank(key)[:, 0:SLOTS], in1=f_b2[:], op=ALU.add)\
                        .then_inc(*outs.empties(key))
                    dve.wait_ge(*outs.emptied(it, key))
                    link(v.tensor_scalar(lg[:, t, 0], lg[:, t, 0], itau[:, 0:1], None, ALU.mult), ("f", "lg", t))
                    settle(dve)
                    link(v.max(top[:, t], lg[:, t, 0]), ("f", "top", t))
                    settle(dve)
                    v.match_replace(lg[:, t, 1], top[:, t], lg[:, t, 0], -FAR)
                    v.tensor_scalar(ntop[:, t:t + 1], top[:, t, 0:1], -1.0, None, ALU.mult)\
                        .then_inc(*s_dv.inc(("f", "struck", t)))
                for t in range(TT):
                    dve.wait_ge(*s_ac.at(it, ("f", "ex", t)))
                    link(v.tensor_tensor(out=alpha[:, t], in0=ex[:, t, 0], in1=ex[:, t, 1], op=ALU.subtract),
                         ("f", "a0", t))
                    link(v.tensor_reduce(asum[:, t:t + 1], alpha[:, t], AX.X, ALU.add), ("f", "asum", t))
                    link(v.reciprocal(arec[:, t:t + 1], asum[:, t:t + 1]), ("f", "arec", t))
                    v.tensor_scalar(alpha[:, t], alpha[:, t], arec[:, t:t + 1], None, ALU.mult)\
                        .then_inc(*s_dv.inc(("f", "alpha", t)))
                for u in range(PAIR):
                    key = ("f", "si", u)
                    dve.wait_ge(*outs.filled(it, key))
                    link(v.tensor_scalar(dn[:, u:u + 1], outs.bank(key)[0:SLOTS, D:D + 1], 1e-8, None, ALU.add),
                         ("f", "dn0", u))
                    link(v.reciprocal(dn[:, u:u + 1], dn[:, u:u + 1]), ("f", "dn1", u))
                    v.tensor_scalar(si[:, u], outs.bank(key)[0:SLOTS, 0:D], dn[:, u:u + 1], None, ALU.mult)\
                        .then_inc(*outs.empties(key))
                for u in range(PAIR):
                    key = ("f", "gi", u)
                    dve.wait_ge(*outs.filled(it, key))
                    v.tensor_tensor(out=gate[:, u], in0=outs.bank(key)[0:SLOTS, 0:3 * D], in1=crz[:], op=ALU.add)\
                        .then_inc(*outs.empties(key))
                dve.wait_ge(*s_ac.at(it, ("f", "ge")))
                link(v.tensor_scalar(rz[:], ge[:], 1.0, None, ALU.add), ("f", "rz0"))
                link(v.reciprocal(rz[:], rz[:]), ("f", "rz"))
                for u in range(PAIR):
                    ins = v.tensor_tensor(out=sn[:, u], in0=rz[:, u, 0:D], in1=ghn[:], op=ALU.mult)
                link(ins, ("f", "rg"))
                v.tensor_tensor(out=gate[:, :, 2 * D:3 * D], in0=gate[:, :, 2 * D:3 * D], in1=sn[:], op=ALU.add)\
                    .then_inc(*s_dv.inc(("f", "npre")))
                dve.wait_ge(*s_ac.at(it, ("f", "gn")))
                for u in range(PAIR):
                    ins = v.tensor_tensor(out=sn[:, u], in0=f_slots[:], in1=gn[:, u], op=ALU.subtract)
                link(ins, ("f", "sn0"))
                link(v.tensor_tensor(out=sn[:], in0=sn[:], in1=rz[:, :, D:2 * D], op=ALU.mult), ("f", "sn1"))
                v.tensor_tensor(out=sn[:], in0=sn[:], in1=gn[:], op=ALU.add).then_inc(*s_dv.inc(("f", "sn")))
                for n, dst, b in (("sq", sq, f_bq), ("sk", sk, f_bk)):
                    dve.wait_ge(*outs.filled(it, ("f", n)))
                    v.tensor_scalar(dst[:], outs.bank(("f", n))[0:DQ, 0:PAIR * SLOTS], b[:, 0:1], None, ALU.add)\
                        .then_inc(*outs.empties(("f", n)))
                dve.wait_ge(*outs.filled(it, ("f", "sv")))
                for u in range(PAIR):
                    ins = v.tensor_tensor(out=svv[:, u], in0=outs.bank(("f", "sv"))[0:SLOTS, u * D:(u + 1) * D],
                                          in1=f_bv[:], op=ALU.add)
                ins.then_inc(*outs.empties(("f", "sv")))
                dve.wait_ge(*misc.filled(it, ("f", "ss")))
                for u in range(PAIR):
                    link(v.tensor_reduce(sm[:, u, 0:1], misc.bank(("f", "ss"))[0:SLOTS, u * SLOTS:(u + 1) * SLOTS],
                                         AX.X, ALU.max, negate=True), ("f", "sm", u))
                for u in range(PAIR):
                    v.tensor_scalar(sm[:, u, 1:2], sm[:, u, 0:1], DQ ** -0.5, None, ALU.mult)\
                        .then_inc(*s_dv.inc(("f", "smax", u)))
                dve.wait_ge(*misc.emptied(it, ("f", "ss")))
                link(v.reciprocal(sm[:, :, 3], sm[:, :, 2]), ("f", "sr"))
                dve.wait_ge(*outs.filled(it, ("f", "comm")))
                for u in range(PAIR):
                    ins = v.scalar_tensor_tensor(out=sy[:, u], in0=outs.bank(("f", "comm"))[0:SLOTS, u * D:(u + 1) * D],
                                                 scalar=sm[:, u, 3:4], in1=sn[:, u], op0=ALU.mult, op1=ALU.add)
                ins.then_inc(*outs.empties(("f", "comm")))
                dve.wait_ge(*outs.emptied(it, ("f", "comm")))
                for u in range(PAIR):
                    ins = v.bn_stats(sst[:, u], sy[:, u])
                link(ins, ("f", "sst"))
                settle(dve)
                for u in range(PAIR):
                    ins = v.bn_aggr(smv[:, u], sst[:, u])
                link(ins, ("f", "smv"))
                v.tensor_scalar(srs[:, :, 0], smv[:, :, 1], EPS, None, ALU.add)\
                    .then_inc(*s_dv.inc((("ln", "slots"), "ve")))
                dve.wait_ge(*s_po.at(it, (("ln", "slots"), "rstd")))
                for u in range(PAIR):
                    ins = v.tensor_scalar(sy[:, u], sy[:, u], smv[:, u, 0:1], srs[:, u, 1:2], ALU.subtract, ALU.mult)
                link(ins, ("f", "y0"))
                for u in range(PAIR):
                    ins = v.tensor_tensor(out=sy[:, u], in0=sy[:, u], in1=f_lng[:], op=ALU.mult)
                link(ins, ("f", "y1"))
                for u in range(PAIR):
                    ins = v.tensor_tensor(out=sy[:, u], in0=sy[:, u], in1=f_lnb[:], op=ALU.add)
                ins.then_inc(*s_dv.inc(("f", "sy")))
                dve.wait_ge(*outs.filled(it, ("f", "svT")))
                v.tensor_scalar(svT[:], outs.bank(("f", "svT"))[:, 0:PAIR * SLOTS], f_bvp[:, 0:1], None, ALU.add)\
                    .then_inc(*outs.empties(("f", "svT")))
                dve.wait_ge(*outs.filled(it, ("f", "svo")))
                v.tensor_copy(svo[:].rearrange("p u d -> p (u d)"), outs.bank(("f", "svo"))[0:SLOTS, 0:PAIR * D])\
                    .then_inc(*outs.empties(("f", "svo")))
                norm("f0", ("y", "f0"), None)

                attn64(1)
                norm("a1", ("y", "a1"), None)
                xattn("last", None, None, None, ys)
                norm("x1", ("y", "x1"), None)

                for t in range(TT):
                    key = ("m", "rl", t)
                    dve.wait_ge(*outs.filled(it, key))
                    v.tensor_copy(rl[:, t, 0, 0:NE], outs.bank(key)[:, 0:NE]).then_inc(*outs.empties(key))
                    dve.wait_ge(*outs.emptied(it, key))
                    settle(dve)
                    link(v.max(rtop[:, t], rl[:, t, 0, 0:NE]), ("m", "top", t))
                    link(v.tensor_copy(rtwo[:, t, 0:TOP], rtop[:, t, 0:TOP]), ("m", "two", t))
                    settle(dve)
                    link(v.match_replace(rl[:, t, 1], rtwo[:, t], rl[:, t, 0], -FAR), ("m", "rep", t))
                    v.tensor_scalar(nrt[:, t:t + 1], rtop[:, t, 0:1], -1.0, None, ALU.mult)\
                        .then_inc(*s_dv.inc(("m", "struck", t)))
                    link(v.tensor_tensor(out=chosen[:, t], in0=rl[:, t, 0, 0:NE], in1=rl[:, t, 1, 0:NE], op=ALU.not_equal),
                         ("m", "chosen", t))
                    v.tensor_copy(chosenb[:, t], chosen[:, t])
                    v.tensor_copy(seenb[:, t], seen[:, t])
                    link(v.tensor_tensor(out=seen[:, t + 1], in0=seen[:, t], in1=chosen[:, t], op=ALU.add),
                         ("m", "seen", t))
                link(v.tensor_copy(seen[:, 0], seen[:, TT]), ("m", "carry"))
                for t in range(TT):
                    dve.wait_ge(*s_ac.at(it, ("m", "ex", t)))
                    link(v.tensor_reduce(rden[:, t:t + 1], rex[:, t, 0], AX.X, ALU.add), ("m", "den", t))
                    link(v.reciprocal(rrec[:, t:t + 1], rden[:, t:t + 1]), ("m", "rec", t))
                    link(v.tensor_tensor(out=wexp[:, t], in0=rex[:, t, 0], in1=rex[:, t, 1], op=ALU.subtract),
                         ("m", "we", t))
                    key = ("m", "pos", t)
                    dve.wait_ge(*outs.filled(it, key))
                    v.tensor_scalar(fits[:, t], outs.bank(key)[:, 0:NE], float(CAPACITY), None, ALU.is_lt)\
                        .then_inc(*outs.empties(key))
                    dve.wait_ge(*outs.emptied(it, key))
                    link(v.scalar_tensor_tensor(out=wgt[:, t], in0=wexp[:, t], scalar=rrec[:, t:t + 1],
                                                in1=fits[:, t], op0=ALU.mult, op1=ALU.mult), ("m", "w", t))
                for e in range(NE):
                    key = ("moe", "y", e)
                    dve.wait_ge(*misc.filled(it, key))
                    y = misc.bank(key).rearrange("p (t d) -> p t d", t=TT)
                    for t in range(TT):
                        if e == 0:
                            ins = v.tensor_scalar(acc[:, t], y[:, t], wgt[:, t, e:e + 1], None, ALU.mult)
                        else:
                            ins = v.scalar_tensor_tensor(out=acc[:, t], in0=y[:, t], scalar=wgt[:, t, e:e + 1],
                                                         in1=acc[:, t], op0=ALU.mult, op1=ALU.add)
                    ins.then_inc(*misc.empties(key))
                    dve.wait_ge(*misc.emptied(it, key))
                norm("moe", None, acc)

        @block.tensor
        def _(pe):
            t_ = nc.tensor
            for ring in (scores, turned, outs, misc):
                ring.open(pe)
            pe.wait_ge(*s_load.once("w"))
            pe.wait_ge(*s_const.once("c"))
            t_.matmul(misc.tensor[:, 0, 0:1], f_slots[:], ones[0:SLOTS, 0:1], start=True, stop=True)\
                .then_inc(*pre.inc("smean"))
            pe.wait_ge(*pred.once("smean"))
            t_.matmul(misc.tensor[0:SLOTS, 0, 8:9], f_w1[:, 1, :], smean[:], start=True, stop=True)
            t_.matmul(misc.tensor[0:SLOTS, 1, 0:3 * D], f_slotsT[:], f_whh[:], start=True, stop=True)\
                .then_inc(*pre.inc("c1"))
            pe.wait_ge(*pred.once("crz"))

            with pe.Fori(0, ITERS) as it:
                def one(ring, key, out_of, lhsT, rhs):
                    bank = ring.take(key)
                    pe.wait_ge(*ring.reusable(it, key))
                    if key[0] == "f":
                        settle(pe)
                    t_.matmul(out_of(bank), lhsT, rhs, start=True, stop=True).then_inc(*ring.fills(key))

                def masked(out, m):
                    t_.matmul(out, identb[:], m[:], start=False, stop=True, skip_group_check=True)

                def attn64(L, wq, wqs, wk, wks, wv, wo, name):
                    def project(c):
                        cols = slice(c * P, (c + 1) * P)
                        if L == 0:
                            for w, m in ((0, wq), (1, wk)):
                                one(misc, ("a0", w, c), lambda b: b, m[:, cols], xT[:])
                        else:
                            for w, ms in ((0, (wq, wqs)), (1, (wk, wks))):
                                for j in range(2):
                                    one(misc, ("a1", w, j, c), lambda b: b, ms[j][:, cols], xT[:])

                    def score(i):
                        c, u, r = order[i]
                        key = (L, "s", c, u, r)
                        s = scores.take(key)
                        pe.wait_ge(*scores.reusable(it, key))
                        if L == 0:
                            pe.wait_ge(*misc.emptied(it, ("a0", 1, c)))
                            pe.wait_ge(*misc.emptied(it, ("a0", 0, c)))
                        else:
                            pe.wait_ge(*s_po.at(it, ("qk1", c, 1)))
                        rows, q0 = slice(HD * r, HD * r + HD), u * SEQ
                        t_.matmul(s[:, 0:P], qT[rows, c, q0:q0 + P], kT[rows, c, q0:q0 + P],
                                  start=True, stop=False, skip_group_check=True)
                        t_.matmul(s[:, P:3 * P], qT[rows, c, q0 + P:q0 + 2 * P], kT[rows, c, q0:q0 + SEQ],
                                  start=False, stop=False, skip_group_check=True)
                        masked(s[:, 0:P], mask)
                        t_.matmul(s[:, 2 * P:3 * P], identb[:], mask[:], start=False, stop=True,
                                  skip_group_check=True).then_inc(*scores.fills(key))

                    def turn(i):
                        key = (L, "t", *order[i])
                        b = turned.take(key)
                        pe.wait_ge(*turned.reusable(it, key))
                        pe.wait_ge(*scores.emptied(it, (L, "s", *order[i])))
                        for j in range(3):
                            ins = t_.transpose(b[:, j * P:(j + 1) * P], probs[:, i % NPR, j * P:(j + 1) * P],
                                               ident[:])
                        ins.then_inc(*turned.fills(key))

                    def values(p):
                        c, u, _ = order[2 * p]
                        key = (L, "o", c, u)
                        b = outs.take(key)
                        pe.wait_ge(*outs.reusable(it, key))
                        for r in range(2):
                            pe.wait_ge(*turned.emptied(it, (L, "t", c, u, r)))
                        for kt, (lo, hi, at) in enumerate(((0, 2 * P, 0), (2 * P, 3 * P, P))):
                            for r in range(2):
                                h = 2 * c + r
                                ins = t_.matmul(b[HD * r:HD * r + HD, at:SEQ], vv[:, 2 * u + kt, h * HD:(h + 1) * HD],
                                                probsT[:, (2 * p + r) % 4, lo:hi], start=(kt == 0), stop=(kt == 1),
                                                skip_group_check=True)
                        ins.then_inc(*outs.fills(key))

                    for t in range(TT):
                        for hf in range(2):
                            one(misc, (L, "v", t, hf), lambda b: b, xT[:, t * P:(t + 1) * P],
                                wv[:, hf * 512:(hf + 1) * 512])
                    project(0)
                    n = len(order)
                    for i in range(n + 3):
                        if i < n:
                            if i % 4 == 0 and order[i][0] + 1 < NC:
                                project(order[i][0] + 1)
                            score(i)
                        if 2 <= i < n + 2:
                            turn(i - 2)
                        if i >= 4 and i % 2 == 0:
                            values((i - 4) // 2)
                    key = (L, "rT")
                    b = misc.take(key)
                    pe.wait_ge(*misc.reusable(it, key))
                    pe.wait_ge(*s_dv.at(it, (L, "rsum")))
                    for t in range(TT):
                        ins = t_.transpose(b[0:NH, t * P:(t + 1) * P], rsum[:, t], ident[:])
                    ins.then_inc(*misc.fills(key))
                    pe.wait_ge(*misc.emptied(it, key))
                    for c in range(NC):
                        one(misc, (L, "R", c), lambda b: b, head_rows[:, c, :], rT[:])
                    values_out(name, lambda: [(oT[:, c], wo[:, c], (L, "R", c)) for c in range(NC)])

                def values_out(name, terms):
                    key = ("y", name)
                    y = misc.take(key)
                    pe.wait_ge(*misc.reusable(it, key))
                    terms = terms()
                    for n, (lhs, rhs, ready) in enumerate(terms):
                        pe.wait_ge(*misc.emptied(it, ready))
                        for t in range(TT):
                            ins = t_.matmul(y[:, t * D:(t + 1) * D], lhs[:, t * P:(t + 1) * P], rhs,
                                            start=(n == 0 and t == 0), stop=(n == len(terms) - 1),
                                            skip_group_check=True)
                    ins.then_inc(*misc.fills(key))

                def to_xT(name):
                    key = ("xT", name)
                    b = misc.take(key)
                    pe.wait_ge(*misc.reusable(it, key))
                    pe.wait_ge(*s_dv.at(it, ("ln", name, "x")))
                    for t in range(TT):
                        ins = t_.transpose(b[:, t * P:(t + 1) * P], xa[:, t, 0:D], ident[:])
                    ins.then_inc(*misc.fills(key))
                    pe.wait_ge(*misc.emptied(it, key))

                def xattn(k, wq, wk, wv):
                    other = xT if k == "self" else ctxT
                    one(misc, (k, 0), lambda b: b, wq[:], xT[:])
                    one(misc, (k, 1), lambda b: b, wk[:], other[:])
                    key = (k, "v")
                    b = misc.take(key)
                    pe.wait_ge(*misc.reusable(it, key))
                    for t in range(TT):
                        ins = t_.matmul(b[:, t * D:(t + 1) * D], other[:, t * P:(t + 1) * P], wv[:],
                                        start=True, stop=True)
                    ins.then_inc(*misc.fills(key))
                    pe.wait_ge(*s_stack.at(it, (k, 1)))
                    for u, h in xorder:
                        key = (k, "s", u, h)
                        s = scores.take(key)
                        pe.wait_ge(*scores.reusable(it, key))
                        q0 = u * SEQ
                        qh, kh = qs[0:MROW, h], ks[0:MROW, h]
                        if k == "self":
                            t_.matmul(s[:, 0:P], qh[:, q0:q0 + P], kh[:, q0:q0 + P],
                                      start=True, stop=False, skip_group_check=True)
                            t_.matmul(s[:, P:3 * P], qh[:, q0 + P:q0 + SEQ], kh[:, q0:q0 + SEQ],
                                      start=False, stop=False, skip_group_check=True)
                            masked(s[:, 0:P], mask)
                            ins = t_.matmul(s[:, 2 * P:3 * P], identb[:], mask[:], start=False, stop=True,
                                            skip_group_check=True)
                        else:
                            for t in range(2):
                                ins = t_.matmul(s[:, t * SEQ:(t + 1) * SEQ], qh[:, q0 + t * P:q0 + (t + 1) * P],
                                                kh[:, q0:q0 + SEQ], start=True, stop=True)
                        ins.then_inc(*scores.fills(key))
                    key = (k, "nmT")
                    b = misc.take(key)
                    pe.wait_ge(*misc.reusable(it, key))
                    pe.wait_ge(*scores.emptied(it, (k, "s", *xorder[-1])))
                    for t in range(TT):
                        ins = t_.transpose(b[0:NH, t * P:(t + 1) * P], nm[:, t], ident[:])
                    ins.then_inc(*misc.fills(key))

                    def score(u, h):
                        key = (k, "st", u, h)
                        s = scores.take(key)
                        pe.wait_ge(*scores.reusable(it, key))
                        q0 = u * SEQ
                        if k == "self":
                            t_.matmul(s[:, 0:SEQ], ks[:, h, q0:q0 + P], qs[:, h, q0:q0 + SEQ],
                                      start=True, stop=False, skip_group_check=True)
                            t_.matmul(s[:, SEQ:3 * P], ks[:, h, q0 + P:q0 + SEQ], qs[:, h, q0 + P:q0 + SEQ],
                                      start=False, stop=False, skip_group_check=True)
                            masked(s[:, 0:P], maskT)
                            ins = t_.matmul(s[:, SEQ:3 * P], identb[:], maskT[:], start=False, stop=True,
                                            skip_group_check=True)
                        else:
                            for t in range(2):
                                ins = t_.matmul(s[:, t * SEQ:(t + 1) * SEQ], ks[:, h, q0 + t * P:q0 + (t + 1) * P],
                                                qs[:, h, q0:q0 + SEQ], start=True, stop=True)
                        ins.then_inc(*scores.fills(key))

                    def values(n):
                        u, gr = n // NG, n % NG
                        key = (k, "o", u, gr)
                        b = outs.take(key)
                        pe.wait_ge(*outs.reusable(it, key))
                        pe.wait_ge(*scores.emptied(it, (k, "st", u, HG * gr + HG - 1)))
                        for kt in range(2):
                            lo, hi, at = ((0, SEQ, 0), (SEQ, 3 * P, P) if k == "self" else (SEQ, 2 * SEQ, 0))[kt]
                            for j in range(HG):
                                h = HG * gr + j
                                ins = t_.matmul(b[32 * j:32 * j + 32, at:SEQ], va[:, 2 * u + kt, h * VW:h * VW + 32],
                                                px[:, (HG * n + j) % NPX, lo:hi], start=(kt == 0), stop=(kt == 1),
                                                skip_group_check=True)
                        ins.then_inc(*outs.fills(key))

                    def turn(n):
                        u, gr = n // NG, n % NG
                        key = (k, "ot", u, gr)
                        b = turned.take(key)
                        pe.wait_ge(*turned.reusable(it, key))
                        pe.wait_ge(*outs.emptied(it, (k, "o", u, gr)))
                        for t in range(2):
                            ins = t_.transpose(b[:, t * P:(t + 1) * P], og[:, n % 2, t * P:(t + 1) * P], ident[:])
                        ins.then_inc(*turned.fills(key))

                    pe.wait_ge(*s_mrow.at(it, k))
                    last = len(xorder) // HG - 1
                    for i, (u, h) in enumerate(xorder):
                        score(u, h)
                        if i >= 5 and (i - 5) % HG == 0:
                            values((i - 5) // HG)
                        if i >= 7 and (i - 7) % HG == 0:
                            turn((i - 7) // HG)
                    values(last)
                    turn(last)

                def from_y(k, name, weight):
                    key = (name, "yT")
                    b = misc.take(key)
                    pe.wait_ge(*misc.reusable(it, key))
                    if name == "x0":
                        pe.wait_ge(*s_dv.at(it, ("x0", "y")))
                    else:
                        pe.wait_ge(*turned.emptied(it, (k, "ot", PAIR - 1, NG - 1)))
                    for t in range(TT):
                        ins = t_.transpose(b[:, t * P:(t + 1) * P], ys[:, t], ident[:])
                    ins.then_inc(*misc.fills(key))
                    values_out(name, lambda: [(yT, weight[:], (name, "yT"))])

                pe.wait_ge(*s_in.at(it, "x"))
                attn64(0, a0_wq, None, a0_wk, None, a0_wv, a0_wo, "a0")
                to_xT("a0")
                xattn("self", s_wq, s_wk, s_wv)
                xattn("cross", c_wq, c_wk, c_wv)
                from_y("cross", "x0", p_w)
                to_xT("x0")

                def pair_transposes(key, src, n, ready):
                    b = misc.take(key)
                    pe.wait_ge(*misc.reusable(it, key))
                    pe.wait_ge(*ready)
                    settle(pe)
                    for u in range(PAIR):
                        m = src.shape[2]
                        ins = t_.transpose(b[0:m, u * SLOTS:(u + 1) * SLOTS], src[:, u], ident[0:n, 0:n])
                    ins.then_inc(*misc.fills(key))
                    pe.wait_ge(*misc.emptied(it, key))

                one(misc, ("f", "h"), lambda b: b[0:SLOTS], f_w1[:, 0, :], xT[:])
                pe.wait_ge(*misc.emptied(it, ("f", "h")))
                for t in range(TT):
                    one(outs, ("f", "lg", t), lambda b: b[:, 0:SLOTS], hT[:, t * P:(t + 1) * P], f_w2[:])
                key = ("f", "aT")
                b = misc.take(key)
                pe.wait_ge(*misc.reusable(it, key))
                pe.wait_ge(*s_dv.at(it, ("f", "alpha", TT - 1)))
                settle(pe)
                for t in range(TT):
                    ins = t_.transpose(b[0:SLOTS, t * P:(t + 1) * P], alpha[:, t], ident[:])
                ins.then_inc(*misc.fills(key))
                for u in range(PAIR):
                    key = ("f", "si", u)
                    b = outs.take(key)
                    pe.wait_ge(*outs.reusable(it, key))
                    for t in range(2):
                        ins = t_.matmul(b[0:SLOTS, 0:D + 1], alpha[:, 2 * u + t], xa[:, 2 * u + t, :],
                                        start=(t == 0), stop=(t == 1))
                    ins.then_inc(*outs.fills(key))
                pair_transposes(("f", "siT"), si, SLOTS, outs.emptied(it, ("f", "si", PAIR - 1)))
                for u in range(PAIR):
                    one(outs, ("f", "gi", u), lambda b: b[0:SLOTS, 0:3 * D], siT[:, u * SLOTS:(u + 1) * SLOTS],
                        f_wih[:])
                pair_transposes(("f", "snT"), sn, SLOTS, s_dv.at(it, ("f", "sn")))
                one(outs, ("f", "sq"), lambda b: b[0:DQ, 0:PAIR * SLOTS], f_wq[:], snT[:])
                one(outs, ("f", "sk"), lambda b: b[0:DQ, 0:PAIR * SLOTS], f_wk[:], snT[:])

                def by_pair(ring, key, rows, width, lhs, rhs, ready=None):
                    b = ring.take(key)
                    pe.wait_ge(*ring.reusable(it, key))
                    if ready is not None:
                        pe.wait_ge(*ready)
                    settle(pe)
                    for u in range(PAIR):
                        ins = t_.matmul(b[0:rows, u * width:(u + 1) * width], lhs[:, u * SLOTS:(u + 1) * SLOTS],
                                        rhs(u), start=True, stop=True)
                    ins.then_inc(*ring.fills(key))

                by_pair(outs, ("f", "sv"), SLOTS, D, snT, lambda u: f_wv[:])
                by_pair(misc, ("f", "ss"), SLOTS, SLOTS, sq, lambda u: sk[:, u * SLOTS:(u + 1) * SLOTS],
                        outs.emptied(it, ("f", "sk")))
                pair_transposes(("f", "spT"), sp_, SLOTS, misc.emptied(it, ("f", "ss")))
                by_pair(outs, ("f", "comm"), SLOTS, D, spT, lambda u: svv[:, u])
                pair_transposes(("f", "syT"), sy, SLOTS, s_dv.at(it, ("f", "sy")))
                one(outs, ("f", "svT"), lambda b: b[:, 0:PAIR * SLOTS], f_wvp[:], syT[:])
                by_pair(outs, ("f", "svo"), SLOTS, D, svT, lambda u: f_wo[:])
                key = ("y", "f0")
                y = misc.take(key)
                pe.wait_ge(*misc.reusable(it, key))
                pe.wait_ge(*outs.emptied(it, ("f", "svo")))
                pe.wait_ge(*misc.emptied(it, ("f", "aT")))
                for t in range(TT):
                    ins = t_.matmul(y[:, t * D:(t + 1) * D], alphaT[:, t * P:(t + 1) * P], svo[:, t // 2, :],
                                    start=True, stop=True)
                ins.then_inc(*misc.fills(key))
                to_xT("f0")

                attn64(1, a1_wq, a1_wqs, a1_wk, a1_wks, a1_wv, a1_wo, "a1")
                to_xT("a1")
                xattn("last", z_wq, z_wk, z_wv)
                from_y("last", "x1", z_wo)
                to_xT("x1")

                for t in range(TT):
                    one(outs, ("m", "rl", t), lambda b: b[:, 0:NE], xT[:, t * P:(t + 1) * P], m_wr[:])

                def places_in_experts():
                    for t in range(TT):
                        key = ("m", "pos", t)
                        b = outs.take(key)
                        pe.wait_ge(*outs.reusable(it, key))
                        pe.wait_ge(*s_dv.at(it, ("m", "seen", t)))
                        t_.matmul(b[:, 0:NE], earlier[:], chosenb[:, t], start=True, stop=False)
                        t_.matmul(b[:, 0:NE], onesb[:], seenb[:, t], start=False, stop=True)\
                            .then_inc(*outs.fills(key))

                def expert_out(e):
                    key = ("moe", "y", e)
                    y = misc.take(key)
                    pe.wait_ge(*misc.reusable(it, key))
                    pe.wait_ge(*scores.emptied(it, ("moe", "h", e, FC - 1)))
                    for t in range(TT):
                        for f in range(FC):
                            ins = t_.matmul(y[:, t * D:(t + 1) * D], hid[:, e % 2, f, t * P:(t + 1) * P],
                                            w2e[:, e % 2, f], start=(f == 0), stop=(f == FC - 1))
                    ins.then_inc(*misc.fills(key))

                for e in range(NE):
                    pe.wait_ge(*s_wexp[e % 2].at(it, e))
                    for f in range(FC):
                        one(scores, ("moe", "h", e, f), lambda b: b, w1e[:, e % 2, f * P:(f + 1) * P], xT[:])
                    if e == 1:
                        places_in_experts()
                    if e >= 1:
                        expert_out(e - 1)
                expert_out(NE - 1)

        for c in closing:
            c.close()


def rotary_tables():
    inv = (np.float32(1.0) / np.float32(10000.0) ** (np.float32(2.0) * np.arange(HD // 2, dtype=np.float32)
                                                     / np.float32(HD))).astype(np.float32)
    ang = (inv[:, None] * np.arange(SEQ, dtype=np.float32)[None]).astype(np.float32)
    cos, sin = np.cos(ang).astype(np.float32), np.sin(ang).astype(np.float32)
    c = np.concatenate([cos, cos, cos, cos])
    s = np.concatenate([-sin, sin, -sin, sin])
    k = np.float32(HD ** -0.5)
    return np.stack([c * k, s * k, c, s])


def lay_out(i):
    at = np.arange(E).reshape(NH, HD // 2, 2)
    even_odd = np.concatenate([at[:, :, 0], at[:, :, 1]], 1).reshape(-1)
    odd_even = np.concatenate([at[:, :, 1], at[:, :, 0]], 1).reshape(-1)
    col = lambda a: a.reshape(-1, 1)
    row = lambda a: a.reshape(1, -1)
    chunks = lambda a, order: a[order].reshape(NC, P).T
    return {
        "x": i["x"], "xT": i["x"].transpose(0, 2, 1), "ctxT": i["ctx_512"].transpose(0, 2, 1),
        "a0_wq": i["L0_attn_wq"].T, "a0_wk": i["L0_attn_wk"].T, "a0_wv": i["L0_attn_wv"].T,
        "a0_wo": i["L0_attn_wo"].T,
        "a1_wq": i["L1_attn_Wq"][:, even_odd], "a1_wqs": i["L1_attn_Wq"][:, odd_even],
        "a1_wk": i["L1_attn_Wk"][:, even_odd], "a1_wks": i["L1_attn_Wk"][:, odd_even],
        "a1_wv": i["L1_attn_Wv"], "a1_wo": i["L1_attn_Wo"],
        "a1_bq": chunks(i["L1_attn_bq"], even_odd), "a1_bqs": chunks(i["L1_attn_bq"], odd_even),
        "a1_bk": chunks(i["L1_attn_bk"], even_odd), "a1_bks": chunks(i["L1_attn_bk"], odd_even),
        "a1_bv": row(i["L1_attn_bv"]), "a1_bo": row(i["L1_attn_bo"]), "rope": rotary_tables(),
        "s_wq": i["L0_xattn_Wq"], "s_wk": i["L0_xattn_Wk"], "s_wv": i["L0_xattn_Wv"],
        "s_bq": col(i["L0_xattn_bq"]), "s_bk": col(i["L0_xattn_bk"]), "s_bv": row(i["L0_xattn_bv"]),
        "c_wq": i["L0_xattn_Wcq"], "c_wk": i["L0_xattn_Wck"], "c_wv": i["L0_xattn_Wcv"],
        "c_bq": col(i["L0_xattn_bcq"]), "c_bk": col(i["L0_xattn_bck"]), "c_bv": row(i["L0_xattn_bcv"]),
        "p_w": i["L0_xattn_Wp"], "p_b": row(i["L0_xattn_bp"]),
        "z_wq": i["L1_xattn_Wq"].T, "z_wk": i["L1_xattn_Wkv"][:D].T, "z_wv": i["L1_xattn_Wkv"][D:].T,
        "z_wo": i["L1_xattn_Wo"].T,
        "f_slots": i["L0_ffn_slot_init"], "f_slotsT": i["L0_ffn_slot_init"].T, "f_w1": i["L0_ffn_w1"],
        "f_b1": col(i["L0_ffn_b1"]), "f_w2": i["L0_ffn_w2"], "f_b2": row(i["L0_ffn_b2"]),
        "f_tau": row(i["L0_ffn_tau"]), "f_wihT": i["L0_ffn_Wih"].T, "f_whhT": i["L0_ffn_Whh"].T,
        "f_bih": row(i["L0_ffn_bih"]), "f_bhh": row(i["L0_ffn_bhh"]),
        "f_wq": i["L0_ffn_wq"], "f_bq": col(i["L0_ffn_bq"]), "f_wk": i["L0_ffn_wk"], "f_bk": col(i["L0_ffn_bk"]),
        "f_wv": i["L0_ffn_wv"], "f_bv": row(i["L0_ffn_bv"]), "f_lng": row(i["L0_ffn_ln_g"]),
        "f_lnb": row(i["L0_ffn_ln_b"]), "f_wvp": i["L0_ffn_wvp"], "f_bvp": col(i["L0_ffn_bvp"]),
        "f_wo": i["L0_ffn_wo"], "f_bo": row(i["L0_ffn_bo"]),
        "m_wr": i["L1_ffn_w_router"], "m_w1": i["L1_ffn_w1"], "m_w2": i["L1_ffn_w2"],
        "m_b": i["L1_ffn_bias"].reshape(1, D),
    }


def program(make_core, places):
    nc = make_core()
    dram = {n: nc.dram_tensor(f"in_{n}", s, F32, kind="ExternalInput").ap() for n, s in INPUTS.items()}
    out = nc.dram_tensor("out_0", (BATCH, SEQ, D), F32, kind="ExternalOutput").ap()
    build(nc, dram, out, places)
    return nc


def kernel(**inputs):
    import concourse.bacc as bacc
    from concourse.bass_utils import run_bass_kernel_spmd

    def make_core():
        return bacc.Bacc("TRN2", target_bir_lowering=False, num_devices=1)

    laid = lay_out({n: np.asarray(a) for n, a in inputs.items()})
    arrays = {f"in_{n}": np.ascontiguousarray(a) for n, a in laid.items()}
    places = {}
    program(make_core, places)
    nc = program(make_core, places)
    r = run_bass_kernel_spmd(nc, [arrays], core_ids=[0])
    return r.results[0]["out_0"]
```

```python
from contextlib import ExitStack

import numpy as np

import concourse.bass as bass
from concourse import mybir

F32 = mybir.dt.float32
BF16 = mybir.dt.bfloat16
ALU = mybir.AluOpType
ACT = mybir.ActivationFunctionType
AX = mybir.AxisListType

P = 128
BATCH, SEQ, D = 8, 256, 128
CTX = 64
PAIR = 2
ITERS = BATCH // PAIR
TOK = PAIR * SEQ
TT = TOK // P
NH = 16
HD = 64
E = NH * HD
NC = E // P
DX = D // NH
NG = 4
HG = NH // NG
VW = DX + 1
XATT = ("self", "cross", "last")
PARTS = 3
STACK = PARTS * PARTS * DX
MROW = STACK
ONES = MROW // 32 * 32
SLOTS, DQ, TOPK = 64, 32, 8
NE, FF, TOP = 8, 512, 2
FC = FF // P
CAPACITY = TOP * BATCH * SEQ // NE
EPS = 1e-5
MASKED = -1e30
FAR = 3e38


class Signal:

    def __init__(self, sem, places, step):
        self.sem, self.places, self.step, self.count, self.base = sem, places, step, 0, 0

    def open(self):
        self.base = 1
        return self.sem, 1

    def inc(self, key):
        self.count += 1
        self.places[key] = self.count
        return self.sem, self.step

    def at(self, it, key):
        return self.sem, (it * self.places.get("all", 1) + self.places.get(key, 1)) * self.step + self.base

    def once(self, key):
        return self.sem, self.places.get(key, 1) * self.step

    def before(self, it):
        return self.sem, it * self.places.get("all", 1) * self.step + self.base

    def close(self):
        self.places["all"] = self.count


class Ring:

    def __init__(self, tensor, full, free, places):
        self.tensor, self.full, self.free, self.places = tensor, full, free, places
        self.count = 0

    def open(self, eng):
        for sem in self.free:
            eng.sem_inc(sem, 1)

    def take(self, key):
        n, banks = self.count, len(self.full)
        self.places[key] = n
        self.count += 1
        return self.tensor[:, n % banks, :]

    def bank(self, key):
        return self.tensor[:, self.places.get(key, 0) % len(self.full), :]

    def _at(self, it, key, more):
        banks = len(self.full)
        n = self.places.get(key, 0)
        total = self.places.get("all", banks)
        each = total // banks + (n % banks < total % banks)
        return n % banks, it * each + n // banks + more

    def reusable(self, it, key):
        b, v = self._at(it, key, 1)
        return self.free[b], v

    def filled(self, it, key):
        b, v = self._at(it, key, 1)
        return self.full[b], v

    def emptied(self, it, key):
        b, v = self._at(it, key, 2)
        return self.free[b], v

    def fills(self, key):
        return self.full[self.places[key] % len(self.full)], 1

    def empties(self, key):
        return self.free[self.places.get(key, 0) % len(self.full)], 1

    def close(self):
        self.places["all"] = self.count


INPUTS = dict(
    x=(BATCH, SEQ, D), xT=(BATCH, D, SEQ), ctxT=(BATCH, CTX, SEQ),
    a0_wq=(D, E), a0_wk=(D, E), a0_wv=(D, E), a0_wo=(E, D),
    a1_wq=(D, E), a1_wqs=(D, E), a1_wk=(D, E), a1_wks=(D, E), a1_wv=(D, E), a1_wo=(E, D),
    a1_bq=(P, NC), a1_bqs=(P, NC), a1_bk=(P, NC), a1_bks=(P, NC), a1_bv=(1, E), a1_bo=(1, D),
    rope=(4, P, SEQ),
    s_wq=(D, D), s_wk=(D, D), s_wv=(D, D), s_bq=(D, 1), s_bk=(D, 1), s_bv=(1, D),
    c_wq=(D, D), c_wk=(CTX, D), c_wv=(CTX, D), c_bq=(D, 1), c_bk=(D, 1), c_bv=(1, D),
    p_w=(D, D), p_b=(1, D),
    z_wq=(D, D), z_wk=(CTX, D), z_wv=(CTX, D), z_wo=(D, D),
    f_slots=(SLOTS, D), f_slotsT=(D, SLOTS), f_w1=(2 * D, SLOTS), f_b1=(SLOTS, 1),
    f_w2=(SLOTS, SLOTS), f_b2=(1, SLOTS), f_tau=(1, 1),
    f_wihT=(D, 3 * D), f_whhT=(D, 3 * D), f_bih=(1, 3 * D), f_bhh=(1, 3 * D),
    f_wq=(D, DQ), f_bq=(DQ, 1), f_wk=(D, DQ), f_bk=(DQ, 1), f_wv=(D, D), f_bv=(1, D),
    f_lng=(1, D), f_lnb=(1, D), f_wvp=(D, D), f_bvp=(D, 1), f_wo=(D, D), f_bo=(1, D),
    m_wr=(D, NE), m_w1=(NE, D, FF), m_w2=(NE, FF, D), m_b=(1, D),
)


def build(nc, dram, out, places):
    with ExitStack() as ctx:
        def sb(name, shape, dt=F32):
            return ctx.enter_context(nc.sbuf_tensor(name, shape, dt))

        def psum(name, banks):
            tensor = ctx.enter_context(nc.psum_tensor(name, [P, banks, 512], F32))
            full = [ctx.enter_context(nc.semaphore(f"{name}_full{b}")) for b in range(banks)]
            free = [ctx.enter_context(nc.semaphore(f"{name}_free{b}")) for b in range(banks)]
            ring = Ring(tensor, full, free, places.setdefault(name, {}))
            closing.append(ring)
            return ring

        def signal(name, step=1):
            s = Signal(ctx.enter_context(nc.semaphore(name)), places.setdefault(name, {}), step)
            closing.append(s)
            return s

        closing = []

        loads = []

        def weight(name, shape=None, source=None):
            t = sb("w_" + name, list(shape or dram[name].shape))
            loads.append((t[:], dram[name] if source is None else source))
            return t

        def across(name, parts=P):
            n = dram[name].shape[1]
            t = sb("w_" + name, [parts, n])
            loads.append((t[:], dram[name].to_broadcast([parts, n])))
            return t

        def chunked(name, n):
            return weight(name, [P, n, D], dram[name].rearrange("(c p) h -> p c h", p=P))

        a0_wq, a0_wk, a0_wv = weight("a0_wq"), weight("a0_wk"), weight("a0_wv")
        a0_wo = chunked("a0_wo", NC)
        s_wq, s_wk, s_wv, s_bq, s_bk, s_bv = (weight("s_wq"), weight("s_wk"), weight("s_wv"),
                                              weight("s_bq"), weight("s_bk"), across("s_bv"))
        c_wq, c_wk, c_wv, c_bq, c_bk, c_bv = (weight("c_wq"), weight("c_wk"), weight("c_wv"),
                                              weight("c_bq"), weight("c_bk"), across("c_bv"))
        p_w, p_b = weight("p_w"), across("p_b")
        f_slots, f_slotsT = weight("f_slots"), weight("f_slotsT")
        f_w1 = weight("f_w1", [P, 2, SLOTS], dram["f_w1"].rearrange("(c p) h -> p c h", p=P))
        f_b1, f_b2, f_w2, f_tau = weight("f_b1"), across("f_b2"), weight("f_w2"), across("f_tau")
        f_wih, f_whh = weight("f_wihT"), weight("f_whhT")
        f_bih, f_bhh = across("f_bih", SLOTS), across("f_bhh", SLOTS)
        f_wq, f_bq, f_wk, f_bk = weight("f_wq"), weight("f_bq"), weight("f_wk"), weight("f_bk")
        f_wv, f_bv = weight("f_wv"), across("f_bv", SLOTS)
        f_lng, f_lnb = across("f_lng", SLOTS), across("f_lnb", SLOTS)
        f_wvp, f_bvp, f_wo, f_bo = weight("f_wvp"), weight("f_bvp"), weight("f_wo"), across("f_bo")
        a1_wq, a1_wqs, a1_wk, a1_wks = (weight("a1_wq"), weight("a1_wqs"), weight("a1_wk"),
                                        weight("a1_wks"))
        a1_wv, a1_wo = weight("a1_wv"), chunked("a1_wo", NC)
        a1_bq, a1_bqs, a1_bk, a1_bks = (weight("a1_bq"), weight("a1_bqs"), weight("a1_bk"),
                                        weight("a1_bks"))
        a1_bv, a1_bo = across("a1_bv"), across("a1_bo")
        rope = weight("rope", [P, 4, SEQ], dram["rope"].rearrange("a p n -> p a n"))
        z_wq, z_wk, z_wv, z_wo = weight("z_wq"), weight("z_wk"), weight("z_wv"), weight("z_wo")
        m_wr, m_b = weight("m_wr"), across("m_b")

        ident = sb("ident", [P, P])
        identb = sb("identb", [P, P], BF16)
        ones = sb("ones", [P, P])
        onesb = sb("onesb", [P, P], BF16)
        mask = sb("mask", [P, P], BF16)
        maskT = sb("maskT", [P, P], BF16)
        earlier = sb("earlier", [P, P], BF16)
        head_rows = sb("head_rows", [PARTS * 32, NC, P], BF16)

        xa = sb("xa", [P, TT, D + 1])
        xb = sb("xb", [P, TT, D])
        xT = sb("xT", [P, TOK])
        ctxT = sb("ctxT", [CTX, TOK])
        stats = sb("stats", [P, TT, 6])
        mv = sb("mv", [P, TT, 2])
        ve = sb("ve", [P, TT])
        rstd = sb("rstd", [P, TT])
        half = sb("half", [P, TT])

        qT = sb("qT", [P, NC, TOK])
        kT = sb("kT", [P, NC, TOK])
        vv = sb("vv", [P, TT, E])
        oT = sb("oT", [P, NC, TOK])
        NPR = 3
        probs = sb("probs", [P, NPR, 3 * P])
        probsT = sb("probsT", [P, 4, 3 * P])
        nmax = sb("nmax", [P, 4, 2])
        sums = sb("sums", [P, TT, NH])
        rsum = sb("rsum", [P, TT, NH])
        rrest = sb("rrest", [P, TT, NH])
        rparts = sb("rparts", [P, TT, PARTS, 32], BF16)
        rot = sb("rot", [P, 2, 2, TOK])

        def over(host, rows, shape, dt=F32, phase="small heads"):
            n = int(np.prod(shape)) // (2 if dt == BF16 else 1)
            at = taken.setdefault((host.name, phase), 0)
            taken[host.name, phase] = at + n
            flat_host = host[:].rearrange("p a b -> p (a b)" if len(host.shape) == 3 else "p a b c -> p (a b c)")
            assert at + n <= flat_host.shape[1]
            v = flat_host[0:rows, at:at + n]
            v = v.bitcast(BF16) if dt == BF16 else v
            if len(shape) == 1:
                return v
            names = "abc"[:len(shape)]
            return v.rearrange(f"p ({' '.join(names)}) -> p {' '.join(names)}",
                               **dict(zip(names[1:], shape[1:])))

        taken = {}
        xr = over(vv, P, [TT, D], phase="norm")
        rT = over(qT, PARTS * 32, [TOK], BF16, phase="row sums")

        rows16 = lambda host: host[:].rearrange("p a b -> p (a b)").bitcast(BF16)\
            .rearrange("p (h n) -> p h n", h=NH)
        qs_ = sb("qs", [P, NH, TOK], BF16)
        ks_ = sb("ks", [P, NH, TOK], BF16)
        stacks = {"self": (qs_[:], ks_[:]), "cross": (rows16(kT), rows16(oT)), "last": (qs_[:], ks_[:])}
        hosts = {("self", 0): (vv, "parts"), ("self", 1): (vv, "parts"),
                 ("cross", 0): (qT, "parts"), ("cross", 1): (qT, "parts"),
                 ("last", 0): (vv, "last parts"), ("last", 1): (qT, "last parts")}
        flat = {kw: over(host, P, [TOK], phase=ph) for kw, (host, ph) in hosts.items()}
        rest = {kw: over(host, P, [TOK], phase=ph) for kw, (host, ph) in hosts.items()}
        part = {kw: over(host, P, [PARTS, TOK], BF16, phase=ph) for kw, (host, ph) in hosts.items()}
        VA = NH * VW + 32 - VW
        vas = [sb(f"va{i}", [P, TT, VA]) for i in range(2)]
        nms = [sb(f"nm{i}", [P, TT, NH]) for i in range(2)]
        va = {"self": vas[0], "cross": vas[1], "last": vas[0]}
        nm = {"self": nms[0], "cross": nms[1], "last": nms[0]}
        nmf = over(rot, NH, [SEQ], phase="small heads")
        nmr = over(rot, NH, [SEQ], phase="small heads")
        nmp = over(rot, NH, [PARTS, SEQ], BF16, phase="small heads")
        NPX = 8
        px = vv[:].rearrange("p a b -> p (a b)").rearrange("p (s n) -> p s n", s=NPX)
        og = over(rot, P, [2, SEQ], phase="small heads")
        den = sb("den", [P, NG, TT, HG])
        ys = over(rot, P, [TT, D], phase="small heads")
        yc = over(qT, P, [TT, D], phase="parts")
        yT = over(qT, P, [TOK], phase="yT")

        c1 = sb("c1", [SLOTS, 1])
        smean = sb("smean", [P, 1])
        itau = sb("itau", [P, 1])
        crz = sb("crz", [SLOTS, 3 * D])
        ghn = sb("ghn", [SLOTS, D])
        hT = over(oT, SLOTS, [TOK])
        lg = over(oT, P, [TT, 2, SLOTS])
        top = sb("top", [P, TT, 8])
        ntop = sb("ntop", [P, TT])
        ex = over(oT, P, [TT, 2, SLOTS])
        alpha = over(kT, P, [TT, SLOTS], phase="slots")
        asum = sb("asum", [P, TT])
        arec = sb("arec", [P, TT])
        alphaT = over(oT, SLOTS, [TOK])
        dn = sb("dn", [SLOTS, PAIR])
        si = over(kT, SLOTS, [PAIR, D], phase="slots")
        siT = over(kT, P, [PAIR * SLOTS], phase="slots")
        gate = over(oT, SLOTS, [PAIR, 3 * D])
        ge = over(oT, SLOTS, [PAIR, 2 * D])
        rz = over(oT, SLOTS, [PAIR, 2 * D])
        gn = over(oT, SLOTS, [PAIR, D])
        sn = over(kT, SLOTS, [PAIR, D], phase="slots")
        snT = over(kT, P, [PAIR * SLOTS], phase="slots")
        sq = sb("sq", [DQ, PAIR * SLOTS])
        sk = sb("sk", [DQ, PAIR * SLOTS])
        svv = over(kT, SLOTS, [PAIR, D], phase="slots")
        sm = sb("sm", [SLOTS, PAIR, 4])
        sp_ = over(kT, SLOTS, [PAIR, SLOTS], phase="slots")
        spT = over(kT, SLOTS, [PAIR * SLOTS], phase="slots")
        sy = over(kT, SLOTS, [PAIR, D], phase="slots")
        sst = sb("sst", [SLOTS, PAIR, 6])
        smv = sb("smv", [SLOTS, PAIR, 2])
        srs = sb("srs", [SLOTS, PAIR, 2])
        syT = over(kT, P, [PAIR * SLOTS], phase="slots")
        svT = over(kT, P, [PAIR * SLOTS], phase="slots")
        svo = over(kT, SLOTS, [PAIR, D], phase="slots")

        hid = oT[:].rearrange("p c n -> p (c n)").rearrange("p (s f n) -> p s f n", s=2, f=FC)
        w1e = rot[:, 0].rearrange("p a n -> p (a n)").rearrange("p (s n) -> p s n", s=2)
        w2e = rot[:, 1].rearrange("p a n -> p (a n)").rearrange("p (s f n) -> p s f n", s=2, f=FC)
        RW = NE + 8 - TOP
        rl = sb("rl", [P, TT, 2, RW])
        rtop = sb("rtop", [P, TT, 8])
        rtwo = sb("rtwo", [P, TT, 8])
        nrt = sb("nrt", [P, TT])
        rex = sb("rex", [P, TT, 2, NE])
        rden = sb("rden", [P, TT])
        rrec = sb("rrec", [P, TT])
        chosen = sb("chosen", [P, TT, NE])
        chosenb = sb("chosenb", [P, TT, NE], BF16)
        seen = sb("seen", [P, TT + 1, NE])
        seenb = sb("seenb", [P, TT, NE], BF16)
        fits = sb("fits", [P, TT, NE])
        wexp = sb("wexp", [P, TT, NE])
        wgt = sb("wgt", [P, TT, NE])
        acc = over(kT, P, [TT, D], phase="experts")

        scores = psum("scores", 3)
        turned = psum("turned", 2)
        outs = psum("outs", 1)
        misc = psum("misc", 2)

        s_load = signal("weights_loaded", 16)
        s_const = signal("constants_made")
        s_fill = signal("fills_made")
        s_in = signal("x_loaded", 16)
        s_out = signal("y_stored", 16)
        s_split = {(k, w): signal(f"parts_stored_{k}{w}", 16) for k in XATT for w in range(2)}
        s_stack = {k: signal(f"parts_stacked_{k}", 16) for k in XATT}
        s_mrow = {(k, u): signal(f"maxima_placed_{k}{u}", 16) for k in XATT for u in range(PAIR)}
        s_w1e = [signal(f"expert_w1_loaded{b}", 16) for b in range(2)]
        s_w2e = [signal(f"expert_w2_loaded{b}", 16) for b in range(2)]
        s_dv = signal("vector_made")
        s_ac = signal("scalar_made")
        s_po = signal("pool_made")
        pre = signal("slot_terms_summed")
        pred = signal("slot_terms_made")
        passed = ctx.enter_context(nc.semaphore("passed"))
        parts_d = [[nc.dram_tensor(f"parts{a}{b}", (PARTS,) * (b + 1) + (P, TOK), BF16, kind="Internal").ap()
                    for b in range(2)] for a in range(3)]

        block = ctx.enter_context(nc.Block())
        def settle(eng):
            eng.sem_inc(passed, 1)

        SCALE = {"self": DX ** -0.5, "cross": DX ** -0.5, "last": DX ** -0.5}

        def units():
            for c in range(NC):
                for u in range(PAIR):
                    for r in range(2):
                        yield c, u, r

        order = list(units())

        def small_heads(ks, side_by_side):
            first = [(k, u, h) for k in ks for u in range(PAIR) for h in range(NH)]
            second = list(first)
            steps, done = [], 0

            def one_second():
                nonlocal done
                k, u, h = second[done]
                steps.append(("p2", k, u, h, done))
                for what, lag in (("av", 5), ("og", 6), ("ot", 7)):
                    if done >= lag and (done - lag) % HG == 0:
                        steps.append(group(what, (done - lag) // HG))
                done += 1

            def group(what, n):
                k, u, h = second[n * HG]
                return what, k, u, h // HG, n

            lead = PAIR * NH if side_by_side else len(first)
            for i, (k, u, h) in enumerate(first):
                steps.append(("p1", k, u, h, i))
                if i >= NH and i % NH == 2:
                    steps.append(("nm",) + first[i - NH][:2] + (0, 0))
                if i >= lead + 3:
                    one_second()
            steps.append(("nm",) + first[-1][:2] + (0, 0))
            while done < len(second):
                one_second()
            n = len(second) // HG - 1
            return steps + [group(what, n) for what in ("av", "og", "ot")]

        L0_STEPS = small_heads(("self", "cross"), True)
        L1_STEPS = small_heads(("last",), False)

        @block.sync
        def _(sync):
            for sig in (s_out, s_mrow["last", PAIR - 1], s_split["last", 1], s_split["last", 0]):
                sync.sem_inc(*sig.open())
            for dst, src in loads:
                sync.dma_start(dst, src).then_inc(*s_load.inc("w"))
            sync.wait_ge(*s_const.once("c"))
            with sync.Fori(0, ITERS) as it:
                def store_and_stack(k, which):
                    a = XATT.index(k)
                    there = parts_d[a][which]
                    mine = part[k, which][:]
                    sync.wait_ge(*s_po.at(it, (k, which, "low")))
                    if which == 0:
                        sync.dma_start(there.rearrange("i p n -> p i n"),
                                       mine).then_inc(*s_split[k, which].inc("store"))
                    else:
                        for i in range(PARTS):
                            sync.dma_start(there[:, i].rearrange("j p n -> p j n"),
                                           mine).then_inc(*s_split[k, which].inc("store"))
                    sync.wait_ge(*s_split[k, which].at(it, "store"))
                    if which == 0:
                        for j in range(PARTS):
                            sync.dma_start(stacks[k][0][PARTS * DX * j:PARTS * DX * (j + 1)],
                                           there.rearrange("i (d h) n -> (i d) h n", d=DX))\
                                .then_inc(*s_stack[k].inc(which))
                    else:
                        sync.dma_start(stacks[k][1][0:STACK], there.rearrange("j i (d h) n -> (j i d) h n", d=DX))\
                            .then_inc(*s_stack[k].inc(which))

                def place_maxima(steps):
                    for what, k, u, _, _ in steps:
                        if what == "nm":
                            sync.wait_ge(*s_dv.at(it, (k, u, "nmlow")))
                            for i in range(PARTS):
                                sync.dma_start(stacks[k][0][MROW + i:MROW + i + 1, :, u * SEQ:(u + 1) * SEQ],
                                               nmp[:, i, :]).then_inc(*s_mrow[k, u].inc("maxima"))

                sync.wait_ge(*s_out.before(it))
                settle(sync)
                for u in range(PAIR):
                    sync.dma_start(xa[:, 2 * u:2 * u + 2, 0:D],
                                   dram["x"][bass.ds(it * PAIR + u, 1)].rearrange("b (t p) d -> p (b t) d", p=P))\
                        .then_inc(*s_in.inc("x"))
                    sync.dma_start(xT[:, u * SEQ:(u + 1) * SEQ],
                                   dram["xT"][bass.ds(it * PAIR + u, 1)].rearrange("b p n -> p (b n)"))\
                        .then_inc(*s_in.inc("x"))
                    sync.dma_start(ctxT[:, u * SEQ:(u + 1) * SEQ],
                                   dram["ctxT"][bass.ds(it * PAIR + u, 1)].rearrange("b p n -> p (b n)"))\
                        .then_inc(*s_in.inc("x"))
                for k in ("self", "cross"):
                    for which in (1, 0):
                        store_and_stack(k, which)
                sync.dma_start(stacks["cross"][1][MROW:MROW + PARTS], ks_[MROW:MROW + PARTS])\
                    .then_inc(*s_stack["cross"].inc("ones"))
                place_maxima(L0_STEPS)
                store_and_stack("last", 1)
                store_and_stack("last", 0)
                place_maxima(L1_STEPS)
                sync.wait_ge(*misc.filled(it, ("x1", "yT")))
                settle(sync)
                for e in range(NE):
                    if e >= 2:
                        sync.wait_ge(*scores.filled(it, ("moe", "h", e - 2, FC - 1)))
                        settle(sync)
                    sync.dma_start(w1e[:, e % 2], dram["m_w1"][e]).then_inc(*s_w1e[e % 2].inc(e))
                    if e >= 2:
                        sync.wait_ge(*misc.filled(it, ("moe", "y", e - 2)))
                    sync.dma_start(w2e[:, e % 2], dram["m_w2"][e].rearrange("(c p) h -> p c h", p=P))\
                        .then_inc(*s_w2e[e % 2].inc(e))
                sync.wait_ge(*s_dv.at(it, ("ln", "moe", "x")))
                settle(sync)
                for u in range(PAIR):
                    sync.dma_start(out[bass.ds(it * PAIR + u, 1)].rearrange("b (t p) d -> p (b t) d", p=P),
                                   xa[:, 2 * u:2 * u + 2, 0:D]).then_inc(*s_out.inc("y"))
            sync.wait_ge(*s_out.before(ITERS))

        @block.gpsimd
        def _(pool):
            g = nc.gpsimd
            fills = [(ident, 0.0), (identb, 0.0), (ones, 1.0), (onesb, 1.0), (mask, 0.0), (maskT, 0.0),
                     (earlier, 1.0), (head_rows, 1.0), (half, -0.5), (xa, 1.0), (vas[0], 1.0), (vas[1], 1.0), (seen, 0.0), (rtwo, FAR), (rl, FAR), (rparts, 0.0)]
            for t, v in fills:
                g.memset(t[:], v).then_inc(*s_fill.inc("fill"))
            pool.wait_ge(s_fill.sem, len(fills))
            for t in (ident, identb):
                g.affine_select(out=t[:], in_=t[:], compare_op=ALU.not_equal, fill=1.0, base=0,
                                pattern=[[-1, P]], channel_multiplier=1).then_inc(*s_const.inc("c"))
            g.affine_select(out=mask[:], in_=mask[:], compare_op=ALU.is_ge, fill=MASKED, base=0,
                            pattern=[[-1, P]], channel_multiplier=1).then_inc(*s_const.inc("c"))
            g.affine_select(out=maskT[:], in_=maskT[:], compare_op=ALU.is_ge, fill=MASKED, base=0,
                            pattern=[[1, P]], channel_multiplier=-1).then_inc(*s_const.inc("c"))
            g.affine_select(out=earlier[:], in_=earlier[:], compare_op=ALU.is_gt, fill=0.0, base=0,
                            pattern=[[1, P]], channel_multiplier=-1).then_inc(*s_const.inc("c"))
            hr = head_rows[0:32]
            g.affine_select(out=hr, in_=hr, compare_op=ALU.is_ge, fill=0.0, base=0,
                            pattern=[[P, NC], [1, P]], channel_multiplier=-HD).then_inc(*s_const.inc("c"))
            pool.wait_ge(*s_const.once("c"))
            g.affine_select(out=hr, in_=hr, compare_op=ALU.is_gt, fill=0.0, base=HD,
                            pattern=[[-P, NC], [-1, P]], channel_multiplier=HD).then_inc(*s_const.inc("c"))
            pool.wait_ge(*s_const.once("c"))
            for i in range(1, PARTS):
                g.tensor_copy(head_rows[32 * i:32 * i + 32], hr).then_inc(*s_const.inc("c"))
            g.memset(ks_[ONES:ONES + 32], 1.0).then_inc(*s_const.inc("c"))
            pool.wait_ge(*s_load.once("w"))

            with pool.Fori(0, ITERS) as it:
                def add_bias(name, bias, after):
                    pool.wait_ge(*after)
                    if bias is None:
                        settle(pool)
                        g.tensor_copy(xb[:], xa[:, :, 0:D]).then_inc(*s_po.inc(("xb", name)))
                    else:
                        g.tensor_tensor(out=xb[:], in0=xa[:, :, 0:D],
                                        in1=bias[:].unsqueeze(1).to_broadcast([P, TT, D]),
                                        op=ALU.add).then_inc(*s_po.inc(("xb", name)))

                def rsqrt(name, n, parts, dst, src, exponent):
                    pool.wait_ge(*s_dv.at(it, (name, "ve")))
                    g.tensor_tensor(out=dst, in0=src, in1=exponent, op=ALU.pow)\
                        .then_inc(*s_po.inc((name, "rstd")))

                def norm(name):
                    rsqrt(("ln", name), TT, P, rstd[:], ve[:], half[:])

                def split(k, w):
                    pool.wait_ge(*s_ac.at(it, (k, w, "high")))
                    g.tensor_tensor(out=rest[k, w][:], in0=flat[k, w][:], in1=part[k, w][:, 0],
                                    op=ALU.subtract).then_inc(*s_po.inc((k, w, "rest")))
                    pool.wait_ge(*s_ac.at(it, (k, w, "mid")))
                    g.tensor_tensor(out=part[k, w][:, 2], in0=rest[k, w][:], in1=part[k, w][:, 1],
                                    op=ALU.subtract).then_inc(*s_po.inc((k, w, "low")))

                pool.wait_ge(*s_in.at(it, "x"))
                add_bias("a0", None, s_in.at(it, "x"))
                norm("a0")
                add_bias("x0", p_b, s_dv.at(it, ("ln", "a0", "x")))
                for k in ("self", "cross"):
                    for w in (1, 0):
                        split(k, w)
                norm("x0")
                add_bias("f0", f_bo, s_dv.at(it, ("ln", "x0", "x")))
                split("last", 1)
                rsqrt(("ln", "slots"), PAIR, SLOTS, srs[:, :, 1], srs[:, :, 0], half[0:SLOTS, 0:PAIR])
                norm("f0")
                add_bias("a1", a1_bo, s_dv.at(it, ("ln", "f0", "x")))
                pool.wait_ge(*s_split["last", 1].at(it, "store"))
                settle(pool)
                for c in range(NC):
                    for w in range(2):
                        n = 2 * c + w
                        for j in range(2):
                            pool.wait_ge(*misc.emptied(it, ("a1", w, j, c)))
                        g.tensor_tensor(out=(qT, kT)[w][:, c], in0=rot[:, n % 2, 0], in1=rot[:, n % 2, 1],
                                        op=ALU.add).then_inc(*s_po.inc(("qk1", c, w)))
                norm("a1")
                add_bias("x1", None, s_dv.at(it, ("ln", "a1", "x")))
                split("last", 0)
                norm("x1")
                add_bias("moe", m_b, s_dv.at(it, ("ln", "x1", "x")))
                norm("moe")

        @block.scalar
        def _(act):
            a = nc.scalar
            act.wait_ge(*s_load.once("w"))
            act.wait_ge(*s_const.once("c"))
            with act.Fori(0, ITERS) as it:
                def attn64(L):
                    def project(c):
                        if L == 0:
                            for w, dst, sc in ((0, qT, HD ** -0.5), (1, kT, 1.0)):
                                act.wait_ge(*misc.filled(it, ("a0", w, c)))
                                a.activation(dst[:, c], misc.bank(("a0", w, c)), ACT.Copy, scale=sc)\
                                    .then_inc(*misc.empties(("a0", w, c)))
                    project(0)
                    for i, (c, u, r) in enumerate(units()):
                        if L == 0 and i % 4 == 0 and c + 1 < NC:
                            project(c + 1)
                        key = (L, "s", c, u, r)
                        h = 2 * c + r
                        if i >= 5 and i % 2 == 1:
                            out_copy(L, (i - 5) // 2)
                        act.wait_ge(*s_dv.at(it, (L, "max", c, u, r)))
                        if i >= NPR:
                            act.wait_ge(*turned.filled(it, (L, "t", *order[i - NPR])))
                        s = scores.bank(key)
                        for t, (lo, hi) in enumerate(((0, P), (P, 3 * P))):
                            ins = a.activation(probs[:, i % NPR, lo:hi], s[:, lo:hi], ACT.Exp,
                                               bias=nmax[:, i % 4, t:t + 1],
                                               accum_out=sums[:, 2 * u + t, h:h + 1])
                        ins.then_inc(*scores.empties(key))
                        if i >= 2 and (i - 2) % 4 == 3:
                            turn_copy(L, i - 2)
                    n = len(order)
                    out_copy(L, n // 2 - 2)
                    turn_copy(L, n - 1)
                    out_copy(L, n // 2 - 1)
                    act.wait_ge(*misc.filled(it, (L, "rT")))
                    a.activation(rT[:], misc.bank((L, "rT"))[0:PARTS * 32], ACT.Copy)\
                        .then_inc(*misc.empties((L, "rT")))

                def turn_copy(L, i):
                    c, u, r = order[i]
                    act.wait_ge(*turned.filled(it, (L, "t", c, u, r)))
                    if i >= 4:
                        act.wait_ge(*outs.filled(it, (L, "o", *order[i - 4][:2])))
                    a.activation(probsT[:, i % 4], turned.bank((L, "t", c, u, r))[:, 0:3 * P], ACT.Copy)\
                        .then_inc(*turned.empties((L, "t", c, u, r)))

                def out_copy(L, j):
                    c, u = order[2 * j][:2]
                    act.wait_ge(*outs.filled(it, (L, "o", c, u)))
                    a.activation(oT[:, c, u * SEQ:(u + 1) * SEQ], outs.bank((L, "o", c, u))[:, 0:SEQ], ACT.Copy)\
                        .then_inc(*outs.empties((L, "o", c, u)))

                def to_xT(name):
                    act.wait_ge(*misc.filled(it, ("xT", name)))
                    a.activation(xT[:], misc.bank(("xT", name)), ACT.Copy)\
                        .then_inc(*misc.empties(("xT", name)))

                def split(k, w, piece):
                    if piece == 0:
                        act.wait_ge(*misc.emptied(it, (k, w)))
                        a.activation(part[k, w][:, 0], flat[k, w][:], ACT.Copy).then_inc(*s_ac.inc((k, w, "high")))
                    else:
                        act.wait_ge(*s_po.at(it, (k, w, "rest")))
                        a.activation(part[k, w][:, 1], rest[k, w][:], ACT.Copy).then_inc(*s_ac.inc((k, w, "mid")))

                def attend(steps):
                    for what, k, u, h, n in steps:
                        if what == "nm":
                            act.wait_ge(*misc.filled(it, (k, u, "nmT")))
                            a.activation(nmf[:], misc.bank((k, u, "nmT"))[0:NH, 0:SEQ], ACT.Copy)\
                                .then_inc(*misc.empties((k, u, "nmT")))
                        elif what == "p2":
                            key = (k, "st", u, h)
                            width = 3 * P if k == "self" else 2 * SEQ
                            act.wait_ge(*scores.filled(it, key))
                            if n >= NPX:
                                act.wait_ge(*outs.filled(it, (steps[0][1], "o", (n - NPX) // HG)))
                            a.activation(px[:, n % NPX, 0:width], scores.bank(key)[:, 0:width], ACT.Exp)\
                                .then_inc(*scores.empties(key))
                        elif what == "og":
                            key = (steps[0][1], "o", n)
                            act.wait_ge(*outs.filled(it, key))
                            if n >= 2:
                                act.wait_ge(*turned.filled(it, (steps[0][1], "ot", n - 2)))
                            a.activation(og[:, n % 2, 0:SEQ], outs.bank(key)[:, 0:SEQ], ACT.Copy)\
                                .then_inc(*outs.empties(key))

                def to_yT(k):
                    act.wait_ge(*misc.filled(it, (k, "yT")))
                    a.activation(yT[:], misc.bank((k, "yT")), ACT.Copy).then_inc(*misc.empties((k, "yT")))

                attn64(0)
                to_xT("a0")
                for k in ("self", "cross"):
                    for piece in range(2):
                        for w in (1, 0):
                            split(k, w, piece)
                attend(L0_STEPS)
                to_yT("x0")
                to_xT("x0")

                act.wait_ge(*misc.filled(it, ("f", "h")))
                act.wait_ge(*s_dv.once("c1"))
                a.activation(hT[:], misc.bank(("f", "h"))[0:SLOTS], ACT.Gelu, bias=c1[:, 0:1])\
                    .then_inc(*misc.empties(("f", "h")))
                for t in range(TT):
                    act.wait_ge(*s_dv.at(it, ("f", "struck", t)))
                    ins = a.activation(ex[:, t], lg[:, t], ACT.Exp, bias=ntop[:, t:t + 1])
                    ins.then_inc(*s_ac.inc(("f", "ex", t)))
                split("last", 1, 0)
                act.wait_ge(*misc.filled(it, ("f", "aT")))
                a.activation(alphaT[:], misc.bank(("f", "aT"))[0:SLOTS], ACT.Copy)\
                    .then_inc(*misc.empties(("f", "aT")))
                act.wait_ge(*misc.filled(it, ("f", "siT")))
                a.activation(siT[:], misc.bank(("f", "siT"))[:, 0:PAIR * SLOTS], ACT.Copy)\
                    .then_inc(*misc.empties(("f", "siT")))
                split("last", 1, 1)
                act.wait_ge(*outs.emptied(it, ("f", "gi", PAIR - 1)))
                a.activation(ge[:], gate[:, :, 0:2 * D], ACT.Exp, scale=-1.0).then_inc(*s_ac.inc(("f", "ge")))
                act.wait_ge(*s_dv.at(it, ("f", "npre")))
                a.activation(gn[:], gate[:, :, 2 * D:3 * D], ACT.Tanh).then_inc(*s_ac.inc(("f", "gn")))
                act.wait_ge(*misc.filled(it, ("f", "snT")))
                a.activation(snT[:], misc.bank(("f", "snT"))[:, 0:PAIR * SLOTS], ACT.Copy)\
                    .then_inc(*misc.empties(("f", "snT")))
                for u in range(PAIR):
                    act.wait_ge(*s_dv.at(it, ("f", "smax", u)))
                    a.activation(sp_[:, u], misc.bank(("f", "ss"))[0:SLOTS, u * SLOTS:(u + 1) * SLOTS], ACT.Exp,
                                 bias=sm[:, u, 1:2], scale=DQ ** -0.5,
                                 accum_out=sm[:, u, 2:3]).then_inc(
                                     *(misc.empties(("f", "ss")) if u == PAIR - 1 else s_ac.inc(("f", "sp", u))))
                act.wait_ge(*misc.filled(it, ("f", "spT")))
                a.activation(spT[:], misc.bank(("f", "spT"))[0:SLOTS, 0:PAIR * SLOTS], ACT.Copy)\
                    .then_inc(*misc.empties(("f", "spT")))
                act.wait_ge(*misc.filled(it, ("f", "syT")))
                a.activation(syT[:], misc.bank(("f", "syT"))[:, 0:PAIR * SLOTS], ACT.Copy)\
                    .then_inc(*misc.empties(("f", "syT")))
                to_xT("f0")

                attn64(1)
                to_xT("a1")
                for piece in range(2):
                    split("last", 0, piece)
                attend(L1_STEPS)
                to_yT("x1")
                to_xT("x1")

                for t in range(TT):
                    act.wait_ge(*s_dv.at(it, ("m", "struck", t)))
                    a.activation(rex[:, t], rl[:, t, :, 0:NE], ACT.Exp, bias=nrt[:, t:t + 1])\
                        .then_inc(*s_ac.inc(("m", "ex", t)))
                for e in range(NE):
                    for f in range(FC):
                        act.wait_ge(*scores.filled(it, ("moe", "h", e, f)))
                        if e >= 2:
                            act.wait_ge(*misc.filled(it, ("moe", "y", e - 2)))
                        a.activation(hid[:, e % 2, f], scores.bank(("moe", "h", e, f)), ACT.Gelu_apprx_tanh)\
                            .then_inc(*scores.empties(("moe", "h", e, f)))

        @block.vector
        def _(dve):
            v = nc.vector
            dve.wait_ge(*s_load.once("w"))
            dve.wait_ge(*s_const.once("c"))
            dve.wait_ge(*pre.at(0, "smean"))
            v.tensor_scalar(smean[:], misc.tensor[:, 0, 0:1], 1.0 / SLOTS, None, ALU.mult)\
                .then_inc(*pred.inc("smean"))
            dve.wait_ge(*pre.at(0, "c1"))
            v.tensor_tensor(out=c1[:], in0=misc.tensor[0:SLOTS, 0, 8:9], in1=f_b1[:], op=ALU.add)\
                .then_inc(*pred.inc("c1"))
            v.tensor_tensor(out=crz[:], in0=misc.tensor[0:SLOTS, 1, 0:3 * D], in1=f_bhh[:], op=ALU.add)\
                .then_inc(*pred.inc("crz"))
            dve.wait_ge(*pred.once("crz"))
            v.tensor_copy(ghn[:], crz[:, 2 * D:3 * D]).then_inc(*pred.inc("ghn"))
            dve.wait_ge(*pred.once("ghn"))
            v.tensor_tensor(out=crz[:, 0:2 * D], in0=crz[:, 0:2 * D], in1=f_bih[:, 0:2 * D], op=ALU.add)\
                .then_inc(*pred.inc("a"))
            v.tensor_copy(crz[:, 2 * D:3 * D], f_bih[:, 2 * D:3 * D]).then_inc(*pred.inc("b"))
            v.tensor_scalar(itau[:], f_tau[:, 0:1], -1.0, None, ALU.mult).then_inc(*pred.inc("t0"))
            dve.wait_ge(*pred.once("t0"))
            v.tensor_tensor(out=itau[:], in0=itau[:], in1=f_tau[:, 0:1], op=ALU.max).then_inc(*pred.inc("t1"))
            dve.wait_ge(*pred.once("t1"))
            v.tensor_scalar(itau[:], itau[:], 0.1, None, ALU.add).then_inc(*pred.inc("t2"))
            dve.wait_ge(*pred.once("t2"))
            v.reciprocal(itau[:], itau[:]).then_inc(*pred.inc("t3"))
            dve.wait_ge(*pred.once("t3"))

            with dve.Fori(0, ITERS) as it:
                def link(ins, key):
                    ins.then_inc(*s_dv.inc(key))
                    dve.wait_ge(*s_dv.at(it, key))

                def attn64(L):
                    def project(c):
                        if L == 0:
                            return
                        for w in range(2):
                            n = 2 * c + w
                            if n >= 2:
                                dve.wait_ge(*s_po.at(it, ("qk1", (n - 2) // 2, n % 2)))
                            for j in range(2):
                                key = ("a1", w, j, c)
                                dve.wait_ge(*misc.filled(it, key))
                                b = ((a1_bq, a1_bqs), (a1_bk, a1_bks))[w][j]
                                ins = v.scalar_tensor_tensor(
                                    out=rot[:, n % 2, j].rearrange("p (u n) -> p u n", u=PAIR),
                                    in0=misc.bank(key).rearrange("p (u n) -> p u n", u=PAIR),
                                    scalar=b[:, c:c + 1],
                                    in1=rope[:, 2 * w + j].unsqueeze(1).to_broadcast([P, PAIR, SEQ]),
                                    op0=ALU.add, op1=ALU.mult)
                                ins.then_inc(*misc.empties(key))

                    for t in range(TT):
                        for hf in range(2):
                            key = (L, "v", t, hf)
                            dve.wait_ge(*misc.filled(it, key))
                            dst = vv[:, t, hf * 512:(hf + 1) * 512]
                            if L == 0:
                                v.tensor_copy(dst, misc.bank(key)).then_inc(*misc.empties(key))
                            else:
                                v.tensor_tensor(out=dst, in0=misc.bank(key),
                                                in1=a1_bv[:, hf * 512:(hf + 1) * 512], op=ALU.add)\
                                    .then_inc(*misc.empties(key))
                    project(0)
                    n = len(order)
                    for i in range(n + 2):
                        if i < n:
                            c, u, r = order[i]
                            if i % 4 == 0 and c + 1 < NC:
                                project(c + 1)
                            key = (L, "s", c, u, r)
                            dve.wait_ge(*scores.filled(it, key))
                            if i >= 4:
                                dve.wait_ge(*scores.emptied(it, (L, "s", *order[i - 4])))
                            s = scores.bank(key)
                            v.tensor_reduce(nmax[:, i % 4, 0:1], s[:, 0:P], AX.X, ALU.max, negate=True)
                            v.tensor_reduce(nmax[:, i % 4, 1:2], s[:, P:3 * P], AX.X, ALU.max, negate=True)\
                                .then_inc(*s_dv.inc((L, "max", c, u, r)))
                        if i >= 2 and (i - 2) % 4 != 3:
                            j = i - 2
                            c, u, r = order[j]
                            dve.wait_ge(*turned.filled(it, (L, "t", c, u, r)))
                            if j >= 4:
                                dve.wait_ge(*outs.filled(it, (L, "o", *order[j - 4][:2])))
                            v.tensor_copy(probsT[:, j % 4], turned.bank((L, "t", c, u, r))[:, 0:3 * P])\
                                .then_inc(*turned.empties((L, "t", c, u, r)))
                    dve.wait_ge(*scores.emptied(it, (L, "s", *order[-1])))
                    dve.wait_ge(*scores.emptied(it, (L, "s", *order[-2])))
                    link(v.reciprocal(rsum[:], sums[:]), (L, "rsum"))
                    link(v.tensor_copy(rparts[:, :, 0, 0:NH], rsum[:]), (L, "rhigh"))
                    link(v.tensor_tensor(out=rrest[:], in0=rsum[:], in1=rparts[:, :, 0, 0:NH], op=ALU.subtract),
                         (L, "rrest"))
                    link(v.tensor_copy(rparts[:, :, 1, 0:NH], rrest[:]), (L, "rmid"))
                    v.tensor_tensor(out=rparts[:, :, 2, 0:NH], in0=rrest[:], in1=rparts[:, :, 1, 0:NH],
                                    op=ALU.subtract).then_inc(*s_dv.inc((L, "rlow")))
                    for c in range(NC):
                        dve.wait_ge(*misc.filled(it, (L, "R", c)))
                        dve.wait_ge(*outs.emptied(it, (L, "o", c, PAIR - 1)))
                        v.tensor_tensor(out=oT[:, c], in0=oT[:, c], in1=misc.bank((L, "R", c)), op=ALU.mult)\
                            .then_inc(*misc.empties((L, "R", c)))

                def norm(name, src, last):
                    dve.wait_ge(*s_po.at(it, ("xb", name)))
                    if last is None:
                        dve.wait_ge(*misc.filled(it, src))
                        y = misc.bank(src).rearrange("p (t d) -> p t d", t=TT)
                        v.tensor_tensor(out=xr[:], in0=xb[:], in1=y, op=ALU.add)\
                            .then_inc(*misc.empties(src))
                        dve.wait_ge(*misc.emptied(it, src))
                    else:
                        link(v.tensor_tensor(out=xr[:], in0=xb[:], in1=acc[:], op=ALU.add), ("ln", name, "r"))
                    for t in range(TT):
                        ins = v.bn_stats(stats[:, t], xr[:, t])
                    link(ins, ("ln", name, "stats"))
                    settle(dve)
                    for t in range(TT):
                        ins = v.bn_aggr(mv[:, t], stats[:, t])
                    link(ins, ("ln", name, "mv"))
                    v.tensor_scalar(ve[:], mv[:, :, 1], EPS, None, ALU.add).then_inc(*s_dv.inc((("ln", name), "ve")))
                    dve.wait_ge(*s_po.at(it, (("ln", name), "rstd")))
                    for t in range(TT):
                        ins = v.tensor_scalar(xa[:, t, 0:D], xr[:, t], mv[:, t, 0:1], rstd[:, t:t + 1],
                                              ALU.subtract, ALU.mult)
                    ins.then_inc(*s_dv.inc(("ln", name, "x")))

                def project(k, w, b):
                    sc = SCALE[k] if w == 0 else 1.0
                    dve.wait_ge(*misc.filled(it, (k, w)))
                    if b is None:
                        ins = v.tensor_scalar(flat[k, w][:], misc.bank((k, w)), sc, None, ALU.mult)
                    else:
                        ins = v.tensor_scalar(flat[k, w][:], misc.bank((k, w)), b[:, 0:1], sc, ALU.add, ALU.mult)
                    ins.then_inc(*misc.empties((k, w)))

                def project_values(k, bv):
                    dve.wait_ge(*misc.filled(it, (k, "v")))
                    dst = va[k][:, :, 0:NH * VW].rearrange("p t (h w) -> p t h w", w=VW)[:, :, :, 0:DX]
                    src = misc.bank((k, "v")).rearrange("p (t h d) -> p t h d", t=TT, h=NH)
                    if bv is None:
                        v.tensor_copy(dst, src).then_inc(*misc.empties((k, "v")))
                    else:
                        for t in range(TT):
                            ins = v.tensor_tensor(out=dst[:, t], in0=src[:, t],
                                                  in1=bv[:].rearrange("p (h d) -> p h d", h=NH), op=ALU.add)
                        ins.then_inc(*misc.empties((k, "v")))

                def attend(steps, dests):
                    placed = None
                    for what, k, u, h, n in steps:
                        if what == "p1":
                            key = (k, "s", u, h)
                            dve.wait_ge(*scores.filled(it, key))
                            s = scores.bank(key)
                            if k == "self":
                                v.tensor_reduce(nm[k][:, 2 * u, h:h + 1], s[:, 0:P], AX.X, ALU.max, negate=True)
                                ins = v.tensor_reduce(nm[k][:, 2 * u + 1, h:h + 1], s[:, P:3 * P], AX.X, ALU.max,
                                                      negate=True)
                            else:
                                ins = v.tensor_reduce(nm[k][:, 2 * u:2 * u + 2, h],
                                                      s.rearrange("p (t n) -> p t n", t=2), AX.X, ALU.max,
                                                      negate=True)
                            ins.then_inc(*scores.empties(key))
                        elif what == "nm":
                            dve.wait_ge(*misc.emptied(it, (k, u, "nmT")))
                            if placed is not None:
                                dve.wait_ge(*s_mrow[placed].at(it, "maxima"))
                            elif k == "self":
                                dve.wait_ge(*s_mrow["last", PAIR - 1].before(it))
                            else:
                                dve.wait_ge(*s_mrow["cross", PAIR - 1].at(it, "maxima"))
                            placed = (k, u)
                            link(v.tensor_copy(nmp[:, 0], nmf[:]), (k, u, "nmhigh"))
                            link(v.tensor_tensor(out=nmr[:], in0=nmf[:], in1=nmp[:, 0], op=ALU.subtract),
                                 (k, u, "nmrest"))
                            link(v.tensor_copy(nmp[:, 1], nmr[:]), (k, u, "nmmid"))
                            v.tensor_tensor(out=nmp[:, 2], in0=nmr[:], in1=nmp[:, 1], op=ALU.subtract)\
                                .then_inc(*s_dv.inc((k, u, "nmlow")))
                        elif what == "ot":
                            key = (steps[0][1], "ot", n)
                            dve.wait_ge(*turned.filled(it, key))
                            o = turned.bank(key)[:, 0:2 * P].rearrange("p (t h w) -> p t h w", t=2, h=HG)
                            link(v.reciprocal(den[:, h, 2 * u:2 * u + 2, :], o[:, :, :, DX]), (k, "den", n))
                            d = den[:, h, 2 * u:2 * u + 2, :].unsqueeze(3).to_broadcast([P, 2, HG, DX])
                            dst = dests[k][:, 2 * u:2 * u + 2, h * HG * DX:(h + 1) * HG * DX]
                            v.tensor_tensor(out=dst.rearrange("p t (h d) -> p t h d", h=HG), in0=o[:, :, :, 0:DX],
                                            in1=d, op=ALU.mult).then_inc(*turned.empties(key))

                attn64(0)
                norm("a0", ("y", "a0"), None)
                for k, b in (("self", (s_bq, s_bk, s_bv)), ("cross", (c_bq, c_bk, c_bv))):
                    for w in (1, 0):
                        project(k, w, b[w])
                    project_values(k, b[2])
                attend(L0_STEPS, {"self": ys, "cross": yc})
                for n in (2 * PAIR * NG - 1, 2 * PAIR * NG - 2):
                    dve.wait_ge(*turned.emptied(it, ("self", "ot", n)))
                v.tensor_tensor(out=ys[:], in0=ys[:], in1=yc[:], op=ALU.add).then_inc(*s_dv.inc(("x0", "y")))
                norm("x0", ("y", "x0"), None)

                for t in range(TT):
                    key = ("f", "lg", t)
                    dve.wait_ge(*outs.filled(it, key))
                    v.tensor_tensor(out=lg[:, t, 0], in0=outs.bank(key)[:, 0:SLOTS], in1=f_b2[:], op=ALU.add)\
                        .then_inc(*outs.empties(key))
                    dve.wait_ge(*outs.emptied(it, key))
                    link(v.tensor_scalar(lg[:, t, 0], lg[:, t, 0], itau[:, 0:1], None, ALU.mult), ("f", "lg", t))
                    settle(dve)
                    link(v.max(top[:, t], lg[:, t, 0]), ("f", "top", t))
                    settle(dve)
                    v.match_replace(lg[:, t, 1], top[:, t], lg[:, t, 0], -FAR)
                    v.tensor_scalar(ntop[:, t:t + 1], top[:, t, 0:1], -1.0, None, ALU.mult)\
                        .then_inc(*s_dv.inc(("f", "struck", t)))
                project("last", 1, None)
                project_values("last", None)
                for t in range(TT):
                    dve.wait_ge(*s_ac.at(it, ("f", "ex", t)))
                    link(v.tensor_tensor(out=alpha[:, t], in0=ex[:, t, 0], in1=ex[:, t, 1], op=ALU.subtract),
                         ("f", "a0", t))
                    link(v.tensor_reduce(asum[:, t:t + 1], alpha[:, t], AX.X, ALU.add), ("f", "asum", t))
                    link(v.reciprocal(arec[:, t:t + 1], asum[:, t:t + 1]), ("f", "arec", t))
                    v.tensor_scalar(alpha[:, t], alpha[:, t], arec[:, t:t + 1], None, ALU.mult)\
                        .then_inc(*s_dv.inc(("f", "alpha", t)))
                for u in range(PAIR):
                    key = ("f", "si", u)
                    dve.wait_ge(*outs.filled(it, key))
                    link(v.tensor_scalar(dn[:, u:u + 1], outs.bank(key)[0:SLOTS, D:D + 1], 1e-8, None, ALU.add),
                         ("f", "dn0", u))
                    link(v.reciprocal(dn[:, u:u + 1], dn[:, u:u + 1]), ("f", "dn1", u))
                    v.tensor_scalar(si[:, u], outs.bank(key)[0:SLOTS, 0:D], dn[:, u:u + 1], None, ALU.mult)\
                        .then_inc(*outs.empties(key))
                for u in range(PAIR):
                    key = ("f", "gi", u)
                    dve.wait_ge(*outs.filled(it, key))
                    v.tensor_tensor(out=gate[:, u], in0=outs.bank(key)[0:SLOTS, 0:3 * D], in1=crz[:], op=ALU.add)\
                        .then_inc(*outs.empties(key))
                dve.wait_ge(*s_ac.at(it, ("f", "ge")))
                link(v.tensor_scalar(rz[:], ge[:], 1.0, None, ALU.add), ("f", "rz0"))
                link(v.reciprocal(rz[:], rz[:]), ("f", "rz"))
                for u in range(PAIR):
                    ins = v.tensor_tensor(out=sn[:, u], in0=rz[:, u, 0:D], in1=ghn[:], op=ALU.mult)
                link(ins, ("f", "rg"))
                v.tensor_tensor(out=gate[:, :, 2 * D:3 * D], in0=gate[:, :, 2 * D:3 * D], in1=sn[:], op=ALU.add)\
                    .then_inc(*s_dv.inc(("f", "npre")))
                dve.wait_ge(*s_ac.at(it, ("f", "gn")))
                for u in range(PAIR):
                    ins = v.tensor_tensor(out=sn[:, u], in0=f_slots[:], in1=gn[:, u], op=ALU.subtract)
                link(ins, ("f", "sn0"))
                link(v.tensor_tensor(out=sn[:], in0=sn[:], in1=rz[:, :, D:2 * D], op=ALU.mult), ("f", "sn1"))
                v.tensor_tensor(out=sn[:], in0=sn[:], in1=gn[:], op=ALU.add).then_inc(*s_dv.inc(("f", "sn")))
                for n, dst, b in (("sq", sq, f_bq), ("sk", sk, f_bk)):
                    dve.wait_ge(*outs.filled(it, ("f", n)))
                    v.tensor_scalar(dst[:], outs.bank(("f", n))[0:DQ, 0:PAIR * SLOTS], b[:, 0:1], None, ALU.add)\
                        .then_inc(*outs.empties(("f", n)))
                dve.wait_ge(*outs.filled(it, ("f", "sv")))
                for u in range(PAIR):
                    ins = v.tensor_tensor(out=svv[:, u], in0=outs.bank(("f", "sv"))[0:SLOTS, u * D:(u + 1) * D],
                                          in1=f_bv[:], op=ALU.add)
                ins.then_inc(*outs.empties(("f", "sv")))
                dve.wait_ge(*misc.filled(it, ("f", "ss")))
                for u in range(PAIR):
                    link(v.tensor_reduce(sm[:, u, 0:1], misc.bank(("f", "ss"))[0:SLOTS, u * SLOTS:(u + 1) * SLOTS],
                                         AX.X, ALU.max, negate=True), ("f", "sm", u))
                for u in range(PAIR):
                    v.tensor_scalar(sm[:, u, 1:2], sm[:, u, 0:1], DQ ** -0.5, None, ALU.mult)\
                        .then_inc(*s_dv.inc(("f", "smax", u)))
                dve.wait_ge(*misc.emptied(it, ("f", "ss")))
                link(v.reciprocal(sm[:, :, 3], sm[:, :, 2]), ("f", "sr"))
                dve.wait_ge(*outs.filled(it, ("f", "comm")))
                for u in range(PAIR):
                    ins = v.scalar_tensor_tensor(out=sy[:, u], in0=outs.bank(("f", "comm"))[0:SLOTS, u * D:(u + 1) * D],
                                                 scalar=sm[:, u, 3:4], in1=sn[:, u], op0=ALU.mult, op1=ALU.add)
                ins.then_inc(*outs.empties(("f", "comm")))
                dve.wait_ge(*outs.emptied(it, ("f", "comm")))
                for u in range(PAIR):
                    ins = v.bn_stats(sst[:, u], sy[:, u])
                link(ins, ("f", "sst"))
                settle(dve)
                for u in range(PAIR):
                    ins = v.bn_aggr(smv[:, u], sst[:, u])
                link(ins, ("f", "smv"))
                v.tensor_scalar(srs[:, :, 0], smv[:, :, 1], EPS, None, ALU.add)\
                    .then_inc(*s_dv.inc((("ln", "slots"), "ve")))
                dve.wait_ge(*s_po.at(it, (("ln", "slots"), "rstd")))
                for u in range(PAIR):
                    ins = v.tensor_scalar(sy[:, u], sy[:, u], smv[:, u, 0:1], srs[:, u, 1:2], ALU.subtract, ALU.mult)
                link(ins, ("f", "y0"))
                for u in range(PAIR):
                    ins = v.tensor_tensor(out=sy[:, u], in0=sy[:, u], in1=f_lng[:], op=ALU.mult)
                link(ins, ("f", "y1"))
                for u in range(PAIR):
                    ins = v.tensor_tensor(out=sy[:, u], in0=sy[:, u], in1=f_lnb[:], op=ALU.add)
                ins.then_inc(*s_dv.inc(("f", "sy")))
                dve.wait_ge(*outs.filled(it, ("f", "svT")))
                v.tensor_scalar(svT[:], outs.bank(("f", "svT"))[:, 0:PAIR * SLOTS], f_bvp[:, 0:1], None, ALU.add)\
                    .then_inc(*outs.empties(("f", "svT")))
                dve.wait_ge(*outs.filled(it, ("f", "svo")))
                v.tensor_copy(svo[:].rearrange("p u d -> p (u d)"), outs.bank(("f", "svo"))[0:SLOTS, 0:PAIR * D])\
                    .then_inc(*outs.empties(("f", "svo")))
                norm("f0", ("y", "f0"), None)

                attn64(1)
                norm("a1", ("y", "a1"), None)
                project("last", 0, None)
                attend(L1_STEPS, {"last": ys})
                norm("x1", ("y", "x1"), None)

                for t in range(TT):
                    key = ("m", "rl", t)
                    dve.wait_ge(*outs.filled(it, key))
                    v.tensor_copy(rl[:, t, 0, 0:NE], outs.bank(key)[:, 0:NE]).then_inc(*outs.empties(key))
                    dve.wait_ge(*outs.emptied(it, key))
                    settle(dve)
                    link(v.max(rtop[:, t], rl[:, t, 0, 0:NE]), ("m", "top", t))
                    link(v.tensor_copy(rtwo[:, t, 0:TOP], rtop[:, t, 0:TOP]), ("m", "two", t))
                    settle(dve)
                    link(v.match_replace(rl[:, t, 1], rtwo[:, t], rl[:, t, 0], -FAR), ("m", "rep", t))
                    v.tensor_scalar(nrt[:, t:t + 1], rtop[:, t, 0:1], -1.0, None, ALU.mult)\
                        .then_inc(*s_dv.inc(("m", "struck", t)))
                    link(v.tensor_tensor(out=chosen[:, t], in0=rl[:, t, 0, 0:NE], in1=rl[:, t, 1, 0:NE], op=ALU.not_equal),
                         ("m", "chosen", t))
                    v.tensor_copy(chosenb[:, t], chosen[:, t])
                    v.tensor_copy(seenb[:, t], seen[:, t])
                    link(v.tensor_tensor(out=seen[:, t + 1], in0=seen[:, t], in1=chosen[:, t], op=ALU.add),
                         ("m", "seen", t))
                link(v.tensor_copy(seen[:, 0], seen[:, TT]), ("m", "carry"))
                for t in range(TT):
                    dve.wait_ge(*s_ac.at(it, ("m", "ex", t)))
                    link(v.tensor_reduce(rden[:, t:t + 1], rex[:, t, 0], AX.X, ALU.add), ("m", "den", t))
                    link(v.reciprocal(rrec[:, t:t + 1], rden[:, t:t + 1]), ("m", "rec", t))
                    link(v.tensor_tensor(out=wexp[:, t], in0=rex[:, t, 0], in1=rex[:, t, 1], op=ALU.subtract),
                         ("m", "we", t))
                    key = ("m", "pos", t)
                    dve.wait_ge(*outs.filled(it, key))
                    v.tensor_scalar(fits[:, t], outs.bank(key)[:, 0:NE], float(CAPACITY), None, ALU.is_lt)\
                        .then_inc(*outs.empties(key))
                    dve.wait_ge(*outs.emptied(it, key))
                    link(v.scalar_tensor_tensor(out=wgt[:, t], in0=wexp[:, t], scalar=rrec[:, t:t + 1],
                                                in1=fits[:, t], op0=ALU.mult, op1=ALU.mult), ("m", "w", t))
                for e in range(NE):
                    key = ("moe", "y", e)
                    dve.wait_ge(*misc.filled(it, key))
                    y = misc.bank(key).rearrange("p (t d) -> p t d", t=TT)
                    for t in range(TT):
                        if e == 0:
                            ins = v.tensor_scalar(acc[:, t], y[:, t], wgt[:, t, e:e + 1], None, ALU.mult)
                        else:
                            ins = v.scalar_tensor_tensor(out=acc[:, t], in0=y[:, t], scalar=wgt[:, t, e:e + 1],
                                                         in1=acc[:, t], op0=ALU.mult, op1=ALU.add)
                    ins.then_inc(*misc.empties(key))
                    dve.wait_ge(*misc.emptied(it, key))
                norm("moe", None, acc)

        @block.tensor
        def _(pe):
            t_ = nc.tensor
            for ring in (scores, turned, outs, misc):
                ring.open(pe)
            pe.wait_ge(*s_load.once("w"))
            pe.wait_ge(*s_const.once("c"))
            t_.matmul(misc.tensor[:, 0, 0:1], f_slots[:], ones[0:SLOTS, 0:1], start=True, stop=True)\
                .then_inc(*pre.inc("smean"))
            pe.wait_ge(*pred.once("smean"))
            t_.matmul(misc.tensor[0:SLOTS, 0, 8:9], f_w1[:, 1, :], smean[:], start=True, stop=True)
            t_.matmul(misc.tensor[0:SLOTS, 1, 0:3 * D], f_slotsT[:], f_whh[:], start=True, stop=True)\
                .then_inc(*pre.inc("c1"))
            pe.wait_ge(*pred.once("crz"))

            with pe.Fori(0, ITERS) as it:
                def one(ring, key, out_of, lhsT, rhs):
                    bank = ring.take(key)
                    pe.wait_ge(*ring.reusable(it, key))
                    if key[0] == "f":
                        settle(pe)
                    t_.matmul(out_of(bank), lhsT, rhs, start=True, stop=True).then_inc(*ring.fills(key))

                def masked(out, m):
                    t_.matmul(out, identb[:], m[:], start=False, stop=True, skip_group_check=True)

                def attn64(L, wq, wqs, wk, wks, wv, wo, name):
                    def project(c):
                        cols = slice(c * P, (c + 1) * P)
                        if L == 0:
                            for w, m in ((0, wq), (1, wk)):
                                one(misc, ("a0", w, c), lambda b: b, m[:, cols], xT[:])
                        else:
                            for w, ms in ((0, (wq, wqs)), (1, (wk, wks))):
                                for j in range(2):
                                    one(misc, ("a1", w, j, c), lambda b: b, ms[j][:, cols], xT[:])

                    def score(i):
                        c, u, r = order[i]
                        key = (L, "s", c, u, r)
                        s = scores.take(key)
                        pe.wait_ge(*scores.reusable(it, key))
                        if L == 0:
                            pe.wait_ge(*misc.emptied(it, ("a0", 1, c)))
                            pe.wait_ge(*misc.emptied(it, ("a0", 0, c)))
                        else:
                            pe.wait_ge(*s_po.at(it, ("qk1", c, 1)))
                        rows, q0 = slice(HD * r, HD * r + HD), u * SEQ
                        t_.matmul(s[:, 0:P], qT[rows, c, q0:q0 + P], kT[rows, c, q0:q0 + P],
                                  start=True, stop=False, skip_group_check=True)
                        t_.matmul(s[:, P:3 * P], qT[rows, c, q0 + P:q0 + 2 * P], kT[rows, c, q0:q0 + SEQ],
                                  start=False, stop=False, skip_group_check=True)
                        masked(s[:, 0:P], mask)
                        t_.matmul(s[:, 2 * P:3 * P], identb[:], mask[:], start=False, stop=True,
                                  skip_group_check=True).then_inc(*scores.fills(key))

                    def turn(i):
                        key = (L, "t", *order[i])
                        b = turned.take(key)
                        pe.wait_ge(*turned.reusable(it, key))
                        pe.wait_ge(*scores.emptied(it, (L, "s", *order[i])))
                        for j in range(3):
                            ins = t_.transpose(b[:, j * P:(j + 1) * P], probs[:, i % NPR, j * P:(j + 1) * P],
                                               ident[:])
                        ins.then_inc(*turned.fills(key))

                    def values(p):
                        c, u, _ = order[2 * p]
                        key = (L, "o", c, u)
                        b = outs.take(key)
                        pe.wait_ge(*outs.reusable(it, key))
                        for r in range(2):
                            pe.wait_ge(*turned.emptied(it, (L, "t", c, u, r)))
                        for kt, (lo, hi, at) in enumerate(((0, 2 * P, 0), (2 * P, 3 * P, P))):
                            for r in range(2):
                                h = 2 * c + r
                                ins = t_.matmul(b[HD * r:HD * r + HD, at:SEQ], vv[:, 2 * u + kt, h * HD:(h + 1) * HD],
                                                probsT[:, (2 * p + r) % 4, lo:hi], start=(kt == 0), stop=(kt == 1),
                                                skip_group_check=True)
                        ins.then_inc(*outs.fills(key))

                    for t in range(TT):
                        for hf in range(2):
                            one(misc, (L, "v", t, hf), lambda b: b, xT[:, t * P:(t + 1) * P],
                                wv[:, hf * 512:(hf + 1) * 512])
                    project(0)
                    n = len(order)
                    for i in range(n + 3):
                        if i < n:
                            if i % 4 == 0 and order[i][0] + 1 < NC:
                                project(order[i][0] + 1)
                            score(i)
                        if 2 <= i < n + 2:
                            turn(i - 2)
                        if i >= 4 and i % 2 == 0:
                            values((i - 4) // 2)
                    key = (L, "rT")
                    b = misc.take(key)
                    pe.wait_ge(*misc.reusable(it, key))
                    pe.wait_ge(*s_dv.at(it, (L, "rlow")))
                    for t in range(TT):
                        ins = t_.matmul(b[0:PARTS * 32, t * P:(t + 1) * P],
                                        rparts[:, t].rearrange("p a h -> p (a h)"), identb[:],
                                        start=True, stop=True)
                    ins.then_inc(*misc.fills(key))
                    pe.wait_ge(*misc.emptied(it, key))
                    for c in range(NC):
                        one(misc, (L, "R", c), lambda b: b, head_rows[:, c, :], rT[:])
                    values_out(name, lambda: [(oT[:, c], wo[:, c], (L, "R", c)) for c in range(NC)])

                def values_out(name, terms):
                    key = ("y", name)
                    y = misc.take(key)
                    pe.wait_ge(*misc.reusable(it, key))
                    terms = terms()
                    for n, (lhs, rhs, ready) in enumerate(terms):
                        pe.wait_ge(*misc.emptied(it, ready))
                        for t in range(TT):
                            ins = t_.matmul(y[:, t * D:(t + 1) * D], lhs[:, t * P:(t + 1) * P], rhs,
                                            start=(n == 0 and t == 0), stop=(n == len(terms) - 1),
                                            skip_group_check=True)
                    ins.then_inc(*misc.fills(key))

                def to_xT(name):
                    key = ("xT", name)
                    b = misc.take(key)
                    pe.wait_ge(*misc.reusable(it, key))
                    pe.wait_ge(*s_dv.at(it, ("ln", name, "x")))
                    for t in range(TT):
                        ins = t_.transpose(b[:, t * P:(t + 1) * P], xa[:, t, 0:D], ident[:])
                    ins.then_inc(*misc.fills(key))
                    pe.wait_ge(*misc.emptied(it, key))

                def project_small(k, w, weight):
                    other = xT if w == 0 or k == "self" else ctxT
                    if w < 2:
                        one(misc, (k, w), lambda b: b, weight[:], other[:])
                        return
                    key = (k, "v")
                    b = misc.take(key)
                    pe.wait_ge(*misc.reusable(it, key))
                    for t in range(TT):
                        ins = t_.matmul(b[:, t * D:(t + 1) * D], other[:, t * P:(t + 1) * P], weight[:],
                                        start=True, stop=True)
                    ins.then_inc(*misc.fills(key))

                def first_scores(k, u, h):
                    key = (k, "s", u, h)
                    s = scores.take(key)
                    pe.wait_ge(*scores.reusable(it, key))
                    if (u, h) == (0, 0):
                        pe.wait_ge(*s_stack[k].at(it, 0 if k != "cross" else "ones"))
                    q0 = u * SEQ
                    qh, kh = stacks[k][0][0:STACK, h], stacks[k][1][0:STACK, h]
                    if k == "self":
                        t_.matmul(s[:, 0:P], qh[:, q0:q0 + P], kh[:, q0:q0 + P],
                                  start=True, stop=False, skip_group_check=True)
                        t_.matmul(s[:, P:3 * P], qh[:, q0 + P:q0 + SEQ], kh[:, q0:q0 + SEQ],
                                  start=False, stop=False, skip_group_check=True)
                        masked(s[:, 0:P], mask)
                        ins = t_.matmul(s[:, 2 * P:3 * P], identb[:], mask[:], start=False, stop=True,
                                        skip_group_check=True)
                    else:
                        for t in range(2):
                            ins = t_.matmul(s[:, t * SEQ:(t + 1) * SEQ], qh[:, q0 + t * P:q0 + (t + 1) * P],
                                            kh[:, q0:q0 + SEQ], start=True, stop=True)
                    ins.then_inc(*scores.fills(key))

                def turned_maxima(k, u):
                    key = (k, u, "nmT")
                    b = misc.take(key)
                    pe.wait_ge(*misc.reusable(it, key))
                    pe.wait_ge(*scores.emptied(it, (k, "s", u, NH - 1)))
                    for t in range(2):
                        ins = t_.transpose(b[0:NH, t * P:(t + 1) * P], nm[k][:, 2 * u + t], ident[:])
                    ins.then_inc(*misc.fills(key))

                def second_scores(k, u, h):
                    key = (k, "st", u, h)
                    s = scores.take(key)
                    pe.wait_ge(*scores.reusable(it, key))
                    if h == 0:
                        pe.wait_ge(*s_mrow[k, u].at(it, "maxima"))
                    q0 = u * SEQ
                    qh, kh = stacks[k][0][0:MROW + PARTS, h], stacks[k][1][0:MROW + PARTS, h]
                    if k == "self":
                        t_.matmul(s[:, 0:SEQ], kh[:, q0:q0 + P], qh[:, q0:q0 + SEQ],
                                  start=True, stop=False, skip_group_check=True)
                        t_.matmul(s[:, SEQ:3 * P], kh[:, q0 + P:q0 + SEQ], qh[:, q0 + P:q0 + SEQ],
                                  start=False, stop=False, skip_group_check=True)
                        masked(s[:, 0:P], maskT)
                        ins = t_.matmul(s[:, SEQ:3 * P], identb[:], maskT[:], start=False, stop=True,
                                        skip_group_check=True)
                    else:
                        for t in range(2):
                            ins = t_.matmul(s[:, t * SEQ:(t + 1) * SEQ], kh[:, q0 + t * P:q0 + (t + 1) * P],
                                            qh[:, q0:q0 + SEQ], start=True, stop=True)
                    ins.then_inc(*scores.fills(key))

                def attend(steps):
                    for what, k, u, h, n in steps:
                        if what == "p1":
                            first_scores(k, u, h)
                        elif what == "nm":
                            turned_maxima(k, u)
                        elif what == "p2":
                            second_scores(k, u, h)
                        elif what == "av":
                            key = (steps[0][1], "o", n)
                            b = outs.take(key)
                            pe.wait_ge(*outs.reusable(it, key))
                            pe.wait_ge(*scores.emptied(it, (k, "st", u, HG * h + HG - 1)))
                            for kt in range(2):
                                lo, hi, at = ((0, SEQ, 0), (SEQ, 3 * P, P) if k == "self" else (SEQ, 2 * SEQ, 0))[kt]
                                for j in range(HG):
                                    c0 = (HG * h + j) * VW
                                    ins = t_.matmul(b[32 * j:32 * j + 32, at:SEQ], va[k][:, 2 * u + kt, c0:c0 + 32],
                                                    px[:, (HG * n + j) % NPX, lo:hi], start=(kt == 0),
                                                    stop=(kt == 1), skip_group_check=True)
                            ins.then_inc(*outs.fills(key))
                        elif what == "ot":
                            key = (steps[0][1], "ot", n)
                            b = turned.take(key)
                            pe.wait_ge(*turned.reusable(it, key))
                            pe.wait_ge(*outs.emptied(it, (steps[0][1], "o", n)))
                            for t in range(2):
                                ins = t_.transpose(b[:, t * P:(t + 1) * P], og[:, n % 2, t * P:(t + 1) * P],
                                                   ident[:])
                            ins.then_inc(*turned.fills(key))

                def from_y(name, weight):
                    key = (name, "yT")
                    b = misc.take(key)
                    pe.wait_ge(*misc.reusable(it, key))
                    if name == "x0":
                        pe.wait_ge(*s_dv.at(it, ("x0", "y")))
                    else:
                        pe.wait_ge(*turned.emptied(it, ("last", "ot", PAIR * NG - 1)))
                    for t in range(TT):
                        ins = t_.transpose(b[:, t * P:(t + 1) * P], ys[:, t], ident[:])
                    ins.then_inc(*misc.fills(key))
                    values_out(name, lambda: [(yT, weight[:], (name, "yT"))])

                pe.wait_ge(*s_in.at(it, "x"))
                attn64(0, a0_wq, None, a0_wk, None, a0_wv, a0_wo, "a0")
                to_xT("a0")
                for k, weights in (("self", (s_wq, s_wk, s_wv)), ("cross", (c_wq, c_wk, c_wv))):
                    for w in (1, 0, 2):
                        project_small(k, w, weights[w])
                attend(L0_STEPS)
                from_y("x0", p_w)
                to_xT("x0")

                def pair_transposes(key, src, n, ready):
                    b = misc.take(key)
                    pe.wait_ge(*misc.reusable(it, key))
                    pe.wait_ge(*ready)
                    settle(pe)
                    for u in range(PAIR):
                        m = src.shape[2]
                        ins = t_.transpose(b[0:m, u * SLOTS:(u + 1) * SLOTS], src[:, u], ident[0:n, 0:n])
                    ins.then_inc(*misc.fills(key))
                    pe.wait_ge(*misc.emptied(it, key))

                one(misc, ("f", "h"), lambda b: b[0:SLOTS], f_w1[:, 0, :], xT[:])
                pe.wait_ge(*misc.emptied(it, ("f", "h")))
                for t in range(TT):
                    one(outs, ("f", "lg", t), lambda b: b[:, 0:SLOTS], hT[:, t * P:(t + 1) * P], f_w2[:])
                project_small("last", 1, z_wk)
                project_small("last", 2, z_wv)
                key = ("f", "aT")
                b = misc.take(key)
                pe.wait_ge(*misc.reusable(it, key))
                pe.wait_ge(*s_dv.at(it, ("f", "alpha", TT - 1)))
                settle(pe)
                for t in range(TT):
                    ins = t_.transpose(b[0:SLOTS, t * P:(t + 1) * P], alpha[:, t], ident[:])
                ins.then_inc(*misc.fills(key))
                for u in range(PAIR):
                    key = ("f", "si", u)
                    b = outs.take(key)
                    pe.wait_ge(*outs.reusable(it, key))
                    for t in range(2):
                        ins = t_.matmul(b[0:SLOTS, 0:D + 1], alpha[:, 2 * u + t], xa[:, 2 * u + t, :],
                                        start=(t == 0), stop=(t == 1))
                    ins.then_inc(*outs.fills(key))
                pair_transposes(("f", "siT"), si, SLOTS, outs.emptied(it, ("f", "si", PAIR - 1)))
                for u in range(PAIR):
                    one(outs, ("f", "gi", u), lambda b: b[0:SLOTS, 0:3 * D], siT[:, u * SLOTS:(u + 1) * SLOTS],
                        f_wih[:])
                pair_transposes(("f", "snT"), sn, SLOTS, s_dv.at(it, ("f", "sn")))
                one(outs, ("f", "sq"), lambda b: b[0:DQ, 0:PAIR * SLOTS], f_wq[:], snT[:])
                one(outs, ("f", "sk"), lambda b: b[0:DQ, 0:PAIR * SLOTS], f_wk[:], snT[:])

                def by_pair(ring, key, rows, width, lhs, rhs, ready=None):
                    b = ring.take(key)
                    pe.wait_ge(*ring.reusable(it, key))
                    if ready is not None:
                        pe.wait_ge(*ready)
                    settle(pe)
                    for u in range(PAIR):
                        ins = t_.matmul(b[0:rows, u * width:(u + 1) * width], lhs[:, u * SLOTS:(u + 1) * SLOTS],
                                        rhs(u), start=True, stop=True)
                    ins.then_inc(*ring.fills(key))

                by_pair(outs, ("f", "sv"), SLOTS, D, snT, lambda u: f_wv[:])
                by_pair(misc, ("f", "ss"), SLOTS, SLOTS, sq, lambda u: sk[:, u * SLOTS:(u + 1) * SLOTS],
                        outs.emptied(it, ("f", "sk")))
                pair_transposes(("f", "spT"), sp_, SLOTS, misc.emptied(it, ("f", "ss")))
                by_pair(outs, ("f", "comm"), SLOTS, D, spT, lambda u: svv[:, u])
                pair_transposes(("f", "syT"), sy, SLOTS, s_dv.at(it, ("f", "sy")))
                one(outs, ("f", "svT"), lambda b: b[:, 0:PAIR * SLOTS], f_wvp[:], syT[:])
                by_pair(outs, ("f", "svo"), SLOTS, D, svT, lambda u: f_wo[:])
                key = ("y", "f0")
                y = misc.take(key)
                pe.wait_ge(*misc.reusable(it, key))
                pe.wait_ge(*outs.emptied(it, ("f", "svo")))
                pe.wait_ge(*misc.emptied(it, ("f", "aT")))
                for t in range(TT):
                    ins = t_.matmul(y[:, t * D:(t + 1) * D], alphaT[:, t * P:(t + 1) * P], svo[:, t // 2, :],
                                    start=True, stop=True)
                ins.then_inc(*misc.fills(key))
                to_xT("f0")

                attn64(1, a1_wq, a1_wqs, a1_wk, a1_wks, a1_wv, a1_wo, "a1")
                to_xT("a1")
                project_small("last", 0, z_wq)
                attend(L1_STEPS)
                from_y("x1", z_wo)
                to_xT("x1")

                for t in range(TT):
                    one(outs, ("m", "rl", t), lambda b: b[:, 0:NE], xT[:, t * P:(t + 1) * P], m_wr[:])

                def places_in_experts():
                    for t in range(TT):
                        key = ("m", "pos", t)
                        b = outs.take(key)
                        pe.wait_ge(*outs.reusable(it, key))
                        pe.wait_ge(*s_dv.at(it, ("m", "seen", t)))
                        t_.matmul(b[:, 0:NE], earlier[:], chosenb[:, t], start=True, stop=False)
                        t_.matmul(b[:, 0:NE], onesb[:], seenb[:, t], start=False, stop=True)\
                            .then_inc(*outs.fills(key))

                def expert_out(e):
                    key = ("moe", "y", e)
                    y = misc.take(key)
                    pe.wait_ge(*misc.reusable(it, key))
                    pe.wait_ge(*s_w2e[e % 2].at(it, e))
                    pe.wait_ge(*scores.emptied(it, ("moe", "h", e, FC - 1)))
                    for t in range(TT):
                        for f in range(FC):
                            ins = t_.matmul(y[:, t * D:(t + 1) * D], hid[:, e % 2, f, t * P:(t + 1) * P],
                                            w2e[:, e % 2, f], start=(f == 0), stop=(f == FC - 1))
                    ins.then_inc(*misc.fills(key))

                for e in range(NE):
                    pe.wait_ge(*s_w1e[e % 2].at(it, e))
                    for f in range(FC):
                        one(scores, ("moe", "h", e, f), lambda b: b, w1e[:, e % 2, f * P:(f + 1) * P], xT[:])
                    if e == 1:
                        places_in_experts()
                    if e >= 1:
                        expert_out(e - 1)
                expert_out(NE - 1)

        for c in closing:
            c.close()


def rotary_tables():
    inv = (np.float32(1.0) / np.float32(10000.0) ** (np.float32(2.0) * np.arange(HD // 2, dtype=np.float32)
                                                     / np.float32(HD))).astype(np.float32)
    ang = (inv[:, None] * np.arange(SEQ, dtype=np.float32)[None]).astype(np.float32)
    cos, sin = np.cos(ang).astype(np.float32), np.sin(ang).astype(np.float32)
    c = np.concatenate([cos, cos, cos, cos])
    s = np.concatenate([-sin, sin, -sin, sin])
    k = np.float32(HD ** -0.5)
    return np.stack([c * k, s * k, c, s])


def lay_out(i):
    at = np.arange(E).reshape(NH, HD // 2, 2)
    even_odd = np.concatenate([at[:, :, 0], at[:, :, 1]], 1).reshape(-1)
    odd_even = np.concatenate([at[:, :, 1], at[:, :, 0]], 1).reshape(-1)
    col = lambda a: a.reshape(-1, 1)
    row = lambda a: a.reshape(1, -1)
    chunks = lambda a, order: a[order].reshape(NC, P).T
    apart = np.arange(D).reshape(NH, DX).T.reshape(-1)
    return {
        "x": i["x"], "xT": i["x"].transpose(0, 2, 1), "ctxT": i["ctx_512"].transpose(0, 2, 1),
        "a0_wq": i["L0_attn_wq"].T, "a0_wk": i["L0_attn_wk"].T, "a0_wv": i["L0_attn_wv"].T,
        "a0_wo": i["L0_attn_wo"].T,
        "a1_wq": i["L1_attn_Wq"][:, even_odd], "a1_wqs": i["L1_attn_Wq"][:, odd_even],
        "a1_wk": i["L1_attn_Wk"][:, even_odd], "a1_wks": i["L1_attn_Wk"][:, odd_even],
        "a1_wv": i["L1_attn_Wv"], "a1_wo": i["L1_attn_Wo"],
        "a1_bq": chunks(i["L1_attn_bq"], even_odd), "a1_bqs": chunks(i["L1_attn_bq"], odd_even),
        "a1_bk": chunks(i["L1_attn_bk"], even_odd), "a1_bks": chunks(i["L1_attn_bk"], odd_even),
        "a1_bv": row(i["L1_attn_bv"]), "a1_bo": row(i["L1_attn_bo"]), "rope": rotary_tables(),
        "s_wq": i["L0_xattn_Wq"][:, apart], "s_wk": i["L0_xattn_Wk"][:, apart], "s_wv": i["L0_xattn_Wv"],
        "s_bq": col(i["L0_xattn_bq"][apart]), "s_bk": col(i["L0_xattn_bk"][apart]), "s_bv": row(i["L0_xattn_bv"]),
        "c_wq": i["L0_xattn_Wcq"][:, apart], "c_wk": i["L0_xattn_Wck"][:, apart], "c_wv": i["L0_xattn_Wcv"],
        "c_bq": col(i["L0_xattn_bcq"][apart]), "c_bk": col(i["L0_xattn_bck"][apart]), "c_bv": row(i["L0_xattn_bcv"]),
        "p_w": i["L0_xattn_Wp"], "p_b": row(i["L0_xattn_bp"]),
        "z_wq": i["L1_xattn_Wq"].T[:, apart], "z_wk": i["L1_xattn_Wkv"][:D].T[:, apart], "z_wv": i["L1_xattn_Wkv"][D:].T,
        "z_wo": i["L1_xattn_Wo"].T,
        "f_slots": i["L0_ffn_slot_init"], "f_slotsT": i["L0_ffn_slot_init"].T, "f_w1": i["L0_ffn_w1"],
        "f_b1": col(i["L0_ffn_b1"]), "f_w2": i["L0_ffn_w2"], "f_b2": row(i["L0_ffn_b2"]),
        "f_tau": row(i["L0_ffn_tau"]), "f_wihT": i["L0_ffn_Wih"].T, "f_whhT": i["L0_ffn_Whh"].T,
        "f_bih": row(i["L0_ffn_bih"]), "f_bhh": row(i["L0_ffn_bhh"]),
        "f_wq": i["L0_ffn_wq"], "f_bq": col(i["L0_ffn_bq"]), "f_wk": i["L0_ffn_wk"], "f_bk": col(i["L0_ffn_bk"]),
        "f_wv": i["L0_ffn_wv"], "f_bv": row(i["L0_ffn_bv"]), "f_lng": row(i["L0_ffn_ln_g"]),
        "f_lnb": row(i["L0_ffn_ln_b"]), "f_wvp": i["L0_ffn_wvp"], "f_bvp": col(i["L0_ffn_bvp"]),
        "f_wo": i["L0_ffn_wo"], "f_bo": row(i["L0_ffn_bo"]),
        "m_wr": i["L1_ffn_w_router"], "m_w1": i["L1_ffn_w1"], "m_w2": i["L1_ffn_w2"],
        "m_b": i["L1_ffn_bias"].reshape(1, D),
    }


def program(make_core, places):
    nc = make_core()
    dram = {n: nc.dram_tensor(f"in_{n}", s, F32, kind="ExternalInput").ap() for n, s in INPUTS.items()}
    out = nc.dram_tensor("out_0", (BATCH, SEQ, D), F32, kind="ExternalOutput").ap()
    build(nc, dram, out, places)
    return nc


def kernel(**inputs):
    import concourse.bacc as bacc
    from concourse.bass_utils import run_bass_kernel_spmd

    def make_core():
        return bacc.Bacc("TRN2", target_bir_lowering=False, num_devices=1)

    laid = lay_out({n: np.asarray(a) for n, a in inputs.items()})
    arrays = {f"in_{n}": np.ascontiguousarray(a) for n, a in laid.items()}
    places = {}
    program(make_core, places)
    nc = program(make_core, places)
    r = run_bass_kernel_spmd(nc, [arrays], core_ids=[0])
    return r.results[0]["out_0"]
```

```python
from contextlib import ExitStack

import numpy as np

import concourse.bass as bass
from concourse import mybir

F32 = mybir.dt.float32
BF16 = mybir.dt.bfloat16
ALU = mybir.AluOpType
ACT = mybir.ActivationFunctionType
AX = mybir.AxisListType

P = 128
BATCH, SEQ, D = 8, 256, 128
CTX = 64
PAIR = 2
ITERS = BATCH // PAIR
TOK = PAIR * SEQ
TT = TOK // P
NH = 16
HD = 64
E = NH * HD
NC = E // P
DX = D // NH
NG = 4
HG = NH // NG
VW = DX + 1
XATT = ("self", "cross", "last")
PARTS = 3
STACK = PARTS * PARTS * DX
MROW = STACK
ONES = MROW // 32 * 32
SLOTS, DQ, TOPK = 64, 32, 8
NE, FF, TOP = 8, 512, 2
FC = FF // P
CAPACITY = TOP * BATCH * SEQ // NE
EPS = 1e-5
MASKED = -1e30
FAR = 3e38


class Signal:

    def __init__(self, sem, places, step):
        self.sem, self.places, self.step, self.count, self.base = sem, places, step, 0, 0

    def open(self):
        self.base = 1
        return self.sem, 1

    def inc(self, key):
        self.count += 1
        self.places[key] = self.count
        return self.sem, self.step

    def at(self, it, key):
        return self.sem, (it * self.places.get("all", 1) + self.places.get(key, 1)) * self.step + self.base

    def once(self, key):
        return self.sem, self.places.get(key, 1) * self.step

    def before(self, it):
        return self.sem, it * self.places.get("all", 1) * self.step + self.base

    def close(self):
        self.places["all"] = self.count


class Ring:

    def __init__(self, tensor, full, free, places):
        self.tensor, self.full, self.free, self.places = tensor, full, free, places
        self.count = 0

    def open(self, eng):
        for sem in self.free:
            eng.sem_inc(sem, 1)

    def take(self, key):
        n, banks = self.count, len(self.full)
        self.places[key] = n
        self.count += 1
        return self.tensor[:, n % banks, :]

    def bank(self, key):
        return self.tensor[:, self.places.get(key, 0) % len(self.full), :]

    def _at(self, it, key, more):
        banks = len(self.full)
        n = self.places.get(key, 0)
        total = self.places.get("all", banks)
        each = total // banks + (n % banks < total % banks)
        return n % banks, it * each + n // banks + more

    def reusable(self, it, key):
        b, v = self._at(it, key, 1)
        return self.free[b], v

    def filled(self, it, key):
        b, v = self._at(it, key, 1)
        return self.full[b], v

    def emptied(self, it, key):
        b, v = self._at(it, key, 2)
        return self.free[b], v

    def fills(self, key):
        return self.full[self.places[key] % len(self.full)], 1

    def empties(self, key):
        return self.free[self.places.get(key, 0) % len(self.full)], 1

    def close(self):
        self.places["all"] = self.count


INPUTS = dict(
    x=(BATCH, SEQ, D), xT=(BATCH, D, SEQ), ctxT=(BATCH, CTX, SEQ),
    a0_wq=(D, E), a0_wk=(D, E), a0_wv=(D, E), a0_wo=(E, D),
    a1_wq=(D, E), a1_wqs=(D, E), a1_wk=(D, E), a1_wks=(D, E), a1_wv=(D, E), a1_wo=(E, D),
    a1_bq=(P, NC), a1_bqs=(P, NC), a1_bk=(P, NC), a1_bks=(P, NC), a1_bv=(1, E), a1_bo=(1, D),
    rope=(4, P, SEQ),
    s_wq=(D, D), s_wk=(D, D), s_wv=(D, D), s_bq=(D, 1), s_bk=(D, 1), s_bv=(1, D),
    c_wq=(D, D), c_wk=(CTX, D), c_wv=(CTX, D), c_bq=(D, 1), c_bk=(D, 1), c_bv=(1, D),
    p_w=(D, D), p_b=(1, D),
    z_wq=(D, D), z_wk=(CTX, D), z_wv=(CTX, D), z_wo=(D, D),
    f_slots=(SLOTS, D), f_slotsT=(D, SLOTS), f_w1=(2 * D, SLOTS), f_b1=(SLOTS, 1),
    f_w2=(SLOTS, SLOTS), f_b2=(1, SLOTS), f_tau=(1, 1),
    f_wihT=(D, 3 * D), f_whhT=(D, 3 * D), f_bih=(D, 3), f_bhh=(D, 3),
    f_wq=(D, DQ), f_bq=(DQ, 1), f_wk=(D, DQ), f_bk=(DQ, 1), f_wv=(D, D), f_bv=(1, D),
    f_lng=(1, D), f_lnb=(1, D), f_wvp=(D, D), f_bvp=(D, 1), f_wo=(D, D), f_bo=(1, D),
    m_wr=(D, NE), m_w1=(NE, D, FF), m_w2=(NE, FF, D), m_b=(1, D),
)


def build(nc, dram, out, places):
    with ExitStack() as ctx:
        def sb(name, shape, dt=F32):
            return ctx.enter_context(nc.sbuf_tensor(name, shape, dt))

        def psum(name, banks):
            tensor = ctx.enter_context(nc.psum_tensor(name, [P, banks, 512], F32))
            full = [ctx.enter_context(nc.semaphore(f"{name}_full{b}")) for b in range(banks)]
            free = [ctx.enter_context(nc.semaphore(f"{name}_free{b}")) for b in range(banks)]
            ring = Ring(tensor, full, free, places.setdefault(name, {}))
            closing.append(ring)
            return ring

        def signal(name, step=1):
            s = Signal(ctx.enter_context(nc.semaphore(name)), places.setdefault(name, {}), step)
            closing.append(s)
            return s

        closing = []

        loads = {}
        FIRST = ("a0_wq", "a0_wk", "a0_wv")
        SLOTW = ("f_slots", "f_w1", "f_slotsT", "f_whhT", "f_b1", "f_bih", "f_bhh", "f_tau", "f_b2")

        def weight(name, shape=None, source=None):
            t = sb("w_" + name, list(shape or dram[name].shape))
            loads[name] = (t[:], dram[name] if source is None else source)
            return t

        def across(name, parts=P):
            n = dram[name].shape[1]
            t = sb("w_" + name, [parts, n])
            loads[name] = (t[:], dram[name].to_broadcast([parts, n]))
            return t

        def chunked(name, n):
            return weight(name, [P, n, D], dram[name].rearrange("(c p) h -> p c h", p=P))

        a0_wq, a0_wk, a0_wv = weight("a0_wq"), weight("a0_wk"), weight("a0_wv")
        a0_wo = chunked("a0_wo", NC)
        s_wq, s_wk, s_wv, s_bq, s_bk, s_bv = (weight("s_wq"), weight("s_wk"), weight("s_wv"),
                                              weight("s_bq"), weight("s_bk"), across("s_bv"))
        c_wq, c_wk, c_wv, c_bq, c_bk, c_bv = (weight("c_wq"), weight("c_wk"), weight("c_wv"),
                                              weight("c_bq"), weight("c_bk"), across("c_bv"))
        p_w, p_b = weight("p_w"), across("p_b")
        f_slots, f_slotsT = weight("f_slots"), weight("f_slotsT")
        f_w1 = weight("f_w1", [P, 2, SLOTS], dram["f_w1"].rearrange("(c p) h -> p c h", p=P))
        f_b1, f_b2, f_w2, f_tau = weight("f_b1"), across("f_b2"), weight("f_w2"), across("f_tau")
        f_wih, f_whh = weight("f_wihT"), weight("f_whhT")
        f_bih, f_bhh = weight("f_bih"), weight("f_bhh")
        f_wq, f_bq, f_wk, f_bk = weight("f_wq"), weight("f_bq"), weight("f_wk"), weight("f_bk")
        f_wv, f_bv = weight("f_wv"), across("f_bv", SLOTS)
        f_lng, f_lnb = across("f_lng", SLOTS), across("f_lnb", SLOTS)
        f_wvp, f_bvp, f_wo, f_bo = weight("f_wvp"), weight("f_bvp"), weight("f_wo"), across("f_bo")
        a1_wq, a1_wqs, a1_wk, a1_wks = (weight("a1_wq"), weight("a1_wqs"), weight("a1_wk"),
                                        weight("a1_wks"))
        a1_wv, a1_wo = weight("a1_wv"), chunked("a1_wo", NC)
        a1_bq, a1_bqs, a1_bk, a1_bks = (weight("a1_bq"), weight("a1_bqs"), weight("a1_bk"),
                                        weight("a1_bks"))
        a1_bv, a1_bo = across("a1_bv"), across("a1_bo")
        rope = weight("rope", [P, 4, SEQ], dram["rope"].rearrange("a p n -> p a n"))
        z_wq, z_wk, z_wv, z_wo = weight("z_wq"), weight("z_wk"), weight("z_wv"), weight("z_wo")
        m_wr, m_b = weight("m_wr"), across("m_b")

        ident = sb("ident", [P, P])
        identb = sb("identb", [P, P], BF16)
        ones = sb("ones", [P, P])
        onesb = sb("onesb", [P, P], BF16)
        mask = sb("mask", [P, P], BF16)
        maskT = sb("maskT", [P, P], BF16)
        earlier = sb("earlier", [P, P], BF16)
        head_rows = sb("head_rows", [PARTS * 32, NC, P], BF16)

        xa = sb("xa", [P, TT, D + 1])
        xb = sb("xb", [P, TT, D])
        xT = sb("xT", [P, TOK])
        ctxT = sb("ctxT", [CTX, TOK])
        stats = sb("stats", [P, TT, 6])
        mv = sb("mv", [P, TT, 2])
        ve = sb("ve", [P, TT])
        rstd = sb("rstd", [P, TT])
        half = sb("half", [P, TT])

        hostA = sb("hostA", [P, NC, TOK])
        hostB = sb("hostB", [P, NC, TOK])
        QK = 2 * 2 * SEQ
        qk = hostA[:].rearrange("p a b -> p (a b)")[:, 0:QK].rearrange("p (s w n) -> p s w n", s=2, w=2)
        vv = sb("vv", [P, TT, E])
        oT = sb("oT", [P, PAIR, NC, SEQ])
        NPR = 3
        probs = sb("probs", [P, NPR, 3 * P])
        probsT = sb("probsT", [P, 4, 3 * P])
        nmax = sb("nmax", [P, 4, 2])
        sums = sb("sums", [P, TT, NH])
        rsum = sb("rsum", [P, TT, NH])
        rrest = sb("rrest", [P, TT, NH])
        rparts = sb("rparts", [P, TT, PARTS, 32], BF16)
        rot = sb("rot", [P, 2, 2, TOK])

        def over(host, rows, shape, dt=F32, phase="small heads"):
            n = int(np.prod(shape)) // (2 if dt == BF16 else 1)
            at = taken.setdefault((host.name, phase), QK if host is hostA else 0)
            taken[host.name, phase] = at + n
            flat_host = host[:].rearrange("p a b -> p (a b)" if len(host.shape) == 3 else "p a b c -> p (a b c)")
            assert at + n <= flat_host.shape[1]
            v = flat_host[0:rows, at:at + n]
            v = v.bitcast(BF16) if dt == BF16 else v
            if len(shape) == 1:
                return v
            names = "abc"[:len(shape)]
            return v.rearrange(f"p ({' '.join(names)}) -> p {' '.join(names)}",
                               **dict(zip(names[1:], shape[1:])))

        taken = {}
        rT = sb("rT", [PARTS * 32, SEQ], BF16)

        rows16 = lambda flat_host: flat_host.bitcast(BF16).rearrange("p (u h n) -> p u h n", u=PAIR, h=NH)
        qs_ = sb("qs", [P, PAIR, NH, SEQ], BF16)
        ks_ = sb("ks", [P, PAIR, NH, SEQ], BF16)
        stacks = {"self": (qs_[:], ks_[:]), "cross": (rows16(hostB[:].rearrange("p a b -> p (a b)")),
                                                rows16(oT[:].rearrange("p u c n -> p (u c n)"))), "last": (qs_[:], ks_[:])}
        PIECES = {"self": ("self", (0, 1)), "cross": ("cross", (0, 1)),
                  "last keys": ("last", (1,)), "last queries": ("last", (0,))}
        flat, rest, part = {}, {}, {}
        for name, (k, holds) in PIECES.items():
            for u in range(PAIR):
                host = {"cross": hostA, "last keys": hostB}.get(name, vv)
                phase = "pieces" if name in ("self", "cross") else name
                if name == "cross":
                    taken.pop((host.name, phase), None)
                if name == "last keys":
                    taken.setdefault((host.name, phase), SEQ)
                if host is vv:
                    taken[host.name, phase] = u * (TT // PAIR) * E
                flat[name, u] = over(host, P, [len(holds), SEQ], phase=phase)
                rest[name, u] = over(host, P, [len(holds), SEQ], phase=phase)
                part[name, u] = over(host, P, [PARTS, len(holds), SEQ], BF16, phase=phase)
        VA = NH * VW + 32 - VW
        vas = [sb(f"va{i}", [P, TT, VA]) for i in range(2)]
        nms = [sb(f"nm{i}", [P, TT, NH]) for i in range(2)]
        va = {"self": vas[0], "cross": vas[1], "last": vas[0]}
        nm = {"self": nms[0], "cross": nms[1], "last": nms[0]}
        nmf = over(rot, NH, [SEQ], phase="small heads")
        nmr = over(rot, NH, [SEQ], phase="small heads")
        nmp = over(rot, NH, [PARTS, SEQ], BF16, phase="small heads")
        NPX = 8
        px = vv[:].rearrange("p a b -> p (a b)").rearrange("p (s n) -> p s n", s=NPX)
        og = over(rot, P, [2, SEQ], phase="small heads")
        den = sb("den", [P, NG, TT, HG])
        ys = over(rot, P, [TT, D], phase="small heads")
        taken["hostA", "sums"] = NC * TOK - TT * D
        yc = over(hostA, P, [TT, D], phase="sums")
        yTu = []
        for u in range(PAIR):
            taken["hostB", "yTu"] = u * NC * TOK // PAIR
            yTu.append(over(hostB, P, [SEQ], phase="yTu"))

        c1 = sb("c1", [SLOTS, 1])
        smean = sb("smean", [P, 1])
        itau = sb("itau", [P, 1])
        crz = sb("crz", [P, 2 * SLOTS])
        ghn = sb("ghn", [P, SLOTS])
        top = sb("top", [P, TT, 8])
        ntop = sb("ntop", [P, TT])
        asum = sb("asum", [P, TT])
        arec = sb("arec", [P, TT])
        sq = sb("sq", [DQ, SLOTS])
        sk = sb("sk", [DQ, SLOTS])
        sm = sb("sm", [SLOTS, PAIR, 4])
        sst = sb("sst", [SLOTS, PAIR, 6])
        smv = sb("smv", [SLOTS, PAIR, 2])
        srs = sb("srs", [SLOTS, PAIR, 2])
        slot = lambda rows, shape, phase="slots": over(hostA, rows, shape, phase=phase)
        hT = slot(SLOTS, [SEQ])
        ex = slot(P, [2, 2, SLOTS], "slots again")
        lg = slot(P, [2, 2, SLOTS])
        alphaT = slot(SLOTS, [SEQ], "slots again")
        alpha = slot(P, [2, SLOTS])
        dnr, siT = slot(P, [SLOTS]), slot(P, [SLOTS])
        rz, npre, gn, snT = slot(P, [2 * SLOTS]), slot(P, [SLOTS]), slot(P, [SLOTS]), slot(P, [SLOTS])
        svv, sp_, spT = slot(SLOTS, [D]), slot(SLOTS, [SLOTS]), slot(SLOTS, [SLOTS])
        sy, syT = slot(SLOTS, [D]), slot(P, [SLOTS])
        svT, svo = slot(P, [SLOTS]), slot(SLOTS, [D])
        assert taken["hostA", "slots"] <= taken["hostA", "sums"] - TT * D

        hid = oT[:].rearrange("p u c n -> p (u c n)").rearrange("p (s f n) -> p s f n", s=2, f=FC)
        w1e = rot[:, 0].rearrange("p a n -> p (a n)").rearrange("p (s n) -> p s n", s=2)
        w2e = rot[:, 1].rearrange("p a n -> p (a n)").rearrange("p (s f n) -> p s f n", s=2, f=FC)
        RW = NE + 8 - TOP
        rl = sb("rl", [P, TT, 2, RW])
        rtop = sb("rtop", [P, TT, 8])
        rtwo = sb("rtwo", [P, TT, 8])
        nrt = sb("nrt", [P, TT])
        rex = sb("rex", [P, TT, 2, NE])
        rden = sb("rden", [P, TT])
        rrec = sb("rrec", [P, TT])
        chosen = sb("chosen", [P, TT, NE])
        chosenb = sb("chosenb", [P, TT, NE], BF16)
        seen = sb("seen", [P, TT + 1, NE])
        seenb = sb("seenb", [P, TT, NE], BF16)
        fits = sb("fits", [P, TT, NE])
        wexp = sb("wexp", [P, TT, NE])
        wgt = sb("wgt", [P, TT, NE])
        taken["hostB", "experts"] = (NC - 1) * TOK
        acc = over(hostB, P, [TT, D], phase="experts")

        scores = psum("scores", 3)
        turned = psum("turned", 2)
        outs = psum("outs", 1)
        misc = psum("misc", 2)

        s_first = signal("first_weights_loaded", 16)
        s_slotw = signal("slot_weights_loaded", 16)
        s_load = signal("weights_loaded", 16)
        s_rest = signal("later_weights_loaded", 16)
        s_const = signal("constants_made")
        s_late = signal("later_constants_made")
        s_fill = signal("fills_made")
        s_in = signal("x_rows_loaded", 16)
        s_inT = signal("x_columns_loaded", 16)
        s_xread = signal("x_columns_read")
        s_normed = signal("y_made")
        s_out = signal("y_stored", 16)
        s_split = {(k, u, w): signal(f"parts_stored_{k}{u}{w}", 16)
                   for k in XATT for u in range(PAIR) for w in range(2)}
        s_stack = {(k, u): signal(f"parts_stacked_{k}{u}", 16) for k in XATT for u in range(PAIR)}
        s_mrow = {(k, u): signal(f"maxima_placed_{k}{u}", 16) for k in XATT for u in range(PAIR)}
        s_w1e = [signal(f"expert_w1_loaded{b}", 16) for b in range(2)]
        s_w2e = [signal(f"expert_w2_loaded{b}", 16) for b in range(2)]
        s_dv = signal("vector_made")
        s_ac = signal("scalar_made")
        s_po = signal("pool_made")
        pre = signal("slot_terms_summed")
        pred = signal("slot_terms_made")
        passed = ctx.enter_context(nc.semaphore("passed"))
        parts_d = {(k, u, w): nc.dram_tensor(f"parts_{k}{u}{w}", (PARTS,) * (w + 1) + (P, SEQ), BF16,
                                             kind="Internal").ap()
                   for k in XATT for u in range(PAIR) for w in range(2)}

        block = ctx.enter_context(nc.Block())
        def settle(eng):
            eng.sem_inc(passed, 1)

        SCALE = {"self": DX ** -0.5, "cross": DX ** -0.5, "last": DX ** -0.5}

        def units():
            for u in range(PAIR):
                for c in range(NC):
                    for r in range(2):
                        yield c, u, r

        order = list(units())

        def tiles(name):
            return slice(2 * name[1], 2 * name[1] + 2) if isinstance(name, tuple) else slice(0, TT)

        def tokens(name):
            return slice(tiles(name).start * P, tiles(name).stop * P)

        def count(sl):
            return range(sl.start, sl.stop)

        def piece_steps(name, u):
            return [("piece", name, u, what) for what in ("project", "high", "mid")]

        def tail_steps(L, u):
            whats = ["sums", "rT"] + [("R", j) for j in range(NC // 2)] + ["out", "sum", "norm", "xT"]
            return [("tail", L, u, what) for what in whats] + piece_steps(("self", "last queries")[L], u)

        VALUES_FROM = NH // 2, NH - 2

        def later_values(L, i):
            n = i - VALUES_FROM[L]
            return [(TT // 2 + n // 2, n % 2)] if 0 <= n < TT else []

        TAIL_FROM = PAIR * NH // 2 + 4

        def slot_steps(u):
            return [("slots", 0, u, what) for what in (
                "ysum", "yT", "y", "sum", "norm", "xT", "h", "lg", "ex", "si", "gi", "gn",
                "qkv", "ss", "sp", "spT", "comm", "sy", "syT", "svT", "svo", "yf", "fsum", "fnorm", "fxT")]

        def schedule(L):
            by_unit = {TAIL_FROM + i: [step] for i, step in enumerate(tail_steps(L, 0))}
            if L == 1:
                slots = slot_steps(1)[SLOTS_BEFORE:]
                for n, step in enumerate(slots):
                    by_unit.setdefault(n // SLOTS_PER_UNIT, []).append(step)
                assert (len(slots) - 1) // SLOTS_PER_UNIT < NH - 2
                for u in range(PAIR):
                    for n, step in enumerate(piece_steps("last keys", u)):
                        by_unit.setdefault(NH - 2 + 3 * u + n, []).append(step)
            n = PAIR * NH + 1
            by_unit[n] = [step for i in sorted(by_unit) if i >= n for step in by_unit[i]]
            return by_unit

        SLOTS_BEFORE = 4
        SLOTS_PER_UNIT = 2
        WOVEN = schedule(0), schedule(1)

        def woven(L, i, middle=False):
            steps = WOVEN[L].get(i, [])
            n = len(steps) // 2 if i < NH else 0
            return steps[:n] if middle else steps[n:]

        def small_heads(L, ks, others, later={}):
            first = [(k, u, h) for u in range(PAIR) for k in ks for h in range(NH)]
            second = list(first)
            steps, done = [], 0

            def one_second():
                nonlocal done
                k, u, h = second[done]
                steps.append(("p2", k, u, h, done))
                groups()
                steps.extend(("do", step, 0, 0, 0) for step in later.get(done, ()))
                done += 1

            def groups():
                for what, lag in LAGS:
                    if done >= lag and (done - lag) % HG == 0 and (done - lag) // HG < len(second) // HG:
                        steps.append(group(what, (done - lag) // HG))

            def group(what, n):
                k, u, h = second[n * HG]
                return what, k, u, h // HG, n

            steps = [("do", step, 0, 0, 0) for step in others.pop(0)]
            for i, (k, u, h) in enumerate(first):
                steps += [("do", step, 0, 0, 0) for step in others.pop(i, ())]
                steps.append(("p1", k, u, h, i))
                if i >= NH and i % NH == MAXIMA_AFTER:
                    steps.append(("nm",) + first[i - NH][:2] + (0, 0))
                if done < len(second) and i >= NH * (done // NH + 1) + (SECOND_AFTER, L1_SECOND_AFTER)[L]:
                    one_second()
            assert not others
            steps.append(("nm",) + first[-1][:2] + (0, 0))
            while done < len(second):
                one_second()
            while done <= len(second) - HG + LAGS[-1][1]:
                groups()
                done += 1
            return steps

        EARLY = 9
        LAGS = ("av", 5), ("og", 6), ("ot", 8)
        MAXIMA_AFTER = 1
        L1_SECOND_AFTER = 10
        SECOND_AFTER = 12
        CROSS_AT = NH + 5
        SLOTS_AT = 2 * NH + 5

        def along(steps):
            return {0: steps[:EARLY]} | {1 + i: [step] for i, step in enumerate(steps[EARLY:])}

        beginning = along(tail_steps(0, 1))
        beginning[0] = piece_steps("cross", 0) + beginning[0]
        L0_STEPS = small_heads(0, ("self", "cross"), beginning | {
            CROSS_AT + i: [step] for i, step in enumerate(piece_steps("cross", 1))},
            {SLOTS_AT + i: [step] for i, step in enumerate(slot_steps(0))})
        assert SLOTS_AT + len(slot_steps(0)) <= 2 * PAIR * NH
        L0_STEPS += [("do", step, 0, 0, 0) for step in slot_steps(1)[:SLOTS_BEFORE]]
        X1 = ("yT", "y", "sum", "norm", "xT")
        X1_AT = NH + 5
        L1_STEPS = small_heads(1, ("last",), along(tail_steps(1, 1)),
                               {X1_AT + i: [("x1", 1, 0, what)] for i, what in enumerate(X1)})
        L1_STEPS += [("do", ("x1", 1, 1, what), 0, 0, 0) for what in X1]

        @block.sync
        def _(sync):
            for sig in (s_xread, s_normed, s_mrow["last", PAIR - 1], s_split["last", 0, 1], s_split["last", 1, 1]):
                sync.sem_inc(*sig.open())
            for name in FIRST:
                sync.dma_start(*loads[name]).then_inc(*s_first.inc("w"))
            with sync.Fori(0, ITERS) as it:
                def store_and_stack(name, u):
                    k, holds = PIECES[name]
                    sync.wait_ge(*s_po.at(it, (name, u, "low")))
                    for n, w in enumerate(holds):
                        mine, there = part[name, u][:, :, n], parts_d[k, u, w]
                        if w == 0:
                            sync.dma_start(there.rearrange("i p n -> p i n"), mine)\
                                .then_inc(*s_split[k, u, w].inc("store"))
                        else:
                            for i in range(PARTS):
                                sync.dma_start(there[:, i].rearrange("j p n -> p j n"), mine)\
                                    .then_inc(*s_split[k, u, w].inc("store"))
                    for w in holds:
                        there, stack = parts_d[k, u, w], stacks[k][w]
                        sync.wait_ge(*s_split[k, u, w].at(it, "store"))
                        if w == 0:
                            for j in range(PARTS):
                                sync.dma_start(stack[PARTS * DX * j:PARTS * DX * (j + 1), u],
                                               there.rearrange("i (d h) n -> (i d) h n", d=DX))\
                                    .then_inc(*s_stack[k, u].inc(w))
                        else:
                            sync.dma_start(stack[0:STACK, u],
                                           there.rearrange("j i (d h) n -> (j i d) h n", d=DX))\
                                .then_inc(*s_stack[k, u].inc(w))
                    if k == "cross":
                        sync.dma_start(stacks[k][1][MROW:MROW + PARTS, u], ks_[MROW:MROW + PARTS, u])\
                            .then_inc(*s_stack[k, u].inc("ones"))

                def other(step):
                    if step[0] == "piece" and step[3] == "mid":
                        store_and_stack(step[1], step[2])

                def place_maxima(steps):
                    for what, k, u, _, _ in steps:
                        if what == "do":
                            other(k)
                        elif what == "nm":
                            sync.wait_ge(*s_dv.at(it, (k, u, "nmlow")))
                            for i in range(PARTS):
                                sync.dma_start(stacks[k][0][MROW + i:MROW + i + 1, u], nmp[:, i, :])\
                                    .then_inc(*s_mrow[k, u].inc("maxima"))

                sync.wait_ge(*s_xread.before(it))
                settle(sync)
                pair = bass.ds(it * PAIR, PAIR)
                sync.dma_start(xT[:].rearrange("p (b n) -> p b n", b=PAIR),
                               dram["xT"][pair].rearrange("b p n -> p b n")).then_inc(*s_inT.inc("x"))
                sync.dma_start(ctxT[:].rearrange("p (b n) -> p b n", b=PAIR),
                               dram["ctxT"][pair].rearrange("b p n -> p b n")).then_inc(*s_inT.inc("x"))
                sync.wait_ge(*s_normed.before(it))
                settle(sync)
                for u in range(PAIR):
                    sync.dma_start(xb[:, 2 * u:2 * u + 2],
                                   dram["x"][bass.ds(it * PAIR + u, 1)].rearrange("b (t p) d -> p (b t) d", p=P))\
                        .then_inc(*s_in.inc("x"))
                sync.wait_ge(*s_late.once("c"))
                for L, steps in enumerate((L0_STEPS, L1_STEPS)):
                    for i in range(PAIR * NH + 2):
                        for step in woven(L, i, middle=True) + woven(L, i):
                            other(step)
                    place_maxima(steps)
                sync.wait_ge(*misc.filled(it, ("x1T", PAIR - 1)))
                settle(sync)
                for e in range(NE):
                    if e >= 2:
                        sync.wait_ge(*scores.filled(it, ("moe", "h", e - 2, FC - 1)))
                        settle(sync)
                    sync.dma_start(w1e[:, e % 2], dram["m_w1"][e]).then_inc(*s_w1e[e % 2].inc(e))
                    if e >= 2:
                        sync.wait_ge(*misc.filled(it, ("moe", "y", e - 2)))
                    sync.dma_start(w2e[:, e % 2], dram["m_w2"][e].rearrange("(c p) h -> p c h", p=P))\
                        .then_inc(*s_w2e[e % 2].inc(e))
            sync.wait_ge(*s_out.before(ITERS))

        @block.gpsimd
        def _(pool):
            g = nc.gpsimd
            fills = [(ident, 0.0), (identb, 0.0), (ones, 1.0), (onesb, 1.0), (mask, 0.0), (maskT, 0.0),
                     (earlier, 1.0), (head_rows, 1.0), (half, -0.5), (xa, 1.0), (vas[0], 1.0), (vas[1], 1.0), (seen, 0.0), (rtwo, FAR), (rl, FAR), (rparts, 0.0)]
            for t, v in fills:
                g.memset(t[:], v).then_inc(*s_fill.inc("fill"))
            pool.wait_ge(s_fill.sem, len(fills))
            for t in (ident, identb):
                g.affine_select(out=t[:], in_=t[:], compare_op=ALU.not_equal, fill=1.0, base=0,
                                pattern=[[-1, P]], channel_multiplier=1).then_inc(*s_const.inc("c"))
            g.affine_select(out=mask[:], in_=mask[:], compare_op=ALU.is_ge, fill=MASKED, base=0,
                            pattern=[[-1, P]], channel_multiplier=1).then_inc(*s_const.inc("c"))
            g.affine_select(out=maskT[:], in_=maskT[:], compare_op=ALU.is_ge, fill=MASKED, base=0,
                            pattern=[[1, P]], channel_multiplier=-1).then_inc(*s_const.inc("c"))
            g.affine_select(out=earlier[:], in_=earlier[:], compare_op=ALU.is_gt, fill=0.0, base=0,
                            pattern=[[1, P]], channel_multiplier=-1).then_inc(*s_const.inc("c"))
            hr = head_rows[0:32]
            g.affine_select(out=hr, in_=hr, compare_op=ALU.is_ge, fill=0.0, base=0,
                            pattern=[[P, NC], [1, P]], channel_multiplier=-HD).then_inc(*s_const.inc("c"))
            pool.wait_ge(*s_const.once("c"))
            g.affine_select(out=hr, in_=hr, compare_op=ALU.is_gt, fill=0.0, base=HD,
                            pattern=[[-P, NC], [-1, P]], channel_multiplier=HD).then_inc(*s_const.inc("c"))
            pool.wait_ge(*s_const.once("c"))
            for i in range(1, PARTS):
                g.tensor_copy(head_rows[32 * i:32 * i + 32], hr).then_inc(*s_late.inc("c"))
            g.memset(ks_[ONES:ONES + 32], 1.0).then_inc(*s_late.inc("c"))
            others = [name for name in loads if name not in FIRST + SLOTW]
            soon = [name for name in others if name[:3] in ("a0_", "s_w", "s_b", "c_w", "c_b", "p_w", "p_b")]
            for name in soon:
                pool.dma_start(*loads[name]).then_inc(*s_load.inc("w"))
            for name in others:
                if name not in soon:
                    pool.dma_start(*loads[name]).then_inc(*s_rest.inc("w"))
            pool.wait_ge(*s_load.once("w"))

            with pool.Fori(0, ITERS) as it:
                def add_bias(name, bias, before):
                    ts = tiles(name)
                    pool.wait_ge(*s_dv.at(it, ("ln", before, "x")))
                    if bias is None:
                        settle(pool)
                        g.tensor_copy(xb[:, ts], xa[:, ts, 0:D]).then_inc(*s_po.inc(("xb", name)))
                    else:
                        g.tensor_tensor(out=xb[:, ts], in0=xa[:, ts, 0:D],
                                        in1=bias[:].unsqueeze(1).to_broadcast([P, ts.stop - ts.start, D]),
                                        op=ALU.add).then_inc(*s_po.inc(("xb", name)))

                def rsqrt(name, dst, src, exponent):
                    pool.wait_ge(*s_dv.at(it, (name, "ve")))
                    g.tensor_tensor(out=dst, in0=src, in1=exponent, op=ALU.pow)\
                        .then_inc(*s_po.inc((name, "rstd")))

                def norm(name):
                    ts = tiles(name)
                    rsqrt(("ln", name), rstd[:, ts], ve[:, ts], half[:, ts])

                def split(name, u):
                    f, rs, p = flat[name, u], rest[name, u], part[name, u]
                    pool.wait_ge(*s_ac.at(it, (name, u, "high")))
                    g.tensor_tensor(out=rs[:], in0=f[:], in1=p[:, 0], op=ALU.subtract)\
                        .then_inc(*s_po.inc((name, u, "rest")))
                    pool.wait_ge(*s_ac.at(it, (name, u, "mid")))
                    g.tensor_tensor(out=p[:, 2], in0=rs[:], in1=p[:, 1], op=ALU.subtract)\
                        .then_inc(*s_po.inc((name, u, "low")))

                def other(step):
                    kind, L, u, what = step
                    if kind == "piece" and what == "mid":
                        split(L, u)
                    elif kind == "tail" and what == "sum":
                        norm((f"a{L}", u))
                    elif kind == "tail" and what == "norm":
                        add_bias((f"x{L}", u), (p_b, None)[L], (f"a{L}", u))
                    elif kind == "x1" and what == "sum":
                        norm(("x1", u))
                    elif kind == "x1" and what == "norm":
                        add_bias(("moe", u), m_b, ("x1", u))
                    elif kind == "slots" and what == "sum":
                        norm(("x0", u))
                    elif kind == "slots" and what == "norm":
                        pool.wait_ge(*s_rest.once("w"))
                        add_bias(("f0", u), f_bo, ("x0", u))
                    elif kind == "slots" and what == "comm":
                        rsqrt(("ln", "slots", u), srs[:, u, 1:2], srs[:, u, 0:1], half[0:SLOTS, 0:1])
                    elif kind == "slots" and what == "fsum":
                        norm(("f0", u))
                    elif kind == "slots" and what == "fnorm":
                        add_bias(("a1", u), a1_bo, ("f0", u))

                def rotate(u, c):
                    place = (u * NC + c) % 2
                    for j in range(2):
                        pool.wait_ge(*misc.emptied(it, (1, "qk", u, c, j)))
                    g.tensor_tensor(out=qk[:, place], in0=rot[:, place, 0].rearrange("p (w n) -> p w n", w=2),
                                    in1=rot[:, place, 1].rearrange("p (w n) -> p w n", w=2),
                                    op=ALU.add).then_inc(*s_po.inc(("qk1", u, c)))

                for L, steps in enumerate((L0_STEPS, L1_STEPS)):
                    if L == 1:
                        rotate(0, 0)
                    for i in range(PAIR * NH + 2):
                        if L == 1 and i % 2 == 0 and i + 2 < len(order):
                            rotate(*order[i + 2][1::-1])
                        for step in woven(L, i, middle=True) + woven(L, i):
                            other(step)
                    for what, step, _, _, _ in steps:
                        if what == "do":
                            other(step)
                norm("moe")
                pool.wait_ge(*s_normed.at(it, "y"))
                settle(pool)
                for u in range(PAIR):
                    pool.dma_start(out[bass.ds(it * PAIR + u, 1)].rearrange("b (t p) d -> p (b t) d", p=P),
                                   xa[:, 2 * u:2 * u + 2, 0:D]).then_inc(*s_out.inc("y"))
                pool.wait_ge(*s_out.at(it, "y"))
                settle(pool)

        @block.scalar
        def _(act):
            a = nc.scalar
            for name in SLOTW:
                act.dma_start(*loads[name]).then_inc(*s_slotw.inc("w"))
            act.wait_ge(*s_const.once("c"))
            with act.Fori(0, ITERS) as it:
                def attn64(L):
                    def project(u, c):
                        if L == 0:
                            key = (L, "qk", u, c, 0)
                            act.wait_ge(*misc.filled(it, key))
                            for w, sc in enumerate((HD ** -0.5, 1.0)):
                                ins = a.activation(qk[:, (u * NC + c) % 2, w],
                                                   misc.bank(key)[:, w * SEQ:(w + 1) * SEQ], ACT.Copy, scale=sc)
                            ins.then_inc(*misc.empties(key))
                    project(0, 0)
                    for i, (c, u, r) in enumerate(units()):
                        if i % 2 == 0 and i + 2 < len(order):
                            project(*order[i + 2][1::-1])
                        key = (L, "s", c, u, r)
                        h = 2 * c + r
                        if i >= 5 and i % 2 == 1:
                            out_copy(L, (i - 5) // 2)
                        for step in woven(L, i, middle=True):
                            other(step)
                        act.wait_ge(*s_dv.at(it, (L, "max", c, u, r)))
                        if i >= NPR:
                            act.wait_ge(*turned.filled(it, (L, "t", *order[i - NPR])))
                        s = scores.bank(key)
                        for t, (lo, hi) in enumerate(((0, P), (P, 3 * P))):
                            ins = a.activation(probs[:, i % NPR, lo:hi], s[:, lo:hi], ACT.Exp,
                                               bias=nmax[:, i % 4, t:t + 1],
                                               accum_out=sums[:, 2 * u + t, h:h + 1])
                        ins.then_inc(*scores.empties(key))
                        if i >= 2 and (i - 2) % 4 == 3:
                            turn_copy(L, i - 2)
                        for step in woven(L, i):
                            other(step)
                    n = len(order)
                    for step in woven(L, n):
                        other(step)
                    out_copy(L, n // 2 - 2)
                    turn_copy(L, n - 1)
                    for step in woven(L, n + 1):
                        other(step)
                    out_copy(L, n // 2 - 1)

                def other(step):
                    kind, L, u, what = step
                    if kind == "piece":
                        split(L, u, what)
                    elif kind == "x1":
                        if what == "yT":
                            turned_copy(yTu[u], ("x1T", u), P)
                        elif what == "xT":
                            to_xT(("x1", u))
                    elif kind == "slots":
                        slots(u, what)
                    elif what == "rT":
                        act.wait_ge(*misc.filled(it, (L, "rT", u)))
                        a.activation(rT[:], misc.bank((L, "rT", u))[0:PARTS * 32, 0:SEQ], ACT.Copy)\
                            .then_inc(*misc.empties((L, "rT", u)))
                    elif what == "xT":
                        to_xT((f"a{L}", u))

                def turn_copy(L, i):
                    c, u, r = order[i]
                    act.wait_ge(*turned.filled(it, (L, "t", c, u, r)))
                    if i >= 4:
                        act.wait_ge(*outs.filled(it, (L, "o", *order[i - 4][:2])))
                    a.activation(probsT[:, i % 4], turned.bank((L, "t", c, u, r))[:, 0:3 * P], ACT.Copy)\
                        .then_inc(*turned.empties((L, "t", c, u, r)))

                def out_copy(L, j):
                    c, u = order[2 * j][:2]
                    act.wait_ge(*outs.filled(it, (L, "o", c, u)))
                    a.activation(oT[:, u, c], outs.bank((L, "o", c, u))[:, 0:SEQ], ACT.Copy)\
                        .then_inc(*outs.empties((L, "o", c, u)))

                def to_xT(name):
                    act.wait_ge(*misc.filled(it, ("xT", name)))
                    ts = tokens(name)
                    a.activation(xT[:, ts], misc.bank(("xT", name))[:, 0:ts.stop - ts.start], ACT.Copy)\
                        .then_inc(*misc.empties(("xT", name)))

                def split(name, u, what):
                    if what == "high":
                        act.wait_ge(*misc.emptied(it, (name, u)))
                        a.activation(part[name, u][:, 0], flat[name, u][:], ACT.Copy)\
                            .then_inc(*s_ac.inc((name, u, "high")))
                    elif what == "mid":
                        act.wait_ge(*s_po.at(it, (name, u, "rest")))
                        a.activation(part[name, u][:, 1], rest[name, u][:], ACT.Copy)\
                            .then_inc(*s_ac.inc((name, u, "mid")))

                def attend(steps):
                    for what, k, u, h, n in steps:
                        if what == "do":
                            other(k)
                        elif what == "nm":
                            act.wait_ge(*misc.filled(it, (k, u, "nmT")))
                            a.activation(nmf[:], misc.bank((k, u, "nmT"))[0:NH, 0:SEQ], ACT.Copy)\
                                .then_inc(*misc.empties((k, u, "nmT")))
                        elif what == "p2":
                            key = (k, "st", u, h)
                            width = 3 * P if k == "self" else 2 * SEQ
                            act.wait_ge(*scores.filled(it, key))
                            if n >= NPX:
                                act.wait_ge(*outs.filled(it, (len(steps), "o", (n - NPX) // HG)))
                            a.activation(px[:, n % NPX, 0:width], scores.bank(key)[:, 0:width], ACT.Exp)\
                                .then_inc(*scores.empties(key))
                        elif what == "og":
                            key = (len(steps), "o", n)
                            act.wait_ge(*outs.filled(it, key))
                            if n >= 2:
                                act.wait_ge(*turned.filled(it, (len(steps), "ot", n - 2)))
                            a.activation(og[:, n % 2, 0:SEQ], outs.bank(key)[:, 0:SEQ], ACT.Copy)\
                                .then_inc(*outs.empties(key))

                def turned_copy(dst, key, rows):
                    act.wait_ge(*misc.filled(it, key))
                    a.activation(dst[:], misc.bank(key)[0:rows, 0:dst.shape[1]], ACT.Copy).then_inc(*misc.empties(key))

                def slots(u, what):
                    if what == "yT":
                        turned_copy(yTu[u], ("yT", u), P)
                    elif what == "xT":
                        to_xT(("x0", u))
                    elif what == "h":
                        act.wait_ge(*s_rest.once("w"))
                        act.wait_ge(*misc.filled(it, ("f", "h", u)))
                        a.activation(hT[:], misc.bank(("f", "h", u))[0:SLOTS, 0:SEQ], ACT.Gelu, bias=c1[:, 0:1])\
                            .then_inc(*misc.empties(("f", "h", u)))
                    elif what == "ex":
                        for t in range(2):
                            act.wait_ge(*s_dv.at(it, ("f", "struck", u, t)))
                            a.activation(ex[:, t], lg[:, t], ACT.Exp, bias=ntop[:, 2 * u + t:2 * u + t + 1])\
                                .then_inc(*s_ac.inc(("f", "ex", u, t)))
                    elif what == "si":
                        turned_copy(alphaT, ("f", "aT", u), SLOTS)
                    elif what == "gi":
                        act.wait_ge(*misc.filled(it, ("f", "gi", u)))
                        a.activation(rz[:], misc.bank(("f", "gi", u))[:, 0:2 * SLOTS], ACT.Tanh, scale=0.5)\
                            .then_inc(*s_ac.inc(("f", "ge", u)))
                    elif what == "gn":
                        act.wait_ge(*misc.emptied(it, ("f", "gi", u)))
                        a.activation(gn[:], npre[:], ACT.Tanh, bias=f_bih[:, 2:3]).then_inc(*s_ac.inc(("f", "gn", u)))
                    elif what == "sp":
                        act.wait_ge(*s_dv.at(it, ("f", "smax", u)))
                        a.activation(sp_[:], misc.bank(("f", "ss", u))[0:SLOTS, 0:SLOTS], ACT.Exp,
                                     bias=sm[:, u, 1:2], scale=DQ ** -0.5,
                                     accum_out=sm[:, u, 2:3]).then_inc(*misc.empties(("f", "ss", u)))
                    elif what == "spT":
                        turned_copy(spT, ("f", "spT", u), SLOTS)
                    elif what == "syT":
                        turned_copy(syT, ("f", "syT", u), P)
                    elif what == "fxT":
                        to_xT(("f0", u))

                attn64(0)
                attend(L0_STEPS)
                attn64(1)
                attend(L1_STEPS)

                for t in range(TT):
                    act.wait_ge(*s_dv.at(it, ("m", "struck")))
                    a.activation(rex[:, t], rl[:, t, :, 0:NE], ACT.Exp, bias=nrt[:, t:t + 1])\
                        .then_inc(*s_ac.inc(("m", "ex", t)))
                for e in range(NE):
                    for f in range(FC):
                        act.wait_ge(*scores.filled(it, ("moe", "h", e, f)))
                        if e >= 2:
                            act.wait_ge(*misc.filled(it, ("moe", "y", e - 2)))
                        a.activation(hid[:, e % 2, f], scores.bank(("moe", "h", e, f)), ACT.Gelu_apprx_tanh)\
                            .then_inc(*scores.empties(("moe", "h", e, f)))
                act.sem_inc(*s_xread.inc("x"))

        @block.vector
        def _(dve):
            v = nc.vector
            dve.wait_ge(*s_slotw.once("w"))
            dve.wait_ge(*s_const.once("c"))
            dve.wait_ge(*pre.at(0, "smean"))
            v.tensor_scalar(smean[:], misc.tensor[:, 0, 0:1], 1.0 / SLOTS, None, ALU.mult)\
                .then_inc(*pred.inc("smean"))
            dve.wait_ge(*pre.at(0, "c1"))
            v.tensor_tensor(out=c1[:], in0=misc.tensor[0:SLOTS, 0, 8:9], in1=f_b1[:], op=ALU.add)\
                .then_inc(*pred.inc("c1"))
            for n in range(2):
                v.tensor_scalar(crz[:, n * SLOTS:(n + 1) * SLOTS], misc.tensor[:, 1, n * SLOTS:(n + 1) * SLOTS],
                                f_bhh[:, n:n + 1], f_bih[:, n:n + 1], ALU.add, ALU.add).then_inc(*pred.inc(("crz", n)))
            v.tensor_scalar(ghn[:], misc.tensor[:, 1, 2 * SLOTS:3 * SLOTS], f_bhh[:, 2:3], None, ALU.add)\
                .then_inc(*pred.inc("crz"))
            v.tensor_scalar(itau[:], f_tau[:, 0:1], -1.0, None, ALU.mult).then_inc(*pred.inc("t0"))
            dve.wait_ge(*pred.once("t0"))
            v.tensor_tensor(out=itau[:], in0=itau[:], in1=f_tau[:, 0:1], op=ALU.max).then_inc(*pred.inc("t1"))
            dve.wait_ge(*pred.once("t1"))
            v.tensor_scalar(itau[:], itau[:], 0.1, None, ALU.add).then_inc(*pred.inc("t2"))
            dve.wait_ge(*pred.once("t2"))
            v.reciprocal(itau[:], itau[:]).then_inc(*pred.inc("t3"))
            dve.wait_ge(*pred.once("t3"))
            v.tensor_scalar(f_b2[:], f_b2[:], itau[:, 0:1], None, ALU.mult).then_inc(*pred.inc("b2"))
            dve.wait_ge(*pred.once("b2"))

            with dve.Fori(0, ITERS) as it:
                def link(ins, key):
                    ins.then_inc(*s_dv.inc(key))
                    dve.wait_ge(*s_dv.at(it, key))

                def attn64(L):
                    def project(u, c):
                        if L == 0:
                            return
                        g = u * NC + c
                        if g >= 2:
                            dve.wait_ge(*s_po.at(it, ("qk1", (g - 2) // NC, (g - 2) % NC)))
                        for j in range(2):
                            key = (L, "qk", u, c, j)
                            dve.wait_ge(*misc.filled(it, key))
                            for w in range(2):
                                b = ((a1_bq, a1_bqs), (a1_bk, a1_bks))[w][j]
                                ins = v.scalar_tensor_tensor(
                                    out=rot[:, g % 2, j, w * SEQ:(w + 1) * SEQ],
                                    in0=misc.bank(key)[:, w * SEQ:(w + 1) * SEQ], scalar=b[:, c:c + 1],
                                    in1=rope[:, 2 * w + j], op0=ALU.add, op1=ALU.mult)
                            ins.then_inc(*misc.empties(key))

                    def values_of(t, hf):
                        key = (L, "v", t, hf)
                        dve.wait_ge(*misc.filled(it, key))
                        dst = vv[:, t, hf * 512:(hf + 1) * 512]
                        if L == 0:
                            v.tensor_copy(dst, misc.bank(key)).then_inc(*misc.empties(key))
                        else:
                            v.tensor_tensor(out=dst, in0=misc.bank(key), in1=a1_bv[:, hf * 512:(hf + 1) * 512],
                                            op=ALU.add).then_inc(*misc.empties(key))

                    project(0, 0)
                    for t in range(TT // 2):
                        for hf in range(2):
                            values_of(t, hf)
                    n = len(order)
                    for i in range(n + 2):
                        if i < n:
                            c, u, r = order[i]
                            if i % 2 == 0 and i + 2 < n:
                                project(*order[i + 2][1::-1])
                            key = (L, "s", c, u, r)
                            dve.wait_ge(*scores.filled(it, key))
                            if i >= 4:
                                dve.wait_ge(*scores.emptied(it, (L, "s", *order[i - 4])))
                            s = scores.bank(key)
                            v.tensor_reduce(nmax[:, i % 4, 0:1], s[:, 0:P], AX.X, ALU.max, negate=True)
                            v.tensor_reduce(nmax[:, i % 4, 1:2], s[:, P:3 * P], AX.X, ALU.max, negate=True)\
                                .then_inc(*s_dv.inc((L, "max", c, u, r)))
                            for t, hf in later_values(L, i):
                                values_of(t, hf)
                        for step in woven(L, i, middle=True):
                            other(step)
                        if i >= 2 and (i - 2) % 4 != 3:
                            j = i - 2
                            c, u, r = order[j]
                            dve.wait_ge(*turned.filled(it, (L, "t", c, u, r)))
                            if j >= 4:
                                dve.wait_ge(*outs.filled(it, (L, "o", *order[j - 4][:2])))
                            v.tensor_copy(probsT[:, j % 4], turned.bank((L, "t", c, u, r))[:, 0:3 * P])\
                                .then_inc(*turned.empties((L, "t", c, u, r)))
                        for step in woven(L, i):
                            other(step)

                def other(step):
                    kind, L, u, what = step
                    if kind == "piece":
                        if what == "project":
                            project_piece(L, u)
                    elif kind == "x1":
                        if what == "sum":
                            norm_sum(("x1", u), ("y", ("x1", u)), None)
                        elif what == "norm":
                            norm_apply(("x1", u))
                    elif kind == "slots":
                        slots(u, what)
                    elif what == "sums":
                        dve.wait_ge(*s_load.once("w"))
                        for r in (0, 1):
                            dve.wait_ge(*scores.emptied(it, (L, "s", NC - 1, u, r)))
                        ts = slice(2 * u, 2 * u + 2)
                        link(v.reciprocal(rsum[:, ts], sums[:, ts]), (L, "rsum", u))
                        link(v.tensor_copy(rparts[:, ts, 0, 0:NH], rsum[:, ts]), (L, "rhigh", u))
                        link(v.tensor_tensor(out=rrest[:, ts], in0=rsum[:, ts], in1=rparts[:, ts, 0, 0:NH],
                                             op=ALU.subtract), (L, "rrest", u))
                        link(v.tensor_copy(rparts[:, ts, 1, 0:NH], rrest[:, ts]), (L, "rmid", u))
                        v.tensor_tensor(out=rparts[:, ts, 2, 0:NH], in0=rrest[:, ts], in1=rparts[:, ts, 1, 0:NH],
                                        op=ALU.subtract).then_inc(*s_dv.inc((L, "rlow", u)))
                    elif what[0] == "R":
                        j = what[1]
                        dve.wait_ge(*misc.filled(it, (L, "R", u, j)))
                        dve.wait_ge(*outs.emptied(it, (L, "o", 2 * j + 1, u)))
                        o = oT[:, u, 2 * j:2 * j + 2]
                        v.tensor_tensor(out=o, in0=o, in1=misc.bank((L, "R", u, j)).rearrange("p (c n) -> p c n", c=2),
                                        op=ALU.mult).then_inc(*misc.empties((L, "R", u, j)))
                    elif what == "sum":
                        norm_sum((f"a{L}", u), ("y", (f"a{L}", u)), None)
                    elif what == "norm":
                        norm_apply((f"a{L}", u))

                def norm(name, src, last):
                    norm_sum(name, src, last)
                    norm_apply(name)

                def norm_sum(name, src, last):
                    if name[0] == "a0":
                        dve.wait_ge(*s_in.at(it, "x"))
                    else:
                        dve.wait_ge(*s_po.at(it, ("xb", ("moe", PAIR - 1) if name == "moe" else name)))
                    ts = tiles(name)
                    if last is None:
                        dve.wait_ge(*misc.filled(it, src))
                        y = misc.bank(src).rearrange("p (t d) -> p t d", d=D)[:, 0:ts.stop - ts.start]
                        v.tensor_tensor(out=xb[:, ts], in0=xb[:, ts], in1=y, op=ALU.add)\
                            .then_inc(*misc.empties(src))
                        dve.wait_ge(*misc.emptied(it, src))
                    else:
                        link(v.tensor_tensor(out=xb[:], in0=xb[:], in1=acc[:], op=ALU.add), ("ln", name, "r"))
                    for t in count(ts):
                        ins = v.bn_stats(stats[:, t], xb[:, t])
                    link(ins, ("ln", name, "stats"))
                    settle(dve)
                    for t in count(ts):
                        ins = v.bn_aggr(mv[:, t], stats[:, t])
                    link(ins, ("ln", name, "mv"))
                    v.tensor_scalar(ve[:, ts], mv[:, ts, 1], EPS, None, ALU.add)\
                        .then_inc(*s_dv.inc((("ln", name), "ve")))

                def norm_apply(name):
                    dve.wait_ge(*s_po.at(it, (("ln", name), "rstd")))
                    for t in count(tiles(name)):
                        ins = v.tensor_scalar(xa[:, t, 0:D], xb[:, t], mv[:, t, 0:1], rstd[:, t:t + 1],
                                              ALU.subtract, ALU.mult)
                    ins.then_inc(*(s_normed.inc("y") if name == "moe" else s_dv.inc(("ln", name, "x"))))

                def project_piece(name, u):
                    k, holds = PIECES[name]
                    bq, bk, bv = {"self": (s_bq, s_bk, s_bv), "cross": (c_bq, c_bk, c_bv)}.get(k, (None,) * 3)
                    dve.wait_ge(*misc.filled(it, (name, u)))
                    if (name, u) == ("cross", 1):
                        dve.wait_ge(*s_split[k, 0, 0].at(it, "store"))
                        settle(dve)
                        dve.wait_ge(*s_split[k, 0, 1].at(it, "store"))
                    for n, w in enumerate(holds):
                        b, sc = ((bq, SCALE[k]), (bk, 1.0))[w]
                        src = misc.bank((name, u))[:, n * SEQ:(n + 1) * SEQ]
                        if b is None:
                            ins = v.tensor_scalar(flat[name, u][:, n], src, sc, None, ALU.mult)
                        else:
                            ins = v.tensor_scalar(flat[name, u][:, n], src, b[:, 0:1], sc, ALU.add, ALU.mult)
                    ins.then_inc(*misc.empties((name, u)))
                    if 1 not in holds:
                        return
                    dve.wait_ge(*misc.filled(it, (k, "v", u)))
                    dst = va[k][:, 2 * u:2 * u + 2, 0:NH * VW].rearrange("p t (h w) -> p t h w", w=VW)[:, :, :, 0:DX]
                    src = misc.bank((k, "v", u))[:, 0:2 * D].rearrange("p (t h d) -> p t h d", t=2, h=NH)
                    if bv is None:
                        v.tensor_copy(dst, src).then_inc(*misc.empties((k, "v", u)))
                    else:
                        for t in range(2):
                            ins = v.tensor_tensor(out=dst[:, t], in0=src[:, t],
                                                  in1=bv[:].rearrange("p (h d) -> p h d", h=NH), op=ALU.add)
                        ins.then_inc(*misc.empties((k, "v", u)))

                def attend(steps, dests):
                    placed = None
                    for what, k, u, h, n in steps:
                        if what == "do":
                            other(k)
                        elif what == "p1":
                            key = (k, "s", u, h)
                            dve.wait_ge(*scores.filled(it, key))
                            s = scores.bank(key)
                            if k == "self":
                                v.tensor_reduce(nm[k][:, 2 * u, h:h + 1], s[:, 0:P], AX.X, ALU.max, negate=True)
                                ins = v.tensor_reduce(nm[k][:, 2 * u + 1, h:h + 1], s[:, P:3 * P], AX.X, ALU.max,
                                                      negate=True)
                            else:
                                ins = v.tensor_reduce(nm[k][:, 2 * u:2 * u + 2, h],
                                                      s.rearrange("p (t n) -> p t n", t=2), AX.X, ALU.max,
                                                      negate=True)
                            ins.then_inc(*scores.empties(key))
                        elif what == "nm":
                            dve.wait_ge(*misc.emptied(it, (k, u, "nmT")))
                            if placed is not None:
                                dve.wait_ge(*s_mrow[placed].at(it, "maxima"))
                            elif k == "self":
                                dve.wait_ge(*s_mrow["last", PAIR - 1].before(it))
                            else:
                                dve.wait_ge(*s_mrow["cross", PAIR - 1].at(it, "maxima"))
                            placed = (k, u)
                            link(v.tensor_copy(nmp[:, 0], nmf[:]), (k, u, "nmhigh"))
                            link(v.tensor_tensor(out=nmr[:], in0=nmf[:], in1=nmp[:, 0], op=ALU.subtract),
                                 (k, u, "nmrest"))
                            link(v.tensor_copy(nmp[:, 1], nmr[:]), (k, u, "nmmid"))
                            v.tensor_tensor(out=nmp[:, 2], in0=nmr[:], in1=nmp[:, 1], op=ALU.subtract)\
                                .then_inc(*s_dv.inc((k, u, "nmlow")))
                        elif what == "ot":
                            key = (len(steps), "ot", n)
                            dve.wait_ge(*turned.filled(it, key))
                            o = turned.bank(key)[:, 0:2 * P].rearrange("p (t h w) -> p t h w", t=2, h=HG)
                            link(v.reciprocal(den[:, h, 2 * u:2 * u + 2, :], o[:, :, :, DX]), (k, "den", n))
                            d = den[:, h, 2 * u:2 * u + 2, :].unsqueeze(3).to_broadcast([P, 2, HG, DX])
                            dst = dests[k][:, 2 * u:2 * u + 2, h * HG * DX:(h + 1) * HG * DX]
                            v.tensor_tensor(out=dst.rearrange("p t (h d) -> p t h d", h=HG), in0=o[:, :, :, 0:DX],
                                            in1=d, op=ALU.mult).then_inc(*turned.empties(key))

                def slots(u, what):
                    ts = slice(2 * u, 2 * u + 2)
                    if what == "ysum":
                        for n in (2 * NG * (u + 1) - 1, 2 * NG * (u + 1) - 2):
                            dve.wait_ge(*turned.emptied(it, (len(L0_STEPS), "ot", n)))
                        v.tensor_tensor(out=ys[:, ts], in0=ys[:, ts], in1=yc[:, ts], op=ALU.add)\
                            .then_inc(*s_dv.inc(("ysum", u)))
                    elif what == "sum":
                        norm_sum(("x0", u), ("y", ("x0", u)), None)
                    elif what == "norm":
                        norm_apply(("x0", u))
                    elif what == "lg":
                        dve.wait_ge(*s_rest.once("w"))
                        key = ("f", "lg", u)
                        dve.wait_ge(*misc.filled(it, key))
                        v.scalar_tensor_tensor(out=lg[:, :, 0],
                                               in0=misc.bank(key)[:, 0:2 * SLOTS].rearrange("p (t n) -> p t n", t=2),
                                               scalar=itau[:, 0:1], in1=f_b2[:].unsqueeze(1).to_broadcast([P, 2, SLOTS]),
                                               op0=ALU.mult, op1=ALU.add).then_inc(*misc.empties(key))
                        dve.wait_ge(*misc.emptied(it, key))
                        settle(dve)
                        for t in range(2):
                            ins = v.max(top[:, 2 * u + t], lg[:, t, 0])
                        link(ins, ("f", "top", u))
                        v.tensor_scalar(ntop[:, ts], top[:, ts, 0], -1.0, None, ALU.mult)
                        for t in range(2):
                            v.match_replace(lg[:, t, 1], top[:, 2 * u + t], lg[:, t, 0], -FAR)\
                                .then_inc(*s_dv.inc(("f", "struck", u, t)))
                    elif what == "ex":
                        dve.wait_ge(*s_ac.at(it, ("f", "ex", u, 1)))
                        link(v.tensor_tensor(out=alpha[:], in0=ex[:, :, 0], in1=ex[:, :, 1], op=ALU.subtract),
                             ("f", "a0", u))
                        link(v.tensor_reduce(asum[:, ts], alpha[:], AX.X, ALU.add), ("f", "asum", u))
                        link(v.reciprocal(arec[:, ts], asum[:, ts]), ("f", "arec", u))
                        v.tensor_tensor(out=alpha[:], in0=alpha[:],
                                        in1=arec[:, ts].unsqueeze(2).to_broadcast([P, 2, SLOTS]),
                                        op=ALU.mult).then_inc(*s_dv.inc(("f", "alpha", u)))
                    elif what == "si":
                        key = ("f", "si", u)
                        dve.wait_ge(*misc.filled(it, key))
                        b = misc.bank(key)
                        link(v.tensor_scalar(dnr[:], b[:, SLOTS:2 * SLOTS], 1e-8, None, ALU.add), ("f", "dn0", u))
                        link(v.reciprocal(dnr[:], dnr[:]), ("f", "dn1", u))
                        v.tensor_tensor(out=siT[:], in0=b[:, 0:SLOTS], in1=dnr[:], op=ALU.mult)\
                            .then_inc(*misc.empties(key))
                    elif what == "gi":
                        key = ("f", "gi", u)
                        dve.wait_ge(*s_ac.at(it, ("f", "ge", u)))
                        link(v.tensor_scalar(rz[:], rz[:], 0.5, 0.5, ALU.mult, ALU.add), ("f", "rz", u))
                        link(v.tensor_tensor(out=npre[:], in0=rz[:, 0:SLOTS], in1=ghn[:], op=ALU.mult), ("f", "rg", u))
                        v.tensor_tensor(out=npre[:], in0=npre[:], in1=misc.bank(key)[:, 2 * SLOTS:3 * SLOTS],
                                        op=ALU.add).then_inc(*misc.empties(key))
                    elif what == "gn":
                        dve.wait_ge(*s_ac.at(it, ("f", "gn", u)))
                        link(v.tensor_tensor(out=snT[:], in0=f_slotsT[:], in1=gn[:], op=ALU.subtract), ("f", "sn0", u))
                        link(v.tensor_tensor(out=snT[:], in0=snT[:], in1=rz[:, SLOTS:2 * SLOTS], op=ALU.mult),
                             ("f", "sn1", u))
                        v.tensor_tensor(out=snT[:], in0=snT[:], in1=gn[:], op=ALU.add)\
                            .then_inc(*s_dv.inc(("f", "sn", u)))
                    elif what == "qkv":
                        key = ("f", "qk", u)
                        dve.wait_ge(*misc.filled(it, key))
                        for n, (dst, b) in enumerate(((sq, f_bq), (sk, f_bk))):
                            ins = v.tensor_scalar(dst[:], misc.bank(key)[0:DQ, n * SLOTS:(n + 1) * SLOTS], b[:, 0:1],
                                                  None, ALU.add)
                        ins.then_inc(*misc.empties(key))
                        key = ("f", "sv", u)
                        dve.wait_ge(*misc.filled(it, key))
                        v.tensor_tensor(out=svv[:], in0=misc.bank(key)[0:SLOTS, 0:D], in1=f_bv[:], op=ALU.add)\
                            .then_inc(*misc.empties(key))
                    elif what == "ss":
                        key = ("f", "ss", u)
                        dve.wait_ge(*misc.filled(it, key))
                        link(v.tensor_reduce(sm[:, u, 0:1], misc.bank(key)[0:SLOTS, 0:SLOTS], AX.X, ALU.max,
                                             negate=True), ("f", "sm", u))
                        v.tensor_scalar(sm[:, u, 1:2], sm[:, u, 0:1], DQ ** -0.5, None, ALU.mult)\
                            .then_inc(*s_dv.inc(("f", "smax", u)))
                    elif what == "sp":
                        dve.wait_ge(*misc.emptied(it, ("f", "ss", u)))
                        link(v.reciprocal(sm[:, u, 3:4], sm[:, u, 2:3]), ("f", "sr", u))
                        v.tensor_scalar(sp_[:], sp_[:], sm[:, u, 3:4], None, ALU.mult).then_inc(*s_dv.inc(("f", "sp", u)))
                    elif what == "comm":
                        key = ("f", "comm", u)
                        dve.wait_ge(*misc.filled(it, key))
                        v.tensor_copy(sy[:], misc.bank(key)[0:SLOTS, 0:D]).then_inc(*misc.empties(key))
                        dve.wait_ge(*misc.emptied(it, key))
                        link(v.bn_stats(sst[:, u], sy[:]), ("f", "sst", u))
                        settle(dve)
                        link(v.bn_aggr(smv[:, u], sst[:, u]), ("f", "smv", u))
                        v.tensor_scalar(srs[:, u, 0:1], smv[:, u, 1:2], EPS, None, ALU.add)\
                            .then_inc(*s_dv.inc((("ln", "slots", u), "ve")))
                    elif what == "sy":
                        dve.wait_ge(*s_po.at(it, (("ln", "slots", u), "rstd")))
                        link(v.tensor_scalar(sy[:], sy[:], smv[:, u, 0:1], srs[:, u, 1:2], ALU.subtract, ALU.mult),
                             ("f", "y0", u))
                        link(v.tensor_tensor(out=sy[:], in0=sy[:], in1=f_lng[:], op=ALU.mult), ("f", "y1", u))
                        v.tensor_tensor(out=sy[:], in0=sy[:], in1=f_lnb[:], op=ALU.add).then_inc(*s_dv.inc(("f", "sy", u)))
                    elif what == "svT":
                        key = ("f", "svT", u)
                        dve.wait_ge(*misc.filled(it, key))
                        v.tensor_scalar(svT[:], misc.bank(key)[:, 0:SLOTS], f_bvp[:, 0:1], None, ALU.add)\
                            .then_inc(*misc.empties(key))
                    elif what == "svo":
                        key = ("f", "svo", u)
                        dve.wait_ge(*misc.filled(it, key))
                        v.tensor_copy(svo[:], misc.bank(key)[0:SLOTS, 0:D]).then_inc(*misc.empties(key))
                    elif what == "fsum":
                        norm_sum(("f0", u), ("y", ("f0", u)), None)
                    elif what == "fnorm":
                        norm_apply(("f0", u))

                attn64(0)
                attend(L0_STEPS, {"self": ys, "cross": yc})
                dve.wait_ge(*s_rest.once("w"))
                attn64(1)
                attend(L1_STEPS, {"last": ys})

                dve.wait_ge(*outs.filled(it, ("m", "rl")))
                v.tensor_copy(rl[:, :, 0, 0:NE], outs.bank(("m", "rl"))[:, 0:TT * NE].rearrange("p (t e) -> p t e", t=TT))\
                    .then_inc(*outs.empties(("m", "rl")))
                dve.wait_ge(*outs.emptied(it, ("m", "rl")))
                settle(dve)
                for t in range(TT):
                    ins = v.max(rtop[:, t], rl[:, t, 0, 0:NE])
                link(ins, ("m", "top"))
                v.tensor_scalar(nrt[:], rtop[:, :, 0], -1.0, None, ALU.mult)
                link(v.tensor_copy(rtwo[:, :, 0:TOP], rtop[:, :, 0:TOP]), ("m", "two"))
                settle(dve)
                for t in range(TT):
                    ins = v.match_replace(rl[:, t, 1], rtwo[:, t], rl[:, t, 0], -FAR)
                link(ins, ("m", "struck"))
                link(v.tensor_tensor(out=chosen[:], in0=rl[:, :, 0, 0:NE], in1=rl[:, :, 1, 0:NE], op=ALU.not_equal),
                     ("m", "chosen"))
                v.tensor_copy(chosenb[:], chosen[:])
                for t in range(TT):
                    link(v.tensor_tensor(out=seen[:, t + 1], in0=seen[:, t], in1=chosen[:, t], op=ALU.add),
                         ("m", "seen", t))
                link(v.tensor_copy(seenb[:], seen[:, 0:TT]), ("m", "seenb"))
                link(v.tensor_copy(seen[:, 0], seen[:, TT]), ("m", "carry"))
                dve.wait_ge(*s_ac.at(it, ("m", "ex", TT - 1)))
                link(v.tensor_reduce(rden[:], rex[:, :, 0], AX.X, ALU.add), ("m", "den"))
                link(v.reciprocal(rrec[:], rden[:]), ("m", "rec"))
                link(v.tensor_tensor(out=wexp[:], in0=rex[:, :, 0], in1=rex[:, :, 1], op=ALU.subtract), ("m", "we"))
                dve.wait_ge(*outs.filled(it, ("m", "pos")))
                v.tensor_scalar(fits[:], outs.bank(("m", "pos"))[:, 0:TT * NE].rearrange("p (t e) -> p t e", t=TT),
                                float(CAPACITY), None, ALU.is_lt).then_inc(*outs.empties(("m", "pos")))
                dve.wait_ge(*outs.emptied(it, ("m", "pos")))
                link(v.tensor_tensor(out=wexp[:], in0=wexp[:], in1=fits[:], op=ALU.mult), ("m", "w0"))
                link(v.tensor_tensor(out=wgt[:], in0=wexp[:], in1=rrec[:].unsqueeze(2).to_broadcast([P, TT, NE]),
                                     op=ALU.mult), ("m", "w"))
                for e in range(NE):
                    key = ("moe", "y", e)
                    dve.wait_ge(*misc.filled(it, key))
                    y = misc.bank(key).rearrange("p (t d) -> p t d", t=TT)
                    for t in range(TT):
                        if e == 0:
                            ins = v.tensor_scalar(acc[:, t], y[:, t], wgt[:, t, e:e + 1], None, ALU.mult)
                        else:
                            ins = v.scalar_tensor_tensor(out=acc[:, t], in0=y[:, t], scalar=wgt[:, t, e:e + 1],
                                                         in1=acc[:, t], op0=ALU.mult, op1=ALU.add)
                    ins.then_inc(*misc.empties(key))
                    dve.wait_ge(*misc.emptied(it, key))
                norm("moe", None, acc)

        @block.tensor
        def _(pe):
            t_ = nc.tensor
            for ring in (scores, turned, outs, misc):
                ring.open(pe)
            pe.wait_ge(*s_slotw.once("w"))
            pe.wait_ge(*s_const.once("c"))
            t_.matmul(misc.tensor[:, 0, 0:1], f_slots[:], ones[0:SLOTS, 0:1], start=True, stop=True)\
                .then_inc(*pre.inc("smean"))
            pe.wait_ge(*pred.once("smean"))
            t_.matmul(misc.tensor[0:SLOTS, 0, 8:9], f_w1[:, 1, :], smean[:], start=True, stop=True)
            for n in range(3):
                ins = t_.matmul(misc.tensor[:, 1, n * SLOTS:(n + 1) * SLOTS], f_whh[:, n * D:(n + 1) * D], f_slotsT[:],
                                start=True, stop=True)
            ins.then_inc(*pre.inc("c1"))
            pe.wait_ge(*pred.once("crz"))

            with pe.Fori(0, ITERS) as it:
                def one(ring, key, out_of, lhsT, rhs):
                    bank = ring.take(key)
                    pe.wait_ge(*ring.reusable(it, key))
                    if key[0] == "f":
                        settle(pe)
                    t_.matmul(out_of(bank), lhsT, rhs, start=True, stop=True).then_inc(*ring.fills(key))

                def masked(out, m):
                    t_.matmul(out, identb[:], m[:], start=False, stop=True, skip_group_check=True)

                def attn64(L, wq, wqs, wk, wks, wv, wo, name):
                    def project(u, c):
                        cols = slice(c * P, (c + 1) * P)
                        for j, ms in enumerate(((wq, wk),) if L == 0 else ((wq, wk), (wqs, wks))):
                            key = (L, "qk", u, c, j)
                            if L == 1 and c == 0:
                                pe.wait_ge(*misc.emptied(it, ("xT", ("f0", u))))
                                settle(pe)
                            b = misc.take(key)
                            pe.wait_ge(*misc.reusable(it, key))
                            for w in range(2):
                                ins = t_.matmul(b[:, w * SEQ:(w + 1) * SEQ], ms[w][:, cols],
                                                xT[:, u * SEQ:(u + 1) * SEQ], start=True, stop=True)
                            ins.then_inc(*misc.fills(key))

                    def score(i):
                        c, u, r = order[i]
                        key = (L, "s", c, u, r)
                        s = scores.take(key)
                        pe.wait_ge(*scores.reusable(it, key))
                        if L == 0:
                            pe.wait_ge(*misc.emptied(it, (L, "qk", u, c, 0)))
                        else:
                            pe.wait_ge(*s_po.at(it, ("qk1", u, c)))
                        mine = qk[HD * r:HD * r + HD, (u * NC + c) % 2]
                        t_.matmul(s[:, 0:P], mine[:, 0, 0:P], mine[:, 1, 0:P],
                                  start=True, stop=False, skip_group_check=True)
                        t_.matmul(s[:, P:3 * P], mine[:, 0, P:2 * P], mine[:, 1],
                                  start=False, stop=False, skip_group_check=True)
                        masked(s[:, 0:P], mask)
                        t_.matmul(s[:, 2 * P:3 * P], identb[:], mask[:], start=False, stop=True,
                                  skip_group_check=True).then_inc(*scores.fills(key))

                    def turn(i):
                        key = (L, "t", *order[i])
                        b = turned.take(key)
                        pe.wait_ge(*turned.reusable(it, key))
                        pe.wait_ge(*scores.emptied(it, (L, "s", *order[i])))
                        for j in range(3):
                            ins = t_.transpose(b[:, j * P:(j + 1) * P], probs[:, i % NPR, j * P:(j + 1) * P],
                                               ident[:])
                        ins.then_inc(*turned.fills(key))

                    def values(p):
                        c, u, _ = order[2 * p]
                        key = (L, "o", c, u)
                        b = outs.take(key)
                        pe.wait_ge(*outs.reusable(it, key))
                        for r in range(2):
                            pe.wait_ge(*turned.emptied(it, (L, "t", c, u, r)))
                        for kt, (lo, hi, at) in enumerate(((0, 2 * P, 0), (2 * P, 3 * P, P))):
                            for r in range(2):
                                h = 2 * c + r
                                ins = t_.matmul(b[HD * r:HD * r + HD, at:SEQ], vv[:, 2 * u + kt, h * HD:(h + 1) * HD],
                                                probsT[:, (2 * p + r) % 4, lo:hi], start=(kt == 0), stop=(kt == 1),
                                                skip_group_check=True)
                        ins.then_inc(*outs.fills(key))

                    def values_of(t, hf):
                        one(misc, (L, "v", t, hf), lambda b: b, xT[:, t * P:(t + 1) * P],
                            wv[:, hf * 512:(hf + 1) * 512])

                    project(0, 0)
                    for t in range(TT // 2):
                        for hf in range(2):
                            values_of(t, hf)
                    n = len(order)
                    for i in range(n + 3):
                        if i < n:
                            if i % 2 == 0 and i + 2 < n:
                                project(*order[i + 2][1::-1])
                            score(i)
                            for t, hf in later_values(L, i):
                                values_of(t, hf)
                        for step in woven(L, i, middle=True):
                            other(step)
                        if 2 <= i < n + 2:
                            turn(i - 2)
                        if i >= 4 and i % 2 == 0:
                            values((i - 4) // 2)
                        for step in woven(L, i):
                            other(step)

                def other(step):
                    kind, L, u, what = step
                    if kind == "piece":
                        if what == "project":
                            project_piece(L, u)
                    elif kind == "x1":
                        x1(u, what)
                    elif kind == "slots":
                        slots(u, what)
                    elif what == "rT":
                        pe.wait_ge(*s_late.once("c"))
                        key = (L, "rT", u)
                        b = misc.take(key)
                        pe.wait_ge(*misc.reusable(it, key))
                        pe.wait_ge(*s_dv.at(it, (L, "rlow", u)))
                        for t in range(2):
                            ins = t_.matmul(b[0:PARTS * 32, t * P:(t + 1) * P],
                                            rparts[:, 2 * u + t].rearrange("p a h -> p (a h)"), identb[:],
                                            start=True, stop=True)
                        ins.then_inc(*misc.fills(key))
                        pe.wait_ge(*misc.emptied(it, key))
                    elif what[0] == "R":
                        key = (L, "R", u, what[1])
                        b = misc.take(key)
                        pe.wait_ge(*misc.reusable(it, key))
                        settle(pe)
                        pe.wait_ge(*misc.emptied(it, (L, "rT", u)))
                        for j in range(2):
                            ins = t_.matmul(b[:, j * SEQ:(j + 1) * SEQ], head_rows[:, 2 * what[1] + j, :], rT[:],
                                            start=True, stop=True)
                        ins.then_inc(*misc.fills(key))
                    elif what == "out":
                        name = (f"a{L}", u)
                        pe.wait_ge(*s_load.once("w"))
                        key = ("y", name)
                        y = misc.take(key)
                        pe.wait_ge(*misc.reusable(it, key))
                        settle(pe)
                        for c in range(NC):
                            pe.wait_ge(*misc.emptied(it, (L, "R", u, c // 2)))
                            for t in range(2):
                                ins = t_.matmul(y[:, t * D:(t + 1) * D], oT[:, u, c, t * P:(t + 1) * P], (a0_wo, a1_wo)[L][:, c],
                                                start=(c == 0 and t == 0), stop=(c == NC - 1),
                                                skip_group_check=True)
                        ins.then_inc(*misc.fills(key))
                    elif what == "xT":
                        to_xT((f"a{L}", u))

                def to_xT(name):
                    key = ("xT", name)
                    b = misc.take(key)
                    pe.wait_ge(*misc.reusable(it, key))
                    pe.wait_ge(*s_dv.at(it, ("ln", name, "x")))
                    for n, t in enumerate(count(tiles(name))):
                        ins = t_.transpose(b[:, n * P:(n + 1) * P], xa[:, t, 0:D], ident[:])
                    ins.then_inc(*misc.fills(key))

                def project_piece(name, u):
                    k, holds = PIECES[name]
                    if w_of := {"self": ("a0", u), "last queries": ("a1", u)}.get(name):
                        pe.wait_ge(*misc.emptied(it, ("xT", w_of)))
                        settle(pe)
                    weights = {"self": (s_wq, s_wk, s_wv), "cross": (c_wq, c_wk, c_wv), "last": (z_wq, z_wk, z_wv)}[k]
                    q0 = u * SEQ
                    key = (name, u)
                    b = misc.take(key)
                    pe.wait_ge(*misc.reusable(it, key))
                    for n, w in enumerate(holds):
                        src = xT if w == 0 or k == "self" else ctxT
                        ins = t_.matmul(b[:, n * SEQ:(n + 1) * SEQ], weights[w][:], src[:, q0:q0 + SEQ],
                                        start=True, stop=True)
                    ins.then_inc(*misc.fills(key))
                    if 1 not in holds:
                        return
                    src = xT if k == "self" else ctxT
                    key = (k, "v", u)
                    b = misc.take(key)
                    pe.wait_ge(*misc.reusable(it, key))
                    for t in range(2):
                        ins = t_.matmul(b[:, t * D:(t + 1) * D], src[:, q0 + t * P:q0 + (t + 1) * P], weights[2][:],
                                        start=True, stop=True)
                    ins.then_inc(*misc.fills(key))

                def first_scores(k, u, h):
                    key = (k, "s", u, h)
                    s = scores.take(key)
                    pe.wait_ge(*scores.reusable(it, key))
                    if h == 0:
                        pe.wait_ge(*s_stack[k, u].at(it, {"self": 1, "cross": "ones", "last": 0}[k]))
                    q0 = 0
                    qh, kh = stacks[k][0][0:STACK, u, h], stacks[k][1][0:STACK, u, h]
                    if k == "self":
                        t_.matmul(s[:, 0:P], qh[:, q0:q0 + P], kh[:, q0:q0 + P],
                                  start=True, stop=False, skip_group_check=True)
                        t_.matmul(s[:, P:3 * P], qh[:, q0 + P:q0 + SEQ], kh[:, q0:q0 + SEQ],
                                  start=False, stop=False, skip_group_check=True)
                        masked(s[:, 0:P], mask)
                        ins = t_.matmul(s[:, 2 * P:3 * P], identb[:], mask[:], start=False, stop=True,
                                        skip_group_check=True)
                    else:
                        for t in range(2):
                            ins = t_.matmul(s[:, t * SEQ:(t + 1) * SEQ], qh[:, q0 + t * P:q0 + (t + 1) * P],
                                            kh[:, q0:q0 + SEQ], start=True, stop=True)
                    ins.then_inc(*scores.fills(key))

                def turned_maxima(k, u):
                    key = (k, u, "nmT")
                    b = misc.take(key)
                    pe.wait_ge(*misc.reusable(it, key))
                    pe.wait_ge(*scores.emptied(it, (k, "s", u, NH - 1)))
                    for t in range(2):
                        ins = t_.transpose(b[0:NH, t * P:(t + 1) * P], nm[k][:, 2 * u + t], ident[:])
                    ins.then_inc(*misc.fills(key))

                def second_scores(k, u, h):
                    key = (k, "st", u, h)
                    s = scores.take(key)
                    pe.wait_ge(*scores.reusable(it, key))
                    if h == 0:
                        pe.wait_ge(*s_mrow[k, u].at(it, "maxima"))
                    q0 = 0
                    qh, kh = stacks[k][0][0:MROW + PARTS, u, h], stacks[k][1][0:MROW + PARTS, u, h]
                    if k == "self":
                        t_.matmul(s[:, 0:SEQ], kh[:, q0:q0 + P], qh[:, q0:q0 + SEQ],
                                  start=True, stop=False, skip_group_check=True)
                        t_.matmul(s[:, SEQ:3 * P], kh[:, q0 + P:q0 + SEQ], qh[:, q0 + P:q0 + SEQ],
                                  start=False, stop=False, skip_group_check=True)
                        masked(s[:, 0:P], maskT)
                        ins = t_.matmul(s[:, SEQ:3 * P], identb[:], maskT[:], start=False, stop=True,
                                        skip_group_check=True)
                    else:
                        for t in range(2):
                            ins = t_.matmul(s[:, t * SEQ:(t + 1) * SEQ], kh[:, q0 + t * P:q0 + (t + 1) * P],
                                            qh[:, q0:q0 + SEQ], start=True, stop=True)
                    ins.then_inc(*scores.fills(key))

                def attend(steps):
                    for what, k, u, h, n in steps:
                        if what == "do":
                            other(k)
                        elif what == "p1":
                            first_scores(k, u, h)
                        elif what == "nm":
                            turned_maxima(k, u)
                        elif what == "p2":
                            second_scores(k, u, h)
                        elif what == "av":
                            key = (len(steps), "o", n)
                            b = outs.take(key)
                            pe.wait_ge(*outs.reusable(it, key))
                            pe.wait_ge(*scores.emptied(it, (k, "st", u, HG * h + HG - 1)))
                            for kt in range(2):
                                lo, hi, at = ((0, SEQ, 0), (SEQ, 3 * P, P) if k == "self" else (SEQ, 2 * SEQ, 0))[kt]
                                for j in range(HG):
                                    c0 = (HG * h + j) * VW
                                    ins = t_.matmul(b[32 * j:32 * j + 32, at:SEQ], va[k][:, 2 * u + kt, c0:c0 + 32],
                                                    px[:, (HG * n + j) % NPX, lo:hi], start=(kt == 0),
                                                    stop=(kt == 1), skip_group_check=True)
                            ins.then_inc(*outs.fills(key))
                        elif what == "ot":
                            key = (len(steps), "ot", n)
                            b = turned.take(key)
                            pe.wait_ge(*turned.reusable(it, key))
                            pe.wait_ge(*outs.emptied(it, (len(steps), "o", n)))
                            for t in range(2):
                                ins = t_.transpose(b[:, t * P:(t + 1) * P], og[:, n % 2, t * P:(t + 1) * P],
                                                   ident[:])
                            ins.then_inc(*turned.fills(key))

                def x1(u, what):
                    halves = [slice(0, P), slice(P, 2 * P)]
                    if what == "yT":
                        key = ("x1T", u)
                        b = misc.take(key)
                        pe.wait_ge(*misc.reusable(it, key))
                        for n in (NG * (u + 1) - 1, NG * (u + 1) - 2):
                            pe.wait_ge(*turned.emptied(it, (len(L1_STEPS), "ot", n)))
                        for t in range(2):
                            ins = t_.transpose(b[:, halves[t]], ys[:, 2 * u + t], ident[:])
                        ins.then_inc(*misc.fills(key))
                    elif what == "y":
                        product(("y", ("x1", u)), P, D, [(t * D, yTu[u][:, halves[t]], z_wo[:], True, True)
                                                        for t in range(2)], [misc.emptied(it, ("x1T", u))])
                    elif what == "xT":
                        to_xT(("x1", u))

                def turn_slots(key, src, ready):
                    b = misc.take(key)
                    pe.wait_ge(*ready)
                    settle(pe)
                    pe.wait_ge(*misc.reusable(it, key))
                    settle(pe)
                    t_.transpose(b[0:src.shape[1], 0:SLOTS], src[:], ident[0:SLOTS, 0:SLOTS])\
                        .then_inc(*misc.fills(key))

                def product(key, rows, columns, terms, ready):
                    b = misc.take(key)
                    for made in ready:
                        pe.wait_ge(*made)
                        settle(pe)
                    pe.wait_ge(*misc.reusable(it, key))
                    settle(pe)
                    for at, lhs, rhs, first, last in terms:
                        ins = t_.matmul(b[0:rows, at:at + columns], lhs, rhs, start=first, stop=last)
                    ins.then_inc(*misc.fills(key))

                def slots(u, what):
                    done = lambda *key: misc.emptied(it, key)
                    cols = slice(u * SEQ, (u + 1) * SEQ)
                    halves = [slice(0, P), slice(P, 2 * P)]
                    if what == "yT":
                        key = ("yT", u)
                        b = misc.take(key)
                        pe.wait_ge(*misc.reusable(it, key))
                        pe.wait_ge(*s_dv.at(it, ("ysum", u)))
                        for t in range(2):
                            ins = t_.transpose(b[:, halves[t]], ys[:, 2 * u + t], ident[:])
                        ins.then_inc(*misc.fills(key))
                    elif what == "y":
                        product(("y", ("x0", u)), P, D, [(t * D, yTu[u][:, halves[t]], p_w[:], True, True)
                                                        for t in range(2)], [done("yT", u)])
                    elif what == "xT":
                        to_xT(("x0", u))
                    elif what == "h":
                        pe.wait_ge(*s_rest.once("w"))
                        product(("f", "h", u), SLOTS, SEQ, [(0, f_w1[:, 0, :], xT[:, cols], True, True)],
                                [done("xT", ("x0", u))])
                    elif what == "lg":
                        product(("f", "lg", u), P, SLOTS, [(t * SLOTS, hT[:, halves[t]], f_w2[:], True, True)
                                                          for t in range(2)], [done("f", "h", u)])
                    elif what == "si":
                        key = ("f", "aT", u)
                        b = misc.take(key)
                        pe.wait_ge(*misc.reusable(it, key))
                        pe.wait_ge(*s_dv.at(it, ("f", "alpha", u)))
                        settle(pe)
                        for t in range(2):
                            ins = t_.transpose(b[0:SLOTS, halves[t]], alpha[:, t], ident[:])
                        ins.then_inc(*misc.fills(key))
                        product(("f", "si", u), P, SLOTS, [(at, lhs(t), alpha[:, t], t == 0, t == 1)
                                for at, lhs in ((0, lambda t: xa[:, 2 * u + t, 0:D]), (SLOTS, lambda t: ones[:]))
                                for t in range(2)], [])
                    elif what == "gi":
                        key = ("f", "gi", u)
                        b = misc.take(key)
                        pe.wait_ge(*done("f", "si", u))
                        settle(pe)
                        pe.wait_ge(*misc.reusable(it, key))
                        settle(pe)
                        t_.matmul(b[:, 0:2 * SLOTS], ident[:], crz[:], start=True, stop=False, skip_group_check=True)
                        for n in range(2):
                            t_.matmul(b[:, n * SLOTS:(n + 1) * SLOTS], f_wih[:, n * D:(n + 1) * D], siT[:],
                                      start=False, stop=(n == 1), skip_group_check=True)
                        t_.matmul(b[:, 2 * SLOTS:3 * SLOTS], f_wih[:, 2 * D:3 * D], siT[:], start=True, stop=True,
                                  skip_group_check=True).then_inc(*misc.fills(key))
                    elif what == "qkv":
                        product(("f", "qk", u), DQ, SLOTS, [(n * SLOTS, w[:], snT[:], True, True)
                                                           for n, w in enumerate((f_wq, f_wk))], [s_dv.at(it, ("f", "sn", u))])
                        product(("f", "sv", u), SLOTS, D, [(0, snT[:], f_wv[:], True, True)], [])
                    elif what == "ss":
                        product(("f", "ss", u), SLOTS, SLOTS, [(0, sq[:], sk[:], True, True)], [done("f", "qk", u)])
                    elif what == "spT":
                        turn_slots(("f", "spT", u), sp_, s_dv.at(it, ("f", "sp", u)))
                    elif what == "comm":
                        product(("f", "comm", u), SLOTS, D, [(0, snT[:], ident[:], True, False),
                                                             (0, spT[:], svv[:], False, True)],
                                [done("f", "sv", u), done("f", "spT", u)])
                    elif what == "syT":
                        turn_slots(("f", "syT", u), sy, s_dv.at(it, ("f", "sy", u)))
                    elif what == "svT":
                        product(("f", "svT", u), P, SLOTS, [(0, f_wvp[:], syT[:], True, True)], [done("f", "syT", u)])
                    elif what == "svo":
                        product(("f", "svo", u), SLOTS, D, [(0, svT[:], f_wo[:], True, True)], [done("f", "svT", u)])
                    elif what == "yf":
                        product(("y", ("f0", u)), P, D, [(t * D, alphaT[:, halves[t]], svo[:], True, True)
                                                        for t in range(2)], [done("f", "aT", u), done("f", "svo", u)])
                    elif what == "fxT":
                        to_xT(("f0", u))

                pe.wait_ge(*s_first.once("w"))
                pe.wait_ge(*s_inT.at(it, "x"))
                attn64(0, a0_wq, None, a0_wk, None, a0_wv, a0_wo, "a0")
                attend(L0_STEPS)
                attn64(1, a1_wq, a1_wqs, a1_wk, a1_wks, a1_wv, a1_wo, "a1")
                attend(L1_STEPS)
                for u in range(PAIR):
                    pe.wait_ge(*misc.emptied(it, ("xT", ("x1", u))))
                    settle(pe)

                b = outs.take(("m", "rl"))
                pe.wait_ge(*outs.reusable(it, ("m", "rl")))
                for t in range(TT):
                    ins = t_.matmul(b[:, t * NE:(t + 1) * NE], xT[:, t * P:(t + 1) * P], m_wr[:], start=True, stop=True)
                ins.then_inc(*outs.fills(("m", "rl")))

                def places_in_experts():
                    key = ("m", "pos")
                    b = outs.take(key)
                    pe.wait_ge(*outs.reusable(it, key))
                    pe.wait_ge(*s_dv.at(it, ("m", "seenb")))
                    for t in range(TT):
                        t_.matmul(b[:, t * NE:(t + 1) * NE], earlier[:], chosenb[:, t], start=True, stop=False)
                        ins = t_.matmul(b[:, t * NE:(t + 1) * NE], onesb[:], seenb[:, t], start=False, stop=True)
                    ins.then_inc(*outs.fills(key))

                def expert_out(e):
                    key = ("moe", "y", e)
                    y = misc.take(key)
                    pe.wait_ge(*misc.reusable(it, key))
                    pe.wait_ge(*s_w2e[e % 2].at(it, e))
                    pe.wait_ge(*scores.emptied(it, ("moe", "h", e, FC - 1)))
                    for t in range(TT):
                        for f in range(FC):
                            ins = t_.matmul(y[:, t * D:(t + 1) * D], hid[:, e % 2, f, t * P:(t + 1) * P],
                                            w2e[:, e % 2, f], start=(f == 0), stop=(f == FC - 1))
                    ins.then_inc(*misc.fills(key))

                for e in range(NE):
                    pe.wait_ge(*s_w1e[e % 2].at(it, e))
                    for f in range(FC):
                        one(scores, ("moe", "h", e, f), lambda b: b, w1e[:, e % 2, f * P:(f + 1) * P], xT[:])
                    if e == 1:
                        places_in_experts()
                    if e >= 1:
                        expert_out(e - 1)
                expert_out(NE - 1)

        for c in closing:
            c.close()


def rotary_tables():
    inv = (np.float32(1.0) / np.float32(10000.0) ** (np.float32(2.0) * np.arange(HD // 2, dtype=np.float32)
                                                     / np.float32(HD))).astype(np.float32)
    ang = (inv[:, None] * np.arange(SEQ, dtype=np.float32)[None]).astype(np.float32)
    cos, sin = np.cos(ang).astype(np.float32), np.sin(ang).astype(np.float32)
    c = np.concatenate([cos, cos, cos, cos])
    s = np.concatenate([-sin, sin, -sin, sin])
    k = np.float32(HD ** -0.5)
    return np.stack([c * k, s * k, c, s])


def lay_out(i):
    at = np.arange(E).reshape(NH, HD // 2, 2)
    even_odd = np.concatenate([at[:, :, 0], at[:, :, 1]], 1).reshape(-1)
    odd_even = np.concatenate([at[:, :, 1], at[:, :, 0]], 1).reshape(-1)
    col = lambda a: a.reshape(-1, 1)
    row = lambda a: a.reshape(1, -1)
    chunks = lambda a, order: a[order].reshape(NC, P).T
    apart = np.arange(D).reshape(NH, DX).T.reshape(-1)
    return {
        "x": i["x"], "xT": i["x"].transpose(0, 2, 1), "ctxT": i["ctx_512"].transpose(0, 2, 1),
        "a0_wq": i["L0_attn_wq"].T, "a0_wk": i["L0_attn_wk"].T, "a0_wv": i["L0_attn_wv"].T,
        "a0_wo": i["L0_attn_wo"].T,
        "a1_wq": i["L1_attn_Wq"][:, even_odd], "a1_wqs": i["L1_attn_Wq"][:, odd_even],
        "a1_wk": i["L1_attn_Wk"][:, even_odd], "a1_wks": i["L1_attn_Wk"][:, odd_even],
        "a1_wv": i["L1_attn_Wv"], "a1_wo": i["L1_attn_Wo"],
        "a1_bq": chunks(i["L1_attn_bq"], even_odd), "a1_bqs": chunks(i["L1_attn_bq"], odd_even),
        "a1_bk": chunks(i["L1_attn_bk"], even_odd), "a1_bks": chunks(i["L1_attn_bk"], odd_even),
        "a1_bv": row(i["L1_attn_bv"]), "a1_bo": row(i["L1_attn_bo"]), "rope": rotary_tables(),
        "s_wq": i["L0_xattn_Wq"][:, apart], "s_wk": i["L0_xattn_Wk"][:, apart], "s_wv": i["L0_xattn_Wv"],
        "s_bq": col(i["L0_xattn_bq"][apart]), "s_bk": col(i["L0_xattn_bk"][apart]), "s_bv": row(i["L0_xattn_bv"]),
        "c_wq": i["L0_xattn_Wcq"][:, apart], "c_wk": i["L0_xattn_Wck"][:, apart], "c_wv": i["L0_xattn_Wcv"],
        "c_bq": col(i["L0_xattn_bcq"][apart]), "c_bk": col(i["L0_xattn_bck"][apart]), "c_bv": row(i["L0_xattn_bcv"]),
        "p_w": i["L0_xattn_Wp"], "p_b": row(i["L0_xattn_bp"]),
        "z_wq": i["L1_xattn_Wq"].T[:, apart], "z_wk": i["L1_xattn_Wkv"][:D].T[:, apart], "z_wv": i["L1_xattn_Wkv"][D:].T,
        "z_wo": i["L1_xattn_Wo"].T,
        "f_slots": i["L0_ffn_slot_init"], "f_slotsT": i["L0_ffn_slot_init"].T, "f_w1": i["L0_ffn_w1"],
        "f_b1": col(i["L0_ffn_b1"]), "f_w2": i["L0_ffn_w2"], "f_b2": row(i["L0_ffn_b2"]),
        "f_tau": row(i["L0_ffn_tau"]), "f_wihT": i["L0_ffn_Wih"].T, "f_whhT": i["L0_ffn_Whh"].T,
        "f_bih": i["L0_ffn_bih"].reshape(3, D).T, "f_bhh": i["L0_ffn_bhh"].reshape(3, D).T,
        "f_wq": i["L0_ffn_wq"], "f_bq": col(i["L0_ffn_bq"]), "f_wk": i["L0_ffn_wk"], "f_bk": col(i["L0_ffn_bk"]),
        "f_wv": i["L0_ffn_wv"], "f_bv": row(i["L0_ffn_bv"]), "f_lng": row(i["L0_ffn_ln_g"]),
        "f_lnb": row(i["L0_ffn_ln_b"]), "f_wvp": i["L0_ffn_wvp"], "f_bvp": col(i["L0_ffn_bvp"]),
        "f_wo": i["L0_ffn_wo"], "f_bo": row(i["L0_ffn_bo"]),
        "m_wr": i["L1_ffn_w_router"], "m_w1": i["L1_ffn_w1"], "m_w2": i["L1_ffn_w2"],
        "m_b": i["L1_ffn_bias"].reshape(1, D),
    }


def program(make_core, places):
    nc = make_core()
    dram = {n: nc.dram_tensor(f"in_{n}", s, F32, kind="ExternalInput").ap() for n, s in INPUTS.items()}
    out = nc.dram_tensor("out_0", (BATCH, SEQ, D), F32, kind="ExternalOutput").ap()
    build(nc, dram, out, places)
    return nc


def kernel(**inputs):
    import concourse.bacc as bacc
    from concourse.bass_utils import run_bass_kernel_spmd

    def make_core():
        return bacc.Bacc("TRN2", target_bir_lowering=False, num_devices=1)

    laid = lay_out({n: np.asarray(a) for n, a in inputs.items()})
    arrays = {f"in_{n}": np.ascontiguousarray(a) for n, a in laid.items()}
    places = {}
    program(make_core, places)
    nc = program(make_core, places)
    r = run_bass_kernel_spmd(nc, [arrays], core_ids=[0])
    return r.results[0]["out_0"]
```
